# Optimizing a Trainium2 kernel written in Bass

```python
import numpy as np
import jax
import jax.numpy as jnp

def _softmax(x, axis=-1):
    return jax.nn.softmax(x, axis=axis)

def _gelu(x):
    return jax.nn.gelu(x, approximate=True)

def _silu(x):
    return jax.nn.silu(x)

def _sigmoid(x):
    return jax.nn.sigmoid(x)

def _layernorm(x, axis=-1, eps=1e-05):
    m = jnp.mean(x, axis=axis, keepdims=True)
    v = jnp.var(x, axis=axis, keepdims=True)
    return (x - m) / jnp.sqrt(v + eps)

def _scatter_add(tgt, idx, src, axis=0):
    return tgt.at[idx].add(src)

def _segment_sum(src, seg, n):
    return jax.ops.segment_sum(src, seg, n)
kernel_name = 'mk_prb_d2_jaxref_r8_09b2d6'

def setup_inputs(seed: int=0):
    np.random.seed(seed)
    _w = jnp.asarray

    def _L0_attn_setup():
        import jax, jax.numpy as jnp
        import numpy as np
        import math
        D_MODEL = 128
        N_HEADS = 16
        HEAD_DIM = D_MODEL // N_HEADS
        FEAT = 16
        WINDOW = 64
        EPS_NORM = 1e-06
        EPS_LIN = 1e-06
        CHUNK = 128

        def rmsnorm(x, w):
            return x * jax.lax.rsqrt(jnp.mean(x * x, axis=-1, keepdims=True) + EPS_NORM) * w

        def taylor_feature_map(x):
            d = x.shape[-1]
            iu, ju = jnp.triu_indices(d)
            scale = jnp.where(iu == ju, 0.5, 1.0 / math.sqrt(2.0)).astype(x.dtype)
            quad = x[..., iu] * x[..., ju] * scale
            ones = jnp.ones(x.shape[:-1] + (1,), dtype=x.dtype)
            return jnp.concatenate([ones, x, quad], axis=-1)

        def linear_attention_causal(q_phi, k_phi, v):
            B, T, H, F = q_phi.shape
            D = v.shape[-1]
            Nc = T // CHUNK
            qc = q_phi.reshape(B, Nc, CHUNK, H, F).transpose(1, 0, 2, 3, 4)
            kc = k_phi.reshape(B, Nc, CHUNK, H, F).transpose(1, 0, 2, 3, 4)
            vc = v.reshape(B, Nc, CHUNK, H, D).transpose(1, 0, 2, 3, 4)
            causal = jnp.tril(jnp.ones((CHUNK, CHUNK), dtype=q_phi.dtype))

            def step(carry, inp):
                kv, ksum = carry
                qb, kb, vb = inp
                A = jnp.einsum('bchf,bshf->bhcs', qb, kb) * causal
                y = jnp.einsum('bhcs,bshd->bchd', A, vb) + jnp.einsum('bchf,bhfd->bchd', qb, kv)
                z = jnp.einsum('bhcs->bch', A) + jnp.einsum('bchf,bhf->bch', qb, ksum)
                kv = kv + jnp.einsum('bshf,bshd->bhfd', kb, vb)
                ksum = ksum + kb.sum(axis=1)
                return ((kv, ksum), y / (z[..., None] + EPS_LIN))
            kv0 = jnp.zeros((B, H, F, D), dtype=q_phi.dtype)
            ks0 = jnp.zeros((B, H, F), dtype=q_phi.dtype)
            _, ys = jax.lax.scan(step, (kv0, ks0), (qc, kc, vc))
            return ys.transpose(1, 0, 2, 3, 4).reshape(B, T, H, D)

        def sliding_window_attention(q, k, v):
            B, T, H, D = q.shape
            scale = 1.0 / math.sqrt(D)
            t = jnp.arange(T)
            allowed = (t[None, :] <= t[:, None]) & (t[None, :] >= t[:, None] - WINDOW)
            scores = jnp.einsum('bqhd,bkhd->bhqk', q, k) * scale
            scores = jnp.where(allowed[None, None], scores, -jnp.inf)
            attn = jax.nn.softmax(scores, axis=-1)
            out = jnp.einsum('bhqk,bkhd->bqhd', attn, v)
            return out.reshape(B, T, H * D)
        key = jax.random.key(seed)
        ks = jax.random.split(key, 7)
        B, T = (2, 256)
        s = 0.02
        return {'x': jax.random.normal(ks[0], (B, T, D_MODEL), jnp.float32), 'norm_w': jnp.ones((D_MODEL,), jnp.float32), 'Wq': jax.random.normal(ks[1], (D_MODEL, D_MODEL), jnp.float32) * s, 'Wk': jax.random.normal(ks[2], (D_MODEL, D_MODEL), jnp.float32) * s, 'Wv': jax.random.normal(ks[3], (D_MODEL, D_MODEL), jnp.float32) * s, 'Wqf': jax.random.normal(ks[4], (HEAD_DIM, FEAT), jnp.float32) * s, 'Wkf': jax.random.normal(ks[5], (HEAD_DIM, FEAT), jnp.float32) * s, 'Wout': jax.random.normal(ks[6], (2 * D_MODEL, D_MODEL), jnp.float32) * s}
    _L0_attn_in = _L0_attn_setup()

    def _L0_ffn_setup():
        import jax, jax.numpy as jnp
        import numpy as np
        D_IN, D_HID = (128, 512)

        def _ternary(key, shape):
            return jax.random.randint(key, shape, -1, 2).astype(jnp.float32)

        def _tlin(x, w, s):
            return jnp.einsum('bsi,oi->bso', x, w) * s
        key = jax.random.key(seed)
        ks = jax.random.split(key, 12)
        inv = lambda fan: 1.0 / np.sqrt(fan).astype(np.float32)
        return {'x': jax.random.normal(ks[0], (4, 256, D_IN), dtype=jnp.float32), 'w1_w': _ternary(ks[1], (D_HID, D_IN)), 'w1_s': jax.random.uniform(ks[2], (D_HID,), dtype=jnp.float32) * inv(D_IN), 'w2_w': _ternary(ks[3], (D_HID, D_IN)), 'w2_s': jax.random.uniform(ks[4], (D_HID,), dtype=jnp.float32) * inv(D_IN), 'h1_w': _ternary(ks[5], (D_HID, D_HID)), 'h1_s': jax.random.uniform(ks[6], (D_HID,), dtype=jnp.float32) * inv(D_HID), 'h2_w': _ternary(ks[7], (D_HID, D_HID)), 'h2_s': jax.random.uniform(ks[8], (D_HID,), dtype=jnp.float32) * inv(D_HID), 'w3_w': _ternary(ks[9], (D_IN, D_HID)), 'w3_s': jax.random.uniform(ks[10], (D_IN,), dtype=jnp.float32) * inv(D_HID)}
    _L0_ffn_in = _L0_ffn_setup()

    def _L1_attn_setup():
        import jax, jax.numpy as jnp
        import numpy as np
        DMODEL = 128
        DHIDDEN = 128
        N_HEAD = 16
        HEAD_DIM = DHIDDEN // N_HEAD
        B, S = (4, 256)

        def _layernorm(x, gamma, beta, eps=1e-05):
            mu = jnp.mean(x, axis=-1, keepdims=True)
            var = jnp.var(x, axis=-1, keepdims=True)
            return (x - mu) * jax.lax.rsqrt(var + eps) * gamma + beta
        key = jax.random.key(seed)
        ks = jax.random.split(key, 10)
        sc = 1.0 / np.sqrt(DMODEL)
        return {'x': jax.random.normal(ks[0], (B, S, DMODEL), dtype=jnp.float32), 'Wq': jax.random.normal(ks[1], (DMODEL, DHIDDEN), dtype=jnp.float32) * sc, 'bq': jnp.zeros((DHIDDEN,), dtype=jnp.float32), 'Wk': jax.random.normal(ks[2], (DMODEL, DHIDDEN), dtype=jnp.float32) * sc, 'bk': jnp.zeros((DHIDDEN,), dtype=jnp.float32), 'Wv': jax.random.normal(ks[3], (DMODEL, DHIDDEN), dtype=jnp.float32) * sc, 'bv': jnp.zeros((DHIDDEN,), dtype=jnp.float32), 'Wo': jax.random.normal(ks[4], (DHIDDEN, DMODEL), dtype=jnp.float32) * sc, 'bo': jnp.zeros((DMODEL,), dtype=jnp.float32), 'ln_gamma': jnp.ones((DMODEL,), dtype=jnp.float32), 'ln_beta': jnp.zeros((DMODEL,), dtype=jnp.float32)}
    _L1_attn_in = _L1_attn_setup()

    def _L1_ffn_setup():
        import jax, jax.numpy as jnp
        import numpy as np
        HIDDEN = 128
        INTER = 512
        N_EXPERTS = 8
        TOP_K = 2
        INIT_STD = 0.02
        key = jax.random.key(seed)
        ks = jax.random.split(key, 6)
        x = jax.random.normal(ks[0], (2, 128, HIDDEN), dtype=jnp.float32)
        Wg = jax.random.normal(ks[1], (N_EXPERTS, HIDDEN), dtype=jnp.float32) * INIT_STD
        W1 = jax.random.normal(ks[2], (N_EXPERTS, HIDDEN, INTER), dtype=jnp.float32) * INIT_STD
        b1 = jnp.zeros((N_EXPERTS, INTER), dtype=jnp.float32)
        W2 = jax.random.normal(ks[3], (N_EXPERTS, INTER, HIDDEN), dtype=jnp.float32) * INIT_STD
        b2 = jnp.zeros((N_EXPERTS, HIDDEN), dtype=jnp.float32)
        return {'x': x, 'Wg': Wg, 'W1': W1, 'b1': b1, 'W2': W2, 'b2': b2}
    _L1_ffn_in = _L1_ffn_setup()
    _d = {'L0_attn_x': _L0_attn_in['x'], 'L0_attn_norm_w': _L0_attn_in['norm_w'], 'L0_attn_Wq': _L0_attn_in['Wq'], 'L0_attn_Wk': _L0_attn_in['Wk'], 'L0_attn_Wv': _L0_attn_in['Wv'], 'L0_attn_Wqf': _L0_attn_in['Wqf'], 'L0_attn_Wkf': _L0_attn_in['Wkf'], 'L0_attn_Wout': _L0_attn_in['Wout'], 'L0_ffn_w1_w': _L0_ffn_in['w1_w'], 'L0_ffn_w1_s': _L0_ffn_in['w1_s'], 'L0_ffn_w2_w': _L0_ffn_in['w2_w'], 'L0_ffn_w2_s': _L0_ffn_in['w2_s'], 'L0_ffn_h1_w': _L0_ffn_in['h1_w'], 'L0_ffn_h1_s': _L0_ffn_in['h1_s'], 'L0_ffn_h2_w': _L0_ffn_in['h2_w'], 'L0_ffn_h2_s': _L0_ffn_in['h2_s'], 'L0_ffn_w3_w': _L0_ffn_in['w3_w'], 'L0_ffn_w3_s': _L0_ffn_in['w3_s'], 'L1_attn_Wq': _L1_attn_in['Wq'], 'L1_attn_bq': _L1_attn_in['bq'], 'L1_attn_Wk': _L1_attn_in['Wk'], 'L1_attn_bk': _L1_attn_in['bk'], 'L1_attn_Wv': _L1_attn_in['Wv'], 'L1_attn_bv': _L1_attn_in['bv'], 'L1_attn_Wo': _L1_attn_in['Wo'], 'L1_attn_bo': _L1_attn_in['bo'], 'L1_attn_ln_gamma': _L1_attn_in['ln_gamma'], 'L1_attn_ln_beta': _L1_attn_in['ln_beta'], 'L1_ffn_Wg': _L1_ffn_in['Wg'], 'L1_ffn_W1': _L1_ffn_in['W1'], 'L1_ffn_b1': _L1_ffn_in['b1'], 'L1_ffn_W2': _L1_ffn_in['W2'], 'L1_ffn_b2': _L1_ffn_in['b2']}
    _x0 = _d['L0_attn_x']
    _d['L0_attn_x'] = jax.random.normal(jax.random.fold_in(jax.random.key(seed), 1), (8, 512, 128), dtype=_x0.dtype)
    del _x0
    return _d

def reference(L0_attn_x, L0_attn_norm_w, L0_attn_Wq, L0_attn_Wk, L0_attn_Wv, L0_attn_Wqf, L0_attn_Wkf, L0_attn_Wout, L0_ffn_w1_w, L0_ffn_w1_s, L0_ffn_w2_w, L0_ffn_w2_s, L0_ffn_h1_w, L0_ffn_h1_s, L0_ffn_h2_w, L0_ffn_h2_s, L0_ffn_w3_w, L0_ffn_w3_s, L1_attn_Wq, L1_attn_bq, L1_attn_Wk, L1_attn_bk, L1_attn_Wv, L1_attn_bv, L1_attn_Wo, L1_attn_bo, L1_attn_ln_gamma, L1_attn_ln_beta, L1_ffn_Wg, L1_ffn_W1, L1_ffn_b1, L1_ffn_W2, L1_ffn_b2):

    def _L0_attn_ref(x, norm_w, Wq, Wk, Wv, Wqf, Wkf, Wout):
        import jax, jax.numpy as jnp
        import numpy as np
        import math
        D_MODEL = 128
        N_HEADS = 16
        HEAD_DIM = D_MODEL // N_HEADS
        FEAT = 16
        WINDOW = 64
        EPS_NORM = 1e-06
        EPS_LIN = 1e-06
        CHUNK = 128

        def rmsnorm(x, w):
            return x * jax.lax.rsqrt(jnp.mean(x * x, axis=-1, keepdims=True) + EPS_NORM) * w

        def taylor_feature_map(x):
            d = x.shape[-1]
            iu, ju = jnp.triu_indices(d)
            scale = jnp.where(iu == ju, 0.5, 1.0 / math.sqrt(2.0)).astype(x.dtype)
            quad = x[..., iu] * x[..., ju] * scale
            ones = jnp.ones(x.shape[:-1] + (1,), dtype=x.dtype)
            return jnp.concatenate([ones, x, quad], axis=-1)

        def linear_attention_causal(q_phi, k_phi, v):
            B, T, H, F = q_phi.shape
            D = v.shape[-1]
            Nc = T // CHUNK
            qc = q_phi.reshape(B, Nc, CHUNK, H, F).transpose(1, 0, 2, 3, 4)
            kc = k_phi.reshape(B, Nc, CHUNK, H, F).transpose(1, 0, 2, 3, 4)
            vc = v.reshape(B, Nc, CHUNK, H, D).transpose(1, 0, 2, 3, 4)
            causal = jnp.tril(jnp.ones((CHUNK, CHUNK), dtype=q_phi.dtype))

            def step(carry, inp):
                kv, ksum = carry
                qb, kb, vb = inp
                A = jnp.einsum('bchf,bshf->bhcs', qb, kb) * causal
                y = jnp.einsum('bhcs,bshd->bchd', A, vb) + jnp.einsum('bchf,bhfd->bchd', qb, kv)
                z = jnp.einsum('bhcs->bch', A) + jnp.einsum('bchf,bhf->bch', qb, ksum)
                kv = kv + jnp.einsum('bshf,bshd->bhfd', kb, vb)
                ksum = ksum + kb.sum(axis=1)
                return ((kv, ksum), y / (z[..., None] + EPS_LIN))
            kv0 = jnp.zeros((B, H, F, D), dtype=q_phi.dtype)
            ks0 = jnp.zeros((B, H, F), dtype=q_phi.dtype)
            _, ys = jax.lax.scan(step, (kv0, ks0), (qc, kc, vc))
            return ys.transpose(1, 0, 2, 3, 4).reshape(B, T, H, D)

        def sliding_window_attention(q, k, v):
            B, T, H, D = q.shape
            scale = 1.0 / math.sqrt(D)
            t = jnp.arange(T)
            allowed = (t[None, :] <= t[:, None]) & (t[None, :] >= t[:, None] - WINDOW)
            scores = jnp.einsum('bqhd,bkhd->bhqk', q, k) * scale
            scores = jnp.where(allowed[None, None], scores, -jnp.inf)
            attn = jax.nn.softmax(scores, axis=-1)
            out = jnp.einsum('bhqk,bkhd->bqhd', attn, v)
            return out.reshape(B, T, H * D)
        B, T, _ = x.shape
        h = rmsnorm(x, norm_w)
        q = (h @ Wq).reshape(B, T, N_HEADS, HEAD_DIM)
        k = (h @ Wk).reshape(B, T, N_HEADS, HEAD_DIM)
        v = (h @ Wv).reshape(B, T, N_HEADS, HEAD_DIM)
        q_phi = taylor_feature_map(q @ Wqf)
        k_phi = taylor_feature_map(k @ Wkf)
        lin = linear_attention_causal(q_phi, k_phi, v).reshape(B, T, D_MODEL)
        win = sliding_window_attention(q, k, v)
        out = jnp.concatenate([lin, win], axis=-1) @ Wout
        return x + out

    def _L0_ffn_ref(x, w1_w, w1_s, w2_w, w2_s, h1_w, h1_s, h2_w, h2_s, w3_w, w3_s):
        import jax, jax.numpy as jnp
        import numpy as np
        D_IN, D_HID = (128, 512)

        def _ternary(key, shape):
            return jax.random.randint(key, shape, -1, 2).astype(jnp.float32)

        def _tlin(x, w, s):
            return jnp.einsum('bsi,oi->bso', x, w) * s
        h = jax.nn.silu(_tlin(x, w1_w, w1_s)) * _tlin(x, w2_w, w2_s)
        h = jax.nn.gelu(_tlin(h, h1_w, h1_s), approximate=False)
        h = jax.nn.gelu(_tlin(h, h2_w, h2_s), approximate=False)
        return _tlin(h, w3_w, w3_s)

    def _L1_attn_ref(x, Wq, bq, Wk, bk, Wv, bv, Wo, bo, ln_gamma, ln_beta):
        import jax, jax.numpy as jnp
        import numpy as np
        DMODEL = 128
        DHIDDEN = 128
        N_HEAD = 16
        HEAD_DIM = DHIDDEN // N_HEAD
        B, S = (4, 256)

        def _layernorm(x, gamma, beta, eps=1e-05):
            mu = jnp.mean(x, axis=-1, keepdims=True)
            var = jnp.var(x, axis=-1, keepdims=True)
            return (x - mu) * jax.lax.rsqrt(var + eps) * gamma + beta
        b, s, _ = x.shape
        h = _layernorm(x, ln_gamma, ln_beta)
        q = h @ Wq + bq
        k = h @ Wk + bk
        v = h @ Wv + bv
        q = q.reshape(b, s, N_HEAD, HEAD_DIM).transpose(0, 2, 1, 3)
        k = k.reshape(b, s, N_HEAD, HEAD_DIM).transpose(0, 2, 1, 3)
        v = v.reshape(b, s, N_HEAD, HEAD_DIM).transpose(0, 2, 1, 3)
        scores = jnp.einsum('bhqd,bhkd->bhqk', q, k) / np.sqrt(HEAD_DIM)
        causal = jnp.tril(jnp.ones((s, s), dtype=bool))
        scores = jnp.where(causal, scores, jnp.finfo(scores.dtype).min)
        attn = jax.nn.softmax(scores, axis=-1)
        out = jnp.einsum('bhqk,bhkd->bhqd', attn, v)
        out = out.transpose(0, 2, 1, 3).reshape(b, s, DHIDDEN)
        return out @ Wo + bo

    def _L1_ffn_ref(x, Wg, W1, b1, W2, b2):
        import jax, jax.numpy as jnp
        import numpy as np
        HIDDEN = 128
        INTER = 512
        N_EXPERTS = 8
        TOP_K = 2
        INIT_STD = 0.02
        orig_shape = x.shape
        xt = x.reshape(-1, HIDDEN)
        T = xt.shape[0]
        logits = xt @ Wg.T
        topk_logits, topk_idx = jax.lax.top_k(logits, TOP_K)
        w = jax.nn.softmax(topk_logits, axis=-1)
        rows = jnp.arange(T)[:, None]
        gates = jnp.zeros((T, N_EXPERTS), xt.dtype).at[rows, topk_idx].add(w)
        h = jnp.einsum('th,ehi->tei', xt, W1) + b1
        h = jax.nn.gelu(h, approximate=False)
        o = jnp.einsum('tei,eih->teh', h, W2) + b2
        y = jnp.einsum('te,teh->th', gates, o)
        return y.reshape(orig_shape)
    x = L0_attn_x
    xn = _layernorm(x, axis=-1)
    x = x + _L0_attn_ref(xn, L0_attn_norm_w, L0_attn_Wq, L0_attn_Wk, L0_attn_Wv, L0_attn_Wqf, L0_attn_Wkf, L0_attn_Wout) + _L0_ffn_ref(xn, L0_ffn_w1_w, L0_ffn_w1_s, L0_ffn_w2_w, L0_ffn_w2_s, L0_ffn_h1_w, L0_ffn_h1_s, L0_ffn_h2_w, L0_ffn_h2_s, L0_ffn_w3_w, L0_ffn_w3_s)
    xn = _layernorm(x, axis=-1)
    x = x + _L1_attn_ref(xn, L1_attn_Wq, L1_attn_bq, L1_attn_Wk, L1_attn_bk, L1_attn_Wv, L1_attn_bv, L1_attn_Wo, L1_attn_bo, L1_attn_ln_gamma, L1_attn_ln_beta) + _L1_ffn_ref(xn, L1_ffn_Wg, L1_ffn_W1, L1_ffn_b1, L1_ffn_W2, L1_ffn_b2)
    return x

_drawn_inputs = setup_inputs


def setup_inputs(seed=0):
    import zlib

    import numpy as np

    out = dict(_drawn_inputs(seed))
    spreads = {'L0_attn_norm_w': (1.0, 0.2),
     'L1_attn_bq': (0.0, 0.1),
     'L1_attn_bk': (0.0, 0.1),
     'L1_attn_bv': (0.0, 0.1),
     'L1_attn_bo': (0.0, 0.1),
     'L1_attn_ln_gamma': (1.0, 0.2),
     'L1_attn_ln_beta': (0.0, 0.1),
     'L1_ffn_b1': (0.0, 0.1),
     'L1_ffn_b2': (0.0, 0.1)}
    factors = {}
    for name, (base, spread) in spreads.items():
        noise = np.random.default_rng([zlib.crc32(name.encode()), seed]).standard_normal(out[name].shape)
        drawn = base * np.exp(spread * noise) if base else spread * noise
        out[name] = jnp.asarray(drawn.astype(out[name].dtype))
    for name, factor in factors.items():
        out[name] = (out[name] * factor).astype(out[name].dtype)
    return out
```

```python
from contextlib import ExitStack

import concourse.bass as bass
from concourse import mybir

F32 = mybir.dt.float32
F32R = mybir.dt.float32r
BF16 = mybir.dt.bfloat16
ALU = mybir.AluOpType
ACT = mybir.ActivationFunctionType
AX_X = mybir.AxisListType.X

P = 128
NB, T = 8, 512
NT = T // P
H, D = 16, 8
G, HG = 4, 4
ROWS = 32
FC = 4
E = 8
WIN = 64
WQ = P + WIN
LIN, SLIDE, CAUSAL = range(3)
NEG = -1e30
EPS_LN, EPS_RMS, EPS_LIN = 1e-5, 1e-6, 1e-6
SCALE = float(D) ** -0.5

TRI_AT = {0: 0, 1: 512, 3: 896, 2: 1024}
TRI_N = {j: T - P * j for j in range(NT)}
PROBS = 1280
SLIDE_AT = {j: WQ * j for j in range(NT)}
SLIDE_N = {j: min(WQ, T - P * j) for j in range(NT)}

EARLY = 4
CMAX_OF = [[0], [1], [2], [3], [4, 5], [6, 7]]
SENT, PLACED = 3 * 16, HG * 16
N_LOADS = 38
SLOTS = 3

BANKS = {"score": 3, "misc": 2}


def tri_units(tag):
    return [f"{tag}{u}" for p in range(H // 2) for u in (f"{2 * p}a", f"{2 * p}b", f"{2 * p + 1}a", f"{2 * p + 1}b", f"_{p}")]


def slide_units(tag):
    return [f"{tag}{h}{u}" for h in range(H) for u in "ab"]


def expert_units(e):
    return [f"moe{e}_{c}" for c in range(FC)] + [f"moe{e}_out"]


UNITS = {
    ("first", "score"): slide_units("smax") + tri_units("lin") + slide_units("slide"),
    ("first", "misc"): ["xnT", "hT", "q", "k", "v", "qm"] + [f"{w}{c}" for c in range(FC) for w in ("gate", "up")]
    + [f"h1_{c}" for c in range(FC)] + ["slide_max", "h2_0"]
    + [u for g in range(1, G) for u in (f"h2_{g}", f"rows{LIN}_{g - 1}")] + [f"rows{LIN}_{G - 1}", f"cols{LIN}"]
    + [f"rows{SLIDE}_{g}" for g in range(G)] + [f"cols{SLIDE}"],
    ("second", "score"): tri_units("cmax") + tri_units("causal"),
    ("second", "misc"): ["xnT", "hT", "q", "k", "v", "logits"] + [u for e in range(EARLY) for u in expert_units(e)]
    + ["causal_max"] + [f"rows{CAUSAL}_{g}" for g in range(G)] + ["gatesT", f"cols{CAUSAL}"],
    ("late", "misc"): [u for e in range(EARLY, E) for u in expert_units(e)],
}
PLACE = {key: {u: (n % BANKS[key[1]], n // BANKS[key[1]]) for n, u in enumerate(units)} for key, units in UNITS.items()}


def units_in(key, bank):
    return len(range(bank, len(UNITS[key]), BANKS[key[1]]))


SHAPES = {
    "x": (NB, T, P), "wq": (P, P), "wqT": (P, P), "wk": (P, P), "wv": (P, P), "wqfT": (16, P), "wkfT": (16, P),
    "wout": (2, P, P), "norm_w": (P, 1),
    "w1T": (P, T), "w2T": (P, T), "h1T": (T, T), "h2T": (T, T), "w3T": (T, P),
    "s1": (P, FC), "s2": (P, FC), "sh1": (P, FC), "sh2": (P, FC), "s3": (P,),
    "wq1": (P, P), "wk1": (P, P), "wv1": (P, P), "wo1": (P, P), "bq1": (P, 1), "bk1": (P, 1), "bv1": (P,), "bo1": (P,),
    "gamma": (P, 1), "beta": (P, 1), "wgT": (P, E),
    "W1": (E, P, T), "b1": (P, E * FC), "W2": (E, T, P), "b2": (E, P),
    "ident": (P, P), "causal_neg": (P, P), "slide_neg": (P, WQ), "earlier": (P, E * E), "blocks": (P, P),
    "slot_q": (H, D, T), "slot_k": (H, D, T),
}


def build(nc, dram, out):
    with ExitStack() as ctx:
        def sb(name, shape, dt=F32):
            return ctx.enter_context(nc.sbuf_tensor(name, shape, dt))

        def pb(name, shape=(P, 512)):
            return ctx.enter_context(nc.psum_tensor(name, list(shape), F32))

        wq, wk, wv, wqm = (sb(n, [P, P]) for n in ("wq_s", "wk_s", "wv_s", "wqm_s"))
        wout = sb("wout_s", [P, 2, P])
        norm_w, gamma, beta, bq1, bk1 = (sb(n + "_s", [P, 1]) for n in ("norm_w", "gamma", "beta", "bq1", "bk1"))
        w1T, w2T = sb("w1T_s", [P, T]), sb("w2T_s", [P, T])
        h1T, h2T, w3T = sb("h1T_s", [P, FC, T]), sb("h2T_s", [P, FC, T]), sb("w3T_s", [P, FC, P])
        s1, s2, sh1, sh2 = (sb(n + "_s", [P, FC]) for n in ("s1", "s2", "sh1", "sh2"))
        bv1, bo1 = (sb(n + "_s", [P, P]) for n in ("bv1", "bo1"))
        wq1, wk1, wv1, wo1 = (sb(n + "_s", [P, P]) for n in ("wq1", "wk1", "wv1", "wo1"))
        wgT = sb("wgT_s", [P, E])
        W1, W2 = sb("W1_s", [P, E, T]), sb("W2_s", [P, E, FC, P])
        b1, b2 = sb("b1_s", [P, E * FC]), sb("b2_s", [E, P])
        ident, identb = sb("ident_s", [P, P]), sb("identb", [P, P], BF16)
        causal_neg, slide_neg = sb("causal_neg_s", [P, P], BF16), sb("slide_neg_s", [P, WQ], BF16)
        earlier = sb("earlier_s", [P, E * E])
        half_neg = sb("half_neg", [P, 2 * NT])

        x_in, xs, xn, hrow = (sb(n, [P, NT, P]) for n in ("x_in", "xs", "xn", "hrow"))
        xnT, hT = sb("xnT_s", [P, T]), sb("hT_s", [P, T])
        bn, mv, pw, rs = sb("bn", [P, NT, 6]), sb("mv", [P, NT, 2]), sb("pw", [P, 2, NT]), sb("rs", [P, 2, NT])
        hi, lo = sb("hi", [P, 2, T], F32R), sb("lo", [P, 2, T], F32R)
        Q, QM, K = sb("Q", [P, G, T], F32R), sb("QM", [P, G, T], F32R), sb("K", [P, H, T], F32R)
        V = sb("V", [P, NT, H, ROWS])
        probs = sb("probs", [P, SLOTS, 2 * PROBS])
        mx, mrow = sb("mx", [P, P]), sb("mrow", [HG * G * NT, P], F32R)
        ot = sb("ot", [P, 2, T])
        den, rden = sb("den", [P, NT, HG]), sb("rden", [P, NT, HG])
        attn = sb("attn", [P, NT, P])
        attnT = sb("attnT", [P, 2, T])
        ha, hb = sb("ha", [P, FC, T]), sb("hb", [P, FC, T])
        x1, y = sb("x1", [P, NT, P]), sb("y", [P, NT, P])
        lg, lgs, ex, exs, gates, rank = (sb(n, [P, NT, E]) for n in ("lg", "lgs", "ex", "exs", "gates", "rank"))
        above, equal = sb("above", [P, NT, E * E]), sb("equal", [P, NT, E * E])
        m1, gsum, rsum = (sb(n, [P, NT]) for n in ("m1", "gsum", "rsum"))
        gatesT = sb("gatesT_s", [E, T])
        x1T = sb("x1T", [P, T])
        result = x1
        wqT, blocks, bdm, s3, causal_f = (ha[:, n // 4, P * (n % 4):P * (n % 4 + 1)] for n in range(5))
        slide_f = ha[:, 2, 0:WQ]
        wqfT, wkfT = (hb[0:16, 0, P * n:P * (n + 1)] for n in range(2))

        score = [pb(f"score{i}") for i in range(BANKS["score"])]
        misc = [pb(f"misc{i}") for i in range(BANKS["misc"])]
        heads = [pb(f"heads{i}") for i in range(2)]
        acc = pb("acc")

        scratch = {n: nc.dram_tensor(f"slots_of_{n}", (H, ROWS, T), F32, kind="Internal").ap() for n in ("q", "k", "qm")}

        counts = {
            "unread": (0, 0), "weights": (0, 0), "slots_set": (0, 0), "setup_pe": (0, 0), "setup_dve": (0, 0), "setup_done": (0, 0),
            "x_loaded": (16, 0), "stored": (16, 16), "xs_ready": (1, 0), "y_init": (1, 0),
            "stats1": (1, 0), "stats2": (1, 0), "powered1": (1, 0), "powered2": (1, 0), "rows1": (2, 0), "rows2": (2, 0),
            "norm1_laps": (2, 0), "norm2_laps": (2, 0), "first_laps": (3 * G, 0), "second_laps": (8 + G, 0),
            "hi_q": (2, 0), "hi_k": (2, 0), "hi_qm": (1, 0),
            "sent_q": (2 * SENT, 16), "sent_k": (2 * SENT, 16), "sent_qm": (SENT, 16),
            "slots_q": (2 * PLACED, 0), "slots_k": (2 * PLACED, 0), "slots_qm": (PLACED, 0), "max_placed": (2 * PLACED, 0),
            "slide_near": (H // 2, 0), "probs_ready": (3 * H // 2, 0),
            "heads_out": (3 * G, 2), "heads_copied": (3 * G, 2),
            "acc_ready": (2, 0), "acc_read": (2, 1), "shifted": (1, 0), "exped": (1, 0), "gated": (1, 0),
        }
        for key in UNITS:
            for bank in range(BANKS[key[1]]):
                for what in ("full", "taken"):
                    counts[f"{key[0]}_{key[1]}_{what}{bank}"] = (units_in(key, bank), 0)
        S = {name: ctx.enter_context(nc.semaphore(name)) for name in counts}

        def due(name, b, count):
            per_sequence, setup = counts[name]
            return b * per_sequence + (setup + count)

        def full_sem(key, unit):
            return S[f"{key[0]}_{key[1]}_full{PLACE[key][unit][0]}"]

        def taken_sem(key, unit):
            return S[f"{key[0]}_{key[1]}_taken{PLACE[key][unit][0]}"]

        def turn_of(key, b, unit):
            return b * units_in(key, PLACE[key][unit][0]) + (PLACE[key][unit][1] + 1)

        def last_units(key):
            return UNITS[key][-BANKS[key[1]]:]

        def bank_of(key, unit):
            return {"score": score, "misc": misc}[key[1]][PLACE[key][unit][0]]

        FM, FS, SM, SS, LM = ("first", "misc"), ("first", "score"), ("second", "misc"), ("second", "score"), ("late", "misc")
        block = ctx.enter_context(nc.Block())
        x_v = dram["x"].rearrange("b (t p) d -> b p t d", p=P)
        out_v = out.rearrange("b (t p) d -> b p t d", p=P)

        @block.sync
        def _(sp):
            loads = [(wqfT, dram["wqfT"]), (wkfT, dram["wkfT"]), (wqT, dram["wqT"]), (blocks, dram["blocks"]),
                     (wk[:, :], dram["wk"]), (wq[:, :], dram["wq"]), (wv[:, :], dram["wv"]), (ident[:, :], dram["ident"]),
                     (wout[:, :, :], dram["wout"].rearrange("a p n -> p a n")), (norm_w[:, :], dram["norm_w"]),
                     (w1T[:, :], dram["w1T"]), (w2T[:, :], dram["w2T"]),
                     (h1T[:, :, :], dram["h1T"].rearrange("(c p) n -> p c n", p=P)), (h2T[:, :, :], dram["h2T"].rearrange("(c p) n -> p c n", p=P)),
                     (w3T[:, :, :], dram["w3T"].rearrange("(c p) n -> p c n", p=P)),
                     (s1[:, :], dram["s1"]), (s2[:, :], dram["s2"]), (sh1[:, :], dram["sh1"]), (sh2[:, :], dram["sh2"]),
                     (s3, dram["s3"].partition_broadcast(P)), (bv1[:, :], dram["bv1"].partition_broadcast(P)),
                     (bo1[:, :], dram["bo1"].partition_broadcast(P)),
                     (wq1[:, :], dram["wq1"]), (wk1[:, :], dram["wk1"]), (wv1[:, :], dram["wv1"]), (wo1[:, :], dram["wo1"]),
                     (bq1[:, :], dram["bq1"]), (bk1[:, :], dram["bk1"]), (gamma[:, :], dram["gamma"]), (beta[:, :], dram["beta"]),
                     (wgT[:, :], dram["wgT"]), (W1[:, :, :], dram["W1"].rearrange("e p n -> p e n")),
                     (W2[:, :, :, :].rearrange("p e c n -> p (e c) n"), dram["W2"].rearrange("e (c p) n -> p (e c) n", p=P)),
                     (b1[:, :], dram["b1"]), (b2[:, :], dram["b2"]), (causal_f, dram["causal_neg"]), (slide_f, dram["slide_neg"]),
                     (earlier[:, :], dram["earlier"]), (x_in[:, :, :], x_v[0])]
            for dst, src in loads[:-1]:
                sp.dma_start(dst, src).then_inc(S["weights"], 16)
            sp.dma_start(*loads[-1]).then_inc(S["x_loaded"], 16)
            assert len(loads) - 1 == N_LOADS
            for n, name in enumerate(("q", "k", "qm")):
                sp.dma_start(scratch[name][:, 3 * D:4 * D, :], dram["slot_k" if name == "k" else "slot_q"]).then_inc(S["slots_set"], 16)
            sp.wait_ge(S["slots_set"], 16 * len(scratch))

            def send(name, part, slots):
                src = {"q": 0, "k": 1, "qm": 0}[name]
                view = scratch[name].rearrange("h (s d) t -> s h d t", d=D)
                for s in slots:
                    sp.dma_start(view[s], part[:, src, :].bitcast(F32)).then_inc(S[f"sent_{name}"], 16)

            def fetch(name, heads_of):
                groups = scratch[name].rearrange("(g i) r t -> i r g t", i=HG)
                for i in range(HG):
                    sp.dma_start(heads_of(i), groups[i]).then_inc(S[f"slots_{name}"], 16)

            def q_rows(i):
                return Q[ROWS * i:ROWS * (i + 1), :, :].bitcast(F32)

            def qm_rows(i):
                return QM[ROWS * i:ROWS * (i + 1), :, :].bitcast(F32)

            def k_rows(i):
                return K[ROWS * i:ROWS * (i + 1), i:H:HG, :].bitcast(F32)

            def place_max(b, key, unit):
                sp.wait_ge(taken_sem(key, unit), turn_of(key, b, unit))
                for i in range(HG):
                    row = ROWS * i + 3 * D
                    sp.dma_start(Q[row:row + 1, :, :].rearrange("p g (n t) -> p (g n) t", t=P).bitcast(F32),
                                 mrow[G * NT * i:G * NT * (i + 1), :].bitcast(F32)).then_inc(S["max_placed"], 16)

            def split_and_spread(b, key, names, nth):
                for name in names:
                    sp.wait_ge(S[f"hi_{name}"], due(f"hi_{name}", b, nth))
                    send(name, hi, (0, 2) if name == "k" else (0, 1))
                    sp.wait_ge(taken_sem(key, name), turn_of(key, b, name))
                    send(name, lo, (1,) if name == "k" else (2,))
                for name in names:
                    sp.wait_ge(S[f"sent_{name}"], due(f"sent_{name}", b, SENT * nth))
                    fetch(name, {"q": q_rows, "k": k_rows, "qm": qm_rows}[name])

            sp.wait_ge(S["setup_done"], 1)
            with sp.Fori(0, NB) as b:
                sp.wait_ge(S["heads_out"], due("heads_out", b, 0))
                sp.sem_inc(S["unread"], 1)
                split_and_spread(b, FM, ("q", "k", "qm"), 1)
                place_max(b, FM, "slide_max")
                sp.wait_ge(S["heads_out"], due("heads_out", b, 2 * G))
                sp.sem_inc(S["unread"], 1)
                split_and_spread(b, SM, ("q", "k"), 2)
                sp.wait_ge(S["xs_ready"], due("xs_ready", b, 1))
                sp.sem_inc(S["unread"], 1)
                sp.dma_start(x_in[:, :, :], x_v[(b + 1) & (NB - 1)]).then_inc(S["x_loaded"], 16)
                place_max(b, SM, "causal_max")
                sp.wait_ge(taken_sem(LM, f"moe{E - 1}_out"), turn_of(LM, b, f"moe{E - 1}_out"))
                sp.dma_start(out_v[b], result[:, :, :]).then_inc(S["stored"], 16)
            sp.wait_ge(S["stored"], 16 + 16 * NB)

        @block.tensor
        def _(pe):
            def to_misc(key, b, unit):
                at = UNITS[key].index(unit)
                if at >= BANKS["misc"]:
                    pe.wait_ge(taken_sem(key, UNITS[key][at - BANKS["misc"]]), turn_of(key, b, UNITS[key][at - BANKS["misc"]]))
                return bank_of(key, unit)

            def turn(key, b, unit, tile, rows=P):
                bank = to_misc(key, b, unit)
                for t in range(NT):
                    mm = pe.transpose(bank[0:rows, t * P:(t + 1) * P], tile(t), ident[:, :])
                mm.then_inc(full_sem(key, unit), 1)

            def project(key, b, unit, w, x):
                pe.matmul(to_misc(key, b, unit)[:, :], w, x, start=True, stop=True).then_inc(full_sem(key, unit), 1)

            def project_rows(key, b, unit, x, w, n=P):
                bank = to_misc(key, b, unit)
                for t in range(NT):
                    mm = pe.matmul(bank[:, t * n:(t + 1) * n], x[:, t * P:(t + 1) * P], w, start=True, stop=True)
                mm.then_inc(full_sem(key, unit), 1)

            def dense(b, unit, w, src, c):
                bank = to_misc(FM, b, unit)
                for k in range(FC):
                    mm = pe.matmul(bank[:, :], w[:, k, c * P:(c + 1) * P], src[:, k, :], start=(k == 0), stop=(k == FC - 1))
                mm.then_inc(full_sem(FM, unit), 1)

            def scores_into(key, b, unit, parts):
                at = UNITS[key].index(unit)
                if at >= BANKS["score"]:
                    pe.wait_ge(taken_sem(key, UNITS[key][at - BANKS["score"]]), turn_of(key, b, UNITS[key][at - BANKS["score"]]))
                bank = bank_of(key, unit)
                for at, n, left, right, mask, mask_at in parts:
                    mm = pe.matmul(bank[:, at:at + n], left, right, start=True, stop=mask is None, skip_group_check=True)
                    if mask is not None:
                        at += mask_at
                        mm = pe.matmul(bank[:, at:at + mask.shape[1]], identb[:, :], mask, start=False, stop=True,
                                       skip_group_check=True)
                mm.then_inc(full_sem(key, unit), 1)

            def q_part(buf, h, a, n):
                return buf[:, h // HG, a:a + n]

            def slide_max(b, h):
                def part(j):
                    if j == 0:
                        return (0, P, q_part(Q, h, 0, P), K[:, h, 0:P], slide_neg[:, WIN:WQ], 0)
                    return (WQ * (j % 2), WQ, q_part(Q, h, P * j, P), K[:, h, P * j - WIN:P * (j + 1)], slide_neg[:, :], 0)
                scores_into(FS, b, f"smax{h}a", [part(0), part(1)])
                scores_into(FS, b, f"smax{h}b", [part(2), part(3)])

            def causal_max(b, p):
                def part(h, j, at):
                    return (at, P * (j + 1), q_part(Q, h, P * j, P), K[:, h, 0:P * (j + 1)], causal_neg[:, :], P * j)
                for h in (2 * p, 2 * p + 1):
                    scores_into(SS, b, f"cmax{h}a", [part(h, 3, 0)])
                    scores_into(SS, b, f"cmax{h}b", [part(h, 2, 0), part(h, 0, 384)])
                scores_into(SS, b, f"cmax_{p}", [part(2 * p, 1, 0), part(2 * p + 1, 1, 256)])

            def tri_scores(key, b, tag, p, buf):
                def part(h, j, at):
                    return (at, TRI_N[j], K[:, h, P * j:P * (j + 1)], q_part(buf, h, P * j, TRI_N[j]), None, 0)
                for h in (2 * p, 2 * p + 1):
                    scores_into(key, b, f"{tag}{h}a", [part(h, 0, 0)])
                    scores_into(key, b, f"{tag}{h}b", [part(h, 1, 0), part(h, 3, 384)])
                scores_into(key, b, f"{tag}_{p}", [part(2 * p, 2, 0), part(2 * p + 1, 2, 256)])

            def slide_scores(b, p):
                def part(h, j):
                    return (WQ * (j % 2), SLIDE_N[j], K[:, h, P * j:P * (j + 1)], q_part(Q, h, P * j, SLIDE_N[j]), None, 0)
                for h in (2 * p, 2 * p + 1):
                    scores_into(FS, b, f"slide{h}a", [part(h, 0), part(h, 1)])
                    scores_into(FS, b, f"slide{h}b", [part(h, 2), part(h, 3)])

            def weigh(b, kind, g):
                nth = G * kind + g
                pe.wait_ge(S["probs_ready"], due("probs_ready", b, 2 * nth + 2))
                pe.wait_ge(S["heads_copied"], due("heads_copied", b, nth - 1))
                starts, widths, head = (SLIDE_AT, SLIDE_N, NT * WQ) if kind == SLIDE else (TRI_AT, TRI_N, PROBS)
                for j in range(NT):
                    for i in range(HG):
                        at = head * (i % 2) + starts[j]
                        mm = pe.matmul(heads[nth % 2][ROWS * i:ROWS * (i + 1), P * j:P * j + widths[j]],
                                       V[:, j, HG * g + i, :], probs[:, (2 * nth + i // 2) % SLOTS, at:at + widths[j]],
                                       start=(j == 0), stop=(j == NT - 1), skip_group_check=True)
                mm.then_inc(S["heads_out"], 1)

            def turn_heads(key, b, kind, g):
                nth = G * kind + g
                pe.wait_ge(S["heads_copied"], due("heads_copied", b, nth + 1))
                turn(key, b, f"rows{kind}_{g}", lambda t: ot[:, nth % 2, t * P:(t + 1) * P])

            def turn_attn(key, b, kind):
                pe.wait_ge(taken_sem(key, f"rows{kind}_{G - 1}"), turn_of(key, b, f"rows{kind}_{G - 1}"))
                turn(key, b, f"cols{kind}", lambda t: attn[:, t, :])

            def turn_max(key, b, unit, scores, last):
                pe.wait_ge(taken_sem(scores, last), turn_of(scores, b, last))
                bank = to_misc(key, b, unit)
                pe.transpose(bank[:, 0:P], mx[:, :], ident[:, :]).then_inc(full_sem(key, unit), 1)

            def expert_in(key, b, e):
                for c in range(FC):
                    project(key, b, f"moe{e}_{c}", W1[:, e, c * P:(c + 1) * P], x1T[:, :])

            def expert_out(key, b, e):
                hidden = (ha, hb)[e % 2]
                pe.wait_ge(taken_sem(key, f"moe{e}_{FC - 2}"), turn_of(key, b, f"moe{e}_{FC - 2}"))
                pe.wait_ge(taken_sem(key, f"moe{e}_{FC - 1}"), turn_of(key, b, f"moe{e}_{FC - 1}"))
                bank = to_misc(key, b, f"moe{e}_out")
                for t in range(NT):
                    for k in range(FC):
                        mm = pe.matmul(bank[:, t * P:(t + 1) * P], hidden[:, k, t * P:(t + 1) * P], W2[:, e, k, :],
                                       start=(k == 0), stop=(k == FC - 1))
                mm.then_inc(full_sem(key, f"moe{e}_out"), 1)

            def first_block(b):
                pe.wait_ge(S["rows1"], due("rows1", b, 1))
                turn(FM, b, "xnT", lambda t: xn[:, t, :])
                pe.wait_ge(S["rows1"], due("rows1", b, 2))
                turn(FM, b, "hT", lambda t: hrow[:, t, :])
                pe.wait_ge(taken_sem(FM, "hT"), turn_of(FM, b, "hT"))
                project(FM, b, "q", wq[:, :], hT[:, :])
                project(FM, b, "k", wk[:, :], hT[:, :])
                project_rows(FM, b, "v", hT, wv[:, :])
                project(FM, b, "qm", wqm[:, :], hT[:, :])
                for c in range(FC):
                    project(FM, b, f"gate{c}", w1T[:, c * P:(c + 1) * P], xnT[:, :])
                    project(FM, b, f"up{c}", w2T[:, c * P:(c + 1) * P], xnT[:, :])
                pe.wait_ge(S["slots_q"], due("slots_q", b, PLACED))
                pe.wait_ge(S["slots_k"], due("slots_k", b, PLACED))
                pe.wait_ge(taken_sem(FM, f"up{FC - 1}"), turn_of(FM, b, f"up{FC - 1}"))
                for h in range(H):
                    slide_max(b, h)
                    if h % HG == HG - 1:
                        dense(b, f"h1_{h // HG}", h1T, ha, h // HG)
                turn_max(FM, b, "slide_max", FS, f"smax{H - 1}b")
                pe.wait_ge(S["slots_qm"], due("slots_qm", b, PLACED))
                for g in range(G):
                    tri_scores(FS, b, "lin", 2 * g, QM)
                    tri_scores(FS, b, "lin", 2 * g + 1, QM)
                    dense(b, f"h2_{g}", h2T, hb, g)
                    if g:
                        turn_heads(FM, b, LIN, g - 1)
                    weigh(b, LIN, g)
                turn_heads(FM, b, LIN, G - 1)
                pe.wait_ge(S["max_placed"], due("max_placed", b, PLACED))
                for g in range(G):
                    slide_scores(b, 2 * g)
                    slide_scores(b, 2 * g + 1)
                    if g:
                        turn_heads(FM, b, SLIDE, g - 1)
                    else:
                        turn_attn(FM, b, LIN)
                    weigh(b, SLIDE, g)
                turn_heads(FM, b, SLIDE, G - 1)
                turn_attn(FM, b, SLIDE)
                pe.wait_ge(S["acc_read"], due("acc_read", b, 0))
                for unit in last_units(FM):
                    pe.wait_ge(taken_sem(FM, unit), turn_of(FM, b, unit))
                for t in range(NT):
                    o = acc[:, t * P:(t + 1) * P]
                    for k in range(FC):
                        pe.matmul(o, ha[:, k, t * P:(t + 1) * P], w3T[:, k, :], start=(k == 0), stop=False)
                    pe.matmul(o, attnT[:, 0, t * P:(t + 1) * P], wout[:, 0, :], start=False, stop=False)
                    mm = pe.matmul(o, attnT[:, 1, t * P:(t + 1) * P], wout[:, 1, :], start=False, stop=True)
                mm.then_inc(S["acc_ready"], 1)

            def second_block(b):
                for unit in last_units(FS):
                    pe.wait_ge(taken_sem(FS, unit), turn_of(FS, b, unit))
                pe.wait_ge(S["rows2"], due("rows2", b, 1))
                turn(SM, b, "xnT", lambda t: xn[:, t, :])
                pe.wait_ge(S["rows2"], due("rows2", b, 2))
                turn(SM, b, "hT", lambda t: hrow[:, t, :])
                pe.wait_ge(taken_sem(SM, "hT"), turn_of(SM, b, "hT"))
                project(SM, b, "q", wq1[:, :], hT[:, :])
                project(SM, b, "k", wk1[:, :], hT[:, :])
                project_rows(SM, b, "v", hT, wv1[:, :])
                project_rows(SM, b, "logits", x1T, wgT[:, :], E)
                for e in range(EARLY):
                    expert_in(SM, b, e)
                    if e == 1:
                        pe.wait_ge(S["slots_q"], due("slots_q", b, 2 * PLACED))
                        pe.wait_ge(S["slots_k"], due("slots_k", b, 2 * PLACED))
                    if e:
                        for p in CMAX_OF[2 * e - 2]:
                            causal_max(b, p)
                    expert_out(SM, b, e)
                    if e:
                        for p in CMAX_OF[2 * e - 1]:
                            causal_max(b, p)
                turn_max(SM, b, "causal_max", SS, f"cmax_{H // 2 - 1}")
                pe.wait_ge(S["max_placed"], due("max_placed", b, 2 * PLACED))
                for g in range(G):
                    tri_scores(SS, b, "causal", 2 * g, Q)
                    tri_scores(SS, b, "causal", 2 * g + 1, Q)
                    if g:
                        turn_heads(SM, b, CAUSAL, g - 1)
                    weigh(b, CAUSAL, g)
                turn_heads(SM, b, CAUSAL, G - 1)
                pe.wait_ge(S["gated"], due("gated", b, 1))
                turn(SM, b, "gatesT", lambda t: gates[:, t, :], rows=E)
                turn_attn(SM, b, CAUSAL)
                pe.wait_ge(S["acc_read"], due("acc_read", b, 1))
                for unit in last_units(SM):
                    pe.wait_ge(taken_sem(SM, unit), turn_of(SM, b, unit))
                for t in range(NT):
                    o = acc[:, t * P:(t + 1) * P]
                    pe.matmul(o, gatesT[:, t * P:(t + 1) * P], b2[:, :], start=True, stop=False)
                    mm = pe.matmul(o, attnT[:, 0, t * P:(t + 1) * P], wo1[:, :], start=False, stop=True)
                mm.then_inc(S["acc_ready"], 1)
                for unit in last_units(SS):
                    pe.wait_ge(taken_sem(SS, unit), turn_of(SS, b, unit))

            def late_experts(b):
                for e in range(EARLY, E):
                    expert_in(LM, b, e)
                    expert_out(LM, b, e)
                for unit in last_units(LM):
                    pe.wait_ge(taken_sem(LM, unit), turn_of(LM, b, unit))

            pe.wait_ge(S["weights"], 16 * N_LOADS)
            pe.matmul(acc[:, 0:P], wqfT, wkfT, start=True, stop=True).then_inc(S["setup_pe"], 1)
            pe.wait_ge(S["setup_dve"], 1)
            pe.matmul(acc[:, P:2 * P], wqT, bdm, start=True, stop=True).then_inc(S["setup_pe"], 1)
            pe.wait_ge(S["setup_done"], 1)
            with pe.Fori(0, NB) as b:
                first_block(b)
                second_block(b)
                late_experts(b)

        @block.scalar
        def _(act):
            def evacuate(key, b, unit, to, func, scale=1.0, bias=0.0):
                act.wait_ge(full_sem(key, unit), turn_of(key, b, unit))
                return act.activation(to, bank_of(key, unit)[:, :], func, scale=scale, bias=bias)

            def split_hi(key, b, unit, nth, bias=0.0):
                before = {("q", 1): ("q", 0), ("qm", 1): ("q", 1), ("q", 2): ("qm", 1), ("k", 1): ("k", 0), ("k", 2): ("k", 1)}
                name, times = before[unit, nth]
                act.wait_ge(S[f"sent_{name}"], due(f"sent_{name}", b, SENT * times))
                evacuate(key, b, unit, hi[:, {"q": 0, "k": 1, "qm": 0}[unit], :], ACT.Identity, bias=bias)\
                    .then_inc(S[f"hi_{unit}"], 1)

            def probs_from(key, b, unit, to, func, scale, bias, n=512):
                act.wait_ge(full_sem(key, unit), turn_of(key, b, unit))
                bank = bank_of(key, unit)[:, 0:n]
                if len(to.shape) == 3:
                    bank = bank.rearrange("p (a n) -> p a n", a=2)
                return act.activation(to, bank, func, scale=scale, bias=bias).then_inc(taken_sem(key, unit), 1)

            def pair_slot(b, kind, p):
                nth = H // 2 * kind + p
                act.wait_ge(S["heads_out"], due("heads_out", b, (nth - SLOTS) // 2 + 1))
                return nth % SLOTS

            def tri_probs(key, b, kind, tag, p, func, scale, bias):
                slot = pair_slot(b, kind, p)
                for n, h in enumerate((2 * p, 2 * p + 1)):
                    probs_from(key, b, f"{tag}{h}a", probs[:, slot, PROBS * n:PROBS * n + 512], func, scale, bias)
                    probs_from(key, b, f"{tag}{h}b", probs[:, slot, PROBS * n + 512:PROBS * n + 1024], func, scale, bias)
                probs_from(key, b, f"{tag}_{p}", probs[:, slot, :].rearrange("p (h n) -> p h n", h=2)[:, :, 1024:PROBS], func, scale, bias)

            def slide_probs(b, p):
                slot = pair_slot(b, SLIDE, p)
                for n, h in enumerate((2 * p, 2 * p + 1)):
                    probs_from(FS, b, f"slide{h}a", probs[:, slot, NT * WQ * n:NT * WQ * n + 2 * WQ], ACT.Exp, SCALE, 0.0, 2 * WQ)
                    probs_from(FS, b, f"slide{h}b", probs[:, slot, NT * WQ * n + 2 * WQ:NT * WQ * n + 3 * WQ + P], ACT.Exp, SCALE, 0.0, WQ + P)

            def gelu(key, b, e):
                hidden = (ha, hb)[e % 2]
                for c in range(FC):
                    evacuate(key, b, f"moe{e}_{c}", hidden[:, c, :], ACT.Gelu, bias=b1[:, FC * e + c:FC * e + c + 1])\
                        .then_inc(taken_sem(key, f"moe{e}_{c}"), 1)

            def first_block(b):
                evacuate(FM, b, "hT", hT[:, :], ACT.Identity, scale=norm_w[:, 0:1]).then_inc(taken_sem(FM, "hT"), 1)
                for name in ("q", "k", "qm"):
                    split_hi(FM, b, name, 1)
                for c in range(FC):
                    evacuate(FM, b, f"gate{c}", ha[:, c, :], ACT.Silu, scale=s1[:, c:c + 1]).then_inc(taken_sem(FM, f"gate{c}"), 1)
                for c in range(FC):
                    evacuate(FM, b, f"h1_{c}", hb[:, c, :], ACT.Gelu, scale=sh1[:, c:c + 1]).then_inc(taken_sem(FM, f"h1_{c}"), 1)
                for g in range(G):
                    tri_probs(FS, b, LIN, "lin", 2 * g, ACT.Square, 0.5, 1.0)
                    tri_probs(FS, b, LIN, "lin", 2 * g + 1, ACT.Square, 0.5, 1.0)
                    evacuate(FM, b, f"h2_{g}", ha[:, g, :], ACT.Gelu, scale=sh2[:, g:g + 1]).then_inc(taken_sem(FM, f"h2_{g}"), 1)
                for p in range(H // 2):
                    slide_probs(b, p)

            def second_block(b):
                evacuate(SM, b, "hT", hT[:, :], ACT.Identity, scale=gamma[:, 0:1], bias=beta[:, 0:1]).then_inc(taken_sem(SM, "hT"), 1)
                split_hi(SM, b, "q", 2, bq1[:, 0:1])
                split_hi(SM, b, "k", 2, bk1[:, 0:1])
                act.wait_ge(S["shifted"], due("shifted", b, 1))
                act.activation(ex[:, :, :], lg[:, :, :], ACT.Exp).then_inc(S["exped"], 1)
                for e in range(EARLY):
                    gelu(SM, b, e)
                for p in range(H // 2):
                    tri_probs(SS, b, CAUSAL, "causal", p, ACT.Exp, SCALE, 0.0)

            def late_experts(b):
                for e in range(EARLY, E):
                    gelu(LM, b, e)

            act.wait_ge(S["setup_done"], 1)
            act.wait_ge(S["weights"], 16 * N_LOADS)
            with act.Fori(0, NB) as b:
                first_block(b)
                second_block(b)
                late_experts(b)

        @block.gpsimd
        def _(pool):
            def mask_tri(key, b, kind, tag, p):
                nth = H // 2 * kind + p
                pair = probs[:, nth % SLOTS, :].rearrange("p (h n) -> p h n", h=2)
                pool.wait_ge(taken_sem(key, f"{tag}_{p}"), turn_of(key, b, f"{tag}_{p}"))
                pool.sem_inc(S["unread"], 1)
                for n in range(2):
                    three = pair[:, n, :].rearrange("p (n c) -> p n c", c=256)[:, 0:5:2, 0:P]
                    pool.affine_select(out=three, in_=three, compare_op=ALU.is_ge, fill=0.0, base=0,
                                       pattern=[[0, 3], [1, P]], channel_multiplier=-1)
                last = pair[:, :, TRI_AT[3]:TRI_AT[3] + P]
                pool.affine_select(out=last, in_=last, compare_op=ALU.is_ge, fill=0.0, base=0,
                                   pattern=[[0, 2], [1, P]], channel_multiplier=-1).then_inc(S["probs_ready"], 1)

            def mask_slide(b, p):
                nth = H // 2 * SLIDE + p
                pool.wait_ge(taken_sem(FS, f"slide{2 * p + 1}b"), turn_of(FS, b, f"slide{2 * p + 1}b"))
                pool.sem_inc(S["unread"], 1)
                tiles = probs[:, nth % SLOTS, 0:2 * NT * WQ].rearrange("p (n c) -> p n c", c=WQ)
                near, far = tiles[:, :, 0:P], tiles[:, :, WIN:WQ]
                pool.affine_select(out=near, in_=near, compare_op=ALU.is_ge, fill=0.0, base=0,
                                   pattern=[[0, 2 * NT], [1, P]], channel_multiplier=-1).then_inc(S["slide_near"], 1)
                pool.wait_ge(S["slide_near"], due("slide_near", b, p + 1))
                pool.sem_inc(S["unread"], 1)
                pool.affine_select(out=far, in_=far, compare_op=ALU.is_ge, fill=0.0, base=0,
                                   pattern=[[0, 2 * NT], [-1, P]], channel_multiplier=1).then_inc(S["probs_ready"], 1)

            def power(b, nth):
                pool.wait_ge(S[f"stats{nth}"], due(f"stats{nth}", b, 1))
                pool.tensor_tensor(rs[:, :, :], pw[:, :, :], half_neg[:, :].rearrange("p (a t) -> p a t", a=2), ALU.pow)\
                    .then_inc(S[f"powered{nth}"], 1)

            def norm_first(b):
                power(b, 1)
                pool.wait_ge(S["rows1"], due("rows1", b, 1))
                pool.tensor_tensor(xs[:, :, :], x_in[:, :, :], xn[:, :, :], ALU.add).then_inc(S["xs_ready"], 1)

            def first_block(b):
                for p in range(H // 2):
                    mask_tri(FS, b, LIN, "lin", p)
                for p in range(H // 2):
                    mask_slide(b, p)

            def second_block(b):
                power(b, 2)
                pool.wait_ge(S["acc_read"], due("acc_read", b, 1))
                pool.tensor_tensor(y[:, :, :], x1[:, :, :], bo1[:, :].unsqueeze(1).to_broadcast([P, NT, P]), ALU.add)\
                    .then_inc(S["y_init"], 1)
                for p in range(H // 2):
                    mask_tri(SS, b, CAUSAL, "causal", p)

            pool.wait_ge(S["setup_done"], 1)
            with pool.Fori(0, NB) as b:
                norm_first(b)
                first_block(b)
                second_block(b)

        @block.vector
        def _(dve):
            def lap(name, b, n, ins):
                ins.then_inc(S[name], 1)
                dve.wait_ge(S[name], due(name, b, n))

            def normalize(b, nth, src, eps_inner):
                for t in range(NT):
                    last = dve.bn_stats(bn[:, t, :], src[:, t, :])
                lap(f"norm{nth}_laps", b, 1, last)
                dve.sem_inc(S["unread"], 1)
                for t in range(NT):
                    last = dve.bn_aggr(mv[:, t, :], bn[:, t, :])
                lap(f"norm{nth}_laps", b, 2, last)
                dve.tensor_scalar(pw[:, 0, :], mv[:, :, 1], EPS_LN, None, ALU.add)
                dve.tensor_scalar(pw[:, 1, :], mv[:, :, 1], 1.0 + eps_inner, eps_inner * EPS_LN, ALU.mult, ALU.add)\
                    .then_inc(S[f"stats{nth}"], 1)
                dve.wait_ge(S[f"powered{nth}"], due(f"powered{nth}", b, 1))
                for n, to in ((0, xn), (1, hrow)):
                    for t in range(NT):
                        last = dve.tensor_scalar(to[:, t, :], src[:, t, :], mv[:, t, 0:1], rs[:, n, t:t + 1], ALU.subtract, ALU.mult)
                    last.then_inc(S[f"rows{nth}"], 1)

            def take(key, b, unit, to, view=lambda x: x[:, :]):
                dve.wait_ge(full_sem(key, unit), turn_of(key, b, unit))
                dve.tensor_copy(to, view(bank_of(key, unit))).then_inc(taken_sem(key, unit), 1)

            def split_lo(key, b, unit, nth, bias):
                src = {"q": 0, "k": 1, "qm": 0}[unit]
                dve.wait_ge(S[f"hi_{unit}"], due(f"hi_{unit}", b, nth))
                if bias is None:
                    ins = dve.tensor_tensor(lo[:, src, :], bank_of(key, unit)[:, :], hi[:, src, :].bitcast(F32), ALU.subtract)
                else:
                    ins = dve.scalar_tensor_tensor(out=lo[:, src, :], in0=bank_of(key, unit)[:, :], scalar=bias,
                                                   in1=hi[:, src, :].bitcast(F32), op0=ALU.add, op1=ALU.subtract)
                ins.then_inc(taken_sem(key, unit), 1)

            def v_heads(bank):
                return bank[:, :].rearrange("p (n d) -> p n d", d=D)

            V_to = V[:, :, :, 0:D].rearrange("p t h d -> p (t h) d")

            def mx_at(h, j):
                at = (h % HG) * G * NT + (h // HG) * NT + j
                return mx[:, at:at + 1]

            def row_max(key, b, unit, heads_and_tiles):
                dve.wait_ge(full_sem(key, unit), turn_of(key, b, unit))
                for h, j, at, n in heads_and_tiles:
                    last = dve.tensor_reduce(mx_at(h, j), bank_of(key, unit)[:, at:at + n], AX_X, ALU.max)
                last.then_inc(taken_sem(key, unit), 1)
                return last

            def causal_max(b, p):
                for h in (2 * p, 2 * p + 1):
                    row_max(SS, b, f"cmax{h}a", [(h, 3, 0, 512)])
                    row_max(SS, b, f"cmax{h}b", [(h, 2, 0, 384), (h, 0, 384, 128)])
                row_max(SS, b, f"cmax_{p}", [(2 * p, 1, 0, 256), (2 * p + 1, 1, 256, 256)])

            def negate_max(key, b, unit):
                dve.wait_ge(full_sem(key, unit), turn_of(key, b, unit))
                dve.tensor_scalar(mrow[:, :], bank_of(key, unit)[0:H * NT, 0:P], -1.0, None, ALU.mult).then_inc(taken_sem(key, unit), 1)

            def copy_heads(b, kind, g):
                nth = G * kind + g
                dve.wait_ge(S["heads_out"], due("heads_out", b, nth + 1))
                dve.tensor_copy(ot[:, nth % 2, :], heads[nth % 2][:, :]).then_inc(S["heads_copied"], 1)

            def divide_rows(key, b, kind, g, chain, done):
                unit = f"rows{kind}_{g}"
                dve.wait_ge(full_sem(key, unit), turn_of(key, b, unit))
                bank = bank_of(key, unit)[:, :].rearrange("p (t i r) -> p t i r", t=NT, r=ROWS)
                if kind == LIN:
                    lap(chain, b, done + 1, dve.tensor_scalar(den[:, :, :], bank[:, :, :, D], EPS_LIN, None, ALU.add))
                    done += 1
                    lap(chain, b, done + 1, dve.reciprocal(rden[:, :, :], den[:, :, :]))
                else:
                    lap(chain, b, done + 1, dve.reciprocal(rden[:, :, :], bank[:, :, :, D]))
                to = attn[:, :, HG * D * g:HG * D * (g + 1)].rearrange("p t (i d) -> p t i d", d=D)
                dve.tensor_tensor(to, bank[:, :, :, 0:D], rden[:, :, :].unsqueeze(3).to_broadcast([P, NT, HG, D]), ALU.mult)\
                    .then_inc(taken_sem(key, unit), 1)
                return done + 1

            def first_block(b):
                take(FM, b, "xnT", xnT[:, :])
                split_lo(FM, b, "q", 1, None)
                split_lo(FM, b, "k", 1, None)
                take(FM, b, "v", V_to, v_heads)
                split_lo(FM, b, "qm", 1, None)
                for c in range(FC):
                    dve.wait_ge(taken_sem(FM, f"gate{c}"), turn_of(FM, b, f"gate{c}"))
                    dve.wait_ge(full_sem(FM, f"up{c}"), turn_of(FM, b, f"up{c}"))
                    dve.scalar_tensor_tensor(out=ha[:, c, :], in0=bank_of(FM, f"up{c}")[:, :], scalar=s2[:, c:c + 1],
                                             in1=ha[:, c, :], op0=ALU.mult, op1=ALU.mult).then_inc(taken_sem(FM, f"up{c}"), 1)
                for h in range(H):
                    row_max(FS, b, f"smax{h}a", [(h, 0, 0, P), (h, 1, WQ, WQ)])
                    row_max(FS, b, f"smax{h}b", [(h, 2, 0, WQ), (h, 3, WQ, WQ)])
                negate_max(FM, b, "slide_max")
                done = 0
                for g in range(G):
                    if g:
                        done = divide_rows(FM, b, LIN, g - 1, "first_laps", done)
                    copy_heads(b, LIN, g)
                done = divide_rows(FM, b, LIN, G - 1, "first_laps", done)
                take(FM, b, f"cols{LIN}", attnT[:, 0, :])
                for g in range(G):
                    if g:
                        done = divide_rows(FM, b, SLIDE, g - 1, "first_laps", done)
                    copy_heads(b, SLIDE, g)
                done = divide_rows(FM, b, SLIDE, G - 1, "first_laps", done)
                take(FM, b, f"cols{SLIDE}", attnT[:, 1, :])
                assert done == counts["first_laps"][0]

            def choose_experts(b):
                def lapped(ins):
                    nonlocal laps
                    laps += 1
                    lap("second_laps", b, laps, ins)
                laps = 0
                dve.wait_ge(full_sem(SM, "logits"), turn_of(SM, b, "logits"))
                dve.tensor_copy(lg[:, :, :], bank_of(SM, "logits")[:, 0:NT * E].rearrange("p (t e) -> p t e", e=E)).then_inc(taken_sem(SM, "logits"), 1)
                dve.wait_ge(taken_sem(SM, "logits"), turn_of(SM, b, "logits"))
                lapped(dve.tensor_reduce(m1[:, :], lg[:, :, :], AX_X, ALU.max))
                dve.tensor_tensor(lgs[:, :, :], lg[:, :, :], m1[:, :].unsqueeze(2).to_broadcast([P, NT, E]), ALU.subtract).then_inc(S["shifted"], 1)
                other, own = lg[:, :, :].unsqueeze(2).to_broadcast([P, NT, E, E]), lg[:, :, :].unsqueeze(3).to_broadcast([P, NT, E, E])
                above4, equal4 = (x[:, :, :].rearrange("p t (e j) -> p t e j", j=E) for x in (above, equal))
                dve.tensor_tensor(above4, other, own, ALU.is_gt)
                lapped(dve.tensor_tensor(equal4, other, own, ALU.is_equal))
                lapped(dve.tensor_tensor(equal[:, :, :], equal[:, :, :], earlier[:, :].unsqueeze(1).to_broadcast([P, NT, E * E]), ALU.mult))
                lapped(dve.tensor_tensor(above[:, :, :], above[:, :, :], equal[:, :, :], ALU.add))
                lapped(dve.tensor_reduce(rank[:, :, :], above4, AX_X, ALU.add))
                dve.wait_ge(S["exped"], due("exped", b, 1))
                lapped(dve.scalar_tensor_tensor(out=exs[:, :, :], in0=rank[:, :, :], scalar=1.5, in1=ex[:, :, :], op0=ALU.is_lt, op1=ALU.mult))
                lapped(dve.tensor_reduce(gsum[:, :], exs[:, :, :], AX_X, ALU.add))
                lapped(dve.reciprocal(rsum[:, :], gsum[:, :]))
                dve.tensor_tensor(gates[:, :, :], exs[:, :, :], rsum[:, :].unsqueeze(2).to_broadcast([P, NT, E]), ALU.mult).then_inc(S["gated"], 1)
                dve.wait_ge(S["gated"], due("gated", b, 1))
                return laps

            def combine(key, b, e, to):
                dve.wait_ge(full_sem(key, f"moe{e}_out"), turn_of(key, b, f"moe{e}_out"))
                for t in range(NT):
                    last = dve.scalar_tensor_tensor(out=to[:, t, :], in0=bank_of(key, f"moe{e}_out")[:, t * P:(t + 1) * P], scalar=gates[:, t, e:e + 1],
                                                    in1=y[:, t, :], op0=ALU.mult, op1=ALU.add)
                last.then_inc(taken_sem(key, f"moe{e}_out"), 1)
                dve.wait_ge(taken_sem(key, f"moe{e}_out"), turn_of(key, b, f"moe{e}_out"))

            def second_block(b):
                dve.wait_ge(S["acc_ready"], due("acc_ready", b, 1))
                dve.wait_ge(S["xs_ready"], due("xs_ready", b, 1))
                dve.tensor_tensor(x1[:, :, :], acc[:, :].rearrange("p (t n) -> p t n", n=P), xs[:, :, :], ALU.add).then_inc(S["acc_read"], 1)
                dve.wait_ge(S["acc_read"], due("acc_read", b, 1))
                normalize(b, 2, x1, EPS_LN)
                take(SM, b, "xnT", x1T[:, :])
                split_lo(SM, b, "q", 2, bq1[:, 0:1])
                split_lo(SM, b, "k", 2, bk1[:, 0:1])
                dve.wait_ge(full_sem(SM, "v"), turn_of(SM, b, "v"))
                dve.tensor_tensor(V[:, :, :, 0:D], bank_of(SM, "v")[:, :].rearrange("p (t h d) -> p t h d", t=NT, d=D),
                                  bv1[:, :].rearrange("p (h d) -> p h d", d=D).unsqueeze(1).to_broadcast([P, NT, H, D]), ALU.add)\
                    .then_inc(taken_sem(SM, "v"), 1)
                done = choose_experts(b)
                dve.wait_ge(S["y_init"], due("y_init", b, 1))
                combine(SM, b, 0, y)
                for e in range(1, EARLY):
                    for p in CMAX_OF[2 * e - 2]:
                        causal_max(b, p)
                    combine(SM, b, e, y)
                    for p in CMAX_OF[2 * e - 1]:
                        causal_max(b, p)
                negate_max(SM, b, "causal_max")
                for g in range(G):
                    if g:
                        done = divide_rows(SM, b, CAUSAL, g - 1, "second_laps", done)
                    copy_heads(b, CAUSAL, g)
                done = divide_rows(SM, b, CAUSAL, G - 1, "second_laps", done)
                assert done == counts["second_laps"][0]
                take(SM, b, "gatesT", gatesT[:, :], lambda x: x[0:E, :])
                take(SM, b, f"cols{CAUSAL}", attnT[:, 0, :])
                dve.wait_ge(S["acc_ready"], due("acc_ready", b, 2))
                dve.tensor_tensor(y[:, :, :], acc[:, :].rearrange("p (t n) -> p t n", n=P), y[:, :, :], ALU.add).then_inc(S["acc_read"], 1)
                dve.wait_ge(S["acc_read"], due("acc_read", b, 2))

            def late_experts(b):
                dve.wait_ge(S["stored"], due("stored", b, 0))
                for e in range(EARLY, E):
                    combine(LM, b, e, result if e == E - 1 else y)

            dve.memset(half_neg[:, :], -0.5)
            dve.memset(mx[:, :], 0.0)
            dve.memset(probs[:, :, :], 0.0)
            dve.memset(K[:, :, :].bitcast(F32), 0.0)
            dve.memset(V[:, :, :, D + 1:ROWS], 0.0)
            dve.memset(V[:, :, :, D:D + 1], 1.0)
            dve.wait_ge(S["weights"], 16 * N_LOADS)
            dve.tensor_copy(identb[:, :], ident[:, :])
            dve.tensor_copy(causal_neg[:, :], causal_f)
            dve.tensor_copy(slide_neg[:, :], slide_f)
            dve.tensor_tensor(w3T[:, :, :], w3T[:, :, :], s3.unsqueeze(1).to_broadcast([P, FC, P]), ALU.mult)
            dve.wait_ge(S["setup_pe"], 1)
            dve.tensor_tensor(bdm, acc[:, 0:P], blocks, ALU.mult).then_inc(S["setup_dve"], 1)
            dve.wait_ge(S["setup_pe"], 2)
            for name, (_, first) in counts.items():
                if first:
                    dve.sem_inc(S[name], first)
            dve.tensor_copy(wqm[:, :], acc[:, P:2 * P]).then_inc(S["setup_done"], 1)
            with dve.Fori(0, NB) as b:
                dve.wait_ge(S["x_loaded"], due("x_loaded", b, 16))
                normalize(b, 1, x_in, EPS_RMS)
                first_block(b)
                second_block(b)
                late_experts(b)


def lay_out(i):
    import numpy as np

    def c(a):
        return np.ascontiguousarray(np.asarray(a, np.float32))

    def chunks(a):
        return c(np.reshape(a, (-1, P)).T)

    q, k = np.arange(P)[:, None], np.arange(P)[None, :]
    w = np.arange(WQ)[None, :]
    e = np.arange(E)
    ones = np.zeros((H, D, T), np.float32)
    ones[:, 0] = 1.0
    return {
        "x": c(i["L0_attn_x"]), "wq": c(i["L0_attn_Wq"]), "wqT": c(np.transpose(i["L0_attn_Wq"])), "wk": c(i["L0_attn_Wk"]),
        "wv": c(i["L0_attn_Wv"]), "wqfT": c(np.tile(np.transpose(i["L0_attn_Wqf"]), (1, H))),
        "wkfT": c(np.tile(np.transpose(i["L0_attn_Wkf"]), (1, H))), "wout": c(np.reshape(i["L0_attn_Wout"], (2, P, P))),
        "norm_w": c(np.reshape(i["L0_attn_norm_w"], (P, 1))),
        "w1T": c(np.transpose(i["L0_ffn_w1_w"])), "w2T": c(np.transpose(i["L0_ffn_w2_w"])), "h1T": c(np.transpose(i["L0_ffn_h1_w"])),
        "h2T": c(np.transpose(i["L0_ffn_h2_w"])), "w3T": c(np.transpose(i["L0_ffn_w3_w"])),
        "s1": chunks(i["L0_ffn_w1_s"]), "s2": chunks(i["L0_ffn_w2_s"]), "sh1": chunks(i["L0_ffn_h1_s"]), "sh2": chunks(i["L0_ffn_h2_s"]),
        "s3": c(i["L0_ffn_w3_s"]),
        "wq1": c(i["L1_attn_Wq"]), "wk1": c(i["L1_attn_Wk"]), "wv1": c(i["L1_attn_Wv"]), "wo1": c(i["L1_attn_Wo"]),
        "bq1": c(np.reshape(i["L1_attn_bq"], (P, 1))), "bk1": c(np.reshape(i["L1_attn_bk"], (P, 1))), "bv1": c(i["L1_attn_bv"]),
        "bo1": c(i["L1_attn_bo"]), "gamma": c(np.reshape(i["L1_attn_ln_gamma"], (P, 1))), "beta": c(np.reshape(i["L1_attn_ln_beta"], (P, 1))),
        "wgT": c(np.transpose(i["L1_ffn_Wg"])), "W1": c(i["L1_ffn_W1"]), "b1": chunks(i["L1_ffn_b1"]), "W2": c(i["L1_ffn_W2"]), "b2": c(i["L1_ffn_b2"]),
        "ident": np.eye(P, dtype=np.float32), "causal_neg": np.where(k <= q, 0.0, NEG).astype(np.float32),
        "slide_neg": np.where((w - WIN <= q) & (w >= q), 0.0, NEG).astype(np.float32),
        "earlier": c(np.broadcast_to((e[None, :] < e[:, None]).reshape(1, -1), (P, E * E))),
        "blocks": (q // D == k // D).astype(np.float32), "slot_q": np.zeros((H, D, T), np.float32), "slot_k": ones,
    }


def kernel(**inputs):
    import concourse.bacc as bacc
    from concourse.bass_utils import run_bass_kernel_spmd as run

    nc = bacc.Bacc("TRN2", target_bir_lowering=False, num_devices=1)
    arrays = lay_out(inputs)
    dram = {name: nc.dram_tensor(f"in_{name}", shape, F32, kind="ExternalInput").ap() for name, shape in SHAPES.items()}
    out = nc.dram_tensor("out", (NB, T, P), F32, kind="ExternalOutput").ap()
    build(nc, dram, out)
    r = run(nc, [{f"in_{name}": a for name, a in arrays.items()}], core_ids=[0])
    return r.results[0]["out"]
```

```python
from contextlib import ExitStack
import math

import concourse.bass as bass
from concourse import mybir

F32 = mybir.dt.float32
F32R = mybir.dt.float32r
BF16 = mybir.dt.bfloat16
ALU = mybir.AluOpType
ACT = mybir.ActivationFunctionType
AX_X = mybir.AxisListType.X

P = 128
NB, T = 8, 512
NT = T // P
H, D = 16, 8
G, HG = 4, 4
ROWS = 32
FC = 4
E = 8
WIN = 64
WQ = P + WIN
LIN, SLIDE, CAUSAL = range(3)
NEG = -1e30
EPS_LN, EPS_RMS, EPS_LIN = 1e-5, 1e-6, 1e-6
SCALE = float(D) ** -0.5

TRI_AT = {0: 0, 1: 512, 3: 896, 2: 1024}
TRI_N = {j: T - P * j for j in range(NT)}
PROBS = 1280
SLIDE_AT = {j: WQ * j for j in range(NT)}
SLIDE_N = {j: min(WQ, T - P * j) for j in range(NT)}

EARLY = 4
SENT, PLACED = 3 * 16, HG * 16
N_LOADS = 38
SLOTS = 3

OUT_BESIDE = {1: 4, 2: 5}
OUT3_BESIDE = 0
CMAX_STEPS = 16
IN_BEHIND = {0: 4, 1: 5, 3: 6}

def banks_of(ring):
    return 3 if ring == "score" else 2


def tri_units(tag):
    return [f"{tag}{u}" for p in range(H // 2) for u in (f"{2 * p}a", f"{2 * p}b", f"{2 * p + 1}a", f"{2 * p + 1}b", f"_{p}")]


def slide_units(tag):
    return [f"{tag}{h}{u}" for h in range(H) for u in "ab"]


def expert_in_units(e):
    return [f"moe{e}_{c}" for c in range(FC)]


def expert_units(e):
    return expert_in_units(e) + [f"moe{e}_out"]


def misc_units(after_another):
    def late(units):
        return units if after_another else []
    units = ["hT1", "xnT1", "q1", "k1", "v1"] + late([f"rows{CAUSAL}_{G - 1}"]) + ["qm1", "gate0"] + late([f"cols{CAUSAL}"]) + ["up0"]
    units += [f"{w}{c}" for c in range(1, FC) for w in ("gate", "up")] + [f"h1_{c}" for c in range(FC)] + ["slide_max"]
    for g in range(G):
        units += [f"h2_{g}"] + ([f"rows{LIN}_{g - 1}"] if g else [])
    for g in range(G):
        units += late([f"moe{OUT_BESIDE[g]}_out"] if g in OUT_BESIDE else [])
        units += [f"rows{SLIDE}_{g - 1}" if g else f"rows{LIN}_{G - 1}"]
        units += late(expert_in_units(IN_BEHIND[g]) if g in IN_BEHIND else []) + ([] if g else [f"cols{LIN}"])
    units += late(["moe6_out"]) + [f"rows{SLIDE}_{G - 1}"] + late(["moe7_0", "moe7_1"]) + [f"cols{SLIDE}"]
    units += late(["moe7_2", "moe7_3", "moe7_out"])
    units += ["hT2", "xnT2", "q2", "k2", "v2", "logits"] + [u for e in range(EARLY - 1) for u in expert_units(e)]
    return units + ["causal_max", "gatesT"] + expert_units(EARLY - 1) + [f"rows{CAUSAL}_{g}" for g in range(G - 1)]


UNITS = {
    "score": slide_units("smax") + tri_units("lin") + slide_units("slide") + tri_units("cmax") + tri_units("causal"),
    "opening": misc_units(False), "steady": misc_units(True),
    "closing": expert_units(4) + [f"rows{CAUSAL}_{G - 1}"] + expert_in_units(5) + [f"cols{CAUSAL}", "moe5_out"]
    + expert_units(6) + expert_units(7),
}
PLACE = {ring: {u: (n % banks_of(ring), n // banks_of(ring)) for n, u in enumerate(units)} for ring, units in UNITS.items()}


def cmax_units(n):
    each = 5 * H // 2
    return each * n // CMAX_STEPS, each * (n + 1) // CMAX_STEPS


def units_in(ring, bank):
    return len(range(bank, len(UNITS[ring]), banks_of(ring)))


SHAPES = {
    "x": (NB, T, P), "wq": (P, P), "wqT": (P, P), "wk": (P, P), "wv": (P, P), "wqfT": (16, P), "wkfT": (16, P),
    "wout": (2, P, P), "norm_w": (P, 1),
    "w1T": (P, T), "w2T": (P, T), "h1T": (T, T), "h2T": (T, T), "w3T": (T, P),
    "s1": (P, FC), "s2": (P, FC), "sh1": (P, FC), "sh2": (P, FC), "s3": (P,),
    "wq1": (P, P), "wk1": (P, P), "wv1": (P, P), "wo1": (P, P), "bq1": (P, 1), "bk1": (P, 1), "bv1": (P,), "bo1": (P,),
    "gamma": (P, 1), "beta": (P, 1), "wgT": (P, E),
    "W1": (E, P, T), "b1": (P, E * FC), "W2": (E, T, P), "b2": (E, P),
    "ident": (P, P), "causal_neg": (P, P), "slide_neg": (P, WQ), "earlier": (P, E * E), "blocks": (P, P),
    "slot_q": (H, D, T), "slot_k": (H, D, T),
}


def build(nc, dram, out):
    with ExitStack() as ctx:
        def sb(name, shape, dt=F32):
            return ctx.enter_context(nc.sbuf_tensor(name, shape, dt))

        def pb(name, shape=(P, 512)):
            return ctx.enter_context(nc.psum_tensor(name, list(shape), F32))

        wq, wk, wv, wqm = (sb(n, [P, P]) for n in ("wq_s", "wk_s", "wv_s", "wqm_s"))
        wout = sb("wout_s", [P, 2, P])
        norm_w, gamma, beta, bq1, bk1 = (sb(n + "_s", [P, 1]) for n in ("norm_w", "gamma", "beta", "bq1", "bk1"))
        w1T, w2T = sb("w1T_s", [P, T]), sb("w2T_s", [P, T])
        h1T, h2T, w3T = sb("h1T_s", [P, FC, T]), sb("h2T_s", [P, FC, T]), sb("w3T_s", [P, FC, P])
        s1, s2, sh1, sh2 = (sb(n + "_s", [P, FC]) for n in ("s1", "s2", "sh1", "sh2"))
        bv1, bo1 = (sb(n + "_s", [P, P]) for n in ("bv1", "bo1"))
        wq1, wk1, wv1, wo1 = (sb(n + "_s", [P, P]) for n in ("wq1", "wk1", "wv1", "wo1"))
        wgT = sb("wgT_s", [P, E])
        W1, W2 = sb("W1_s", [P, E, T]), sb("W2_s", [P, E, FC, P])
        b1, b2 = sb("b1_s", [P, E * FC]), sb("b2_s", [E, P])
        ident, identb = sb("ident_s", [P, P]), sb("identb", [P, P], BF16)
        causal_neg, slide_neg = sb("causal_neg_s", [P, P], BF16), sb("slide_neg_s", [P, WQ], BF16)
        earlier = sb("earlier_s", [P, E * E])
        half_neg, euler = sb("half_neg", [P, NT]), sb("euler", [P, NT, E])

        x_in, xs, xn, hrow = (sb(n, [P, NT, P]) for n in ("x_in", "xs", "xn", "hrow"))
        xnT, hT = sb("xnT_s", [P, T]), sb("hT_s", [P, T])
        bn, mv, pw, rs = sb("bn", [P, NT, 6]), sb("mv", [P, NT, 2]), sb("pw", [P, 2, NT]), sb("rs", [P, 2, NT])
        hi, lo = sb("hi", [P, 2, T], F32R), sb("lo", [P, 2, T], F32R)
        Q, QM, K = sb("Q", [P, G, T], F32R), sb("QM", [P, G, T], F32R), sb("K", [P, H, T], F32R)
        V = sb("V", [P, NT, H, ROWS])
        probs = sb("probs", [P, SLOTS, 2 * PROBS])
        shared = sb("shared", [P, 2 * PROBS + FC * T])
        mx, mrow = sb("mx", [P, P]), sb("mrow", [HG * G * NT, P], F32R)
        ot = sb("ot", [P, 2, T])
        den, rden = sb("den", [P, NT, HG]), sb("rden", [P, NT, HG])
        attn = sb("attn", [P, NT, P])
        attnT = sb("attnT", [P, 2, T])
        ha, hb = (shared[:, at:at + FC * T].rearrange("p (c t) -> p c t", t=T) for at in (2 * PROBS - FC * T, 2 * PROBS))
        x1, y = sb("x1", [P, NT, P]), sb("y", [P, NT, P])
        lg, lgs, ex, exs, gates, rank = (sb(n, [P, NT, E]) for n in ("lg", "lgs", "ex", "exs", "gates", "rank"))
        above, equal = (hrow[:, n:n + 2, :].rearrange("p a (b e) -> p (a b) e", e=E * E) for n in (0, 2))
        m1, gsum, rsum = (sb(n, [P, NT]) for n in ("m1", "gsum", "rsum"))
        gatesT = sb("gatesT_s", [E, T])
        x1T = sb("x1T", [P, T])
        wqT, blocks, bdm, s3, causal_f = (ha[:, n // 4, P * (n % 4):P * (n % 4 + 1)] for n in range(5))
        slide_f = ha[:, 2, 0:WQ]
        wqfT, wkfT = (hb[0:16, 0, P * n:P * (n + 1)] for n in range(2))

        score = [pb(f"score{i}") for i in range(banks_of("score"))]
        misc = [pb(f"misc{i}") for i in range(banks_of("steady"))]
        heads = [pb(f"heads{i}") for i in range(2)]
        acc = pb("acc")

        scratch = {n: nc.dram_tensor(f"slots_of_{n}", (H, ROWS, T), F32, kind="Internal").ap() for n in ("q", "k", "qm")}

        counts = {
            "unread": (0, 0), "weights": (0, 0), "slots_set": (0, 0), "keys_cleared": (0, 0), "setup_pe": (0, 0), "setup_dve": (0, 0), "setup_done": (0, 0),
            "x_loaded": (16, 0), "stored": (16, 16), "xs_ready": (1, 0), "y_init": (1, 0),
            "stats1": (1, 0), "stats2": (1, 0), "powered1": (2, 0), "powered2": (2, 0), "xn1": (1, 0), "xn2": (1, 0), "hrow1": (1, 0), "hrow2": (1, 0),
            "norm1_laps": (2, 0), "norm2_laps": (2, 0), "divide_laps": (4 * G, 0), "choice_laps": (8, 0),
            "hi_q": (2, 0), "hi_k": (2, 0), "hi_qm": (1, 0),
            "sent_q": (2 * SENT, 16), "sent_k": (2 * SENT, 16), "sent_qm": (SENT, 16),
            "slots_q": (2 * 16, 0), "slots_k": (2 * PLACED, 0), "slots_qm": (16, 0), "max_placed": (2 * PLACED, 0),
            "slide_near": (H // 2, 0), "probs_ready": (3 * H // 2, 0),
            "heads_out": (3 * G, 2), "heads_copied": (3 * G, 2),
            "acc_ready": (3, 0), "acc_read": (3, 1), "shifted": (1, 0), "exped": (1, 0), "gated": (1, 0),
        }
        for ring in UNITS:
            for bank in range(banks_of(ring)):
                counts[f"{ring}_full{bank}"] = (units_in(ring, bank), 0)
                counts[f"{ring}_taken{bank}"] = (units_in(ring, bank), 1)
        def slot_of(kind, p):
            if kind == CAUSAL:
                return shared[:, 0:2 * PROBS] if p % (SLOTS + 1) == SLOTS else probs[:, p % (SLOTS + 1), :]
            return probs[:, (H // 2 * kind + p) % SLOTS, :]

        S = {name: ctx.enter_context(nc.semaphore(name)) for name in counts}

        def due(name, sequence, count):
            (b, ahead), (per_sequence, setup) = sequence, counts[name]
            return b * per_sequence + (ahead * per_sequence + setup + count)

        def ring_count(ring, bank, n):
            (name, b), per_body = ring, units_in(ring[0], bank)
            if name == "score":
                return b * per_body + n
            return b * per_body + (n - per_body) if name == "steady" else n

        def full_sem(ring, unit):
            return S[f"{ring[0]}_full{PLACE[ring[0]][unit][0]}"]

        def taken_sem(ring, unit):
            return S[f"{ring[0]}_taken{PLACE[ring[0]][unit][0]}"]

        def full_at(ring, unit):
            bank, n = PLACE[ring[0]][unit]
            return ring_count(ring, bank, n + 1)

        def taken_at(ring, unit):
            bank, n = PLACE[ring[0]][unit]
            return ring_count(ring, bank, n + 2)

        def free_at(ring, unit):
            bank, n = PLACE[ring[0]][unit]
            return ring_count(ring, bank, n + 1)

        def last_units(ring):
            return UNITS[ring[0]][-banks_of(ring[0]):]

        def bank_of(ring, unit):
            return (score if ring[0] == "score" else misc)[PLACE[ring[0]][unit][0]]

        block = ctx.enter_context(nc.Block())
        x_v = dram["x"].rearrange("b (t p) d -> b p t d", p=P)
        out_v = out.rearrange("b (t p) d -> b p t d", p=P)

        @block.sync
        def _(sp):
            loads = [(wqfT, dram["wqfT"]), (wkfT, dram["wkfT"]), (wqT, dram["wqT"]), (blocks, dram["blocks"]),
                     (wk[:, :], dram["wk"]), (wq[:, :], dram["wq"]), (wv[:, :], dram["wv"]), (ident[:, :], dram["ident"]),
                     (wout[:, :, :], dram["wout"].rearrange("a p n -> p a n")), (norm_w[:, :], dram["norm_w"]),
                     (w1T[:, :], dram["w1T"]), (w2T[:, :], dram["w2T"]),
                     (h1T[:, :, :], dram["h1T"].rearrange("(c p) n -> p c n", p=P)), (h2T[:, :, :], dram["h2T"].rearrange("(c p) n -> p c n", p=P)),
                     (w3T[:, :, :], dram["w3T"].rearrange("(c p) n -> p c n", p=P)),
                     (s1[:, :], dram["s1"]), (s2[:, :], dram["s2"]), (sh1[:, :], dram["sh1"]), (sh2[:, :], dram["sh2"]),
                     (s3, dram["s3"].partition_broadcast(P)), (bv1[:, :], dram["bv1"].partition_broadcast(P)),
                     (bo1[:, :], dram["bo1"].partition_broadcast(P)),
                     (wq1[:, :], dram["wq1"]), (wk1[:, :], dram["wk1"]), (wv1[:, :], dram["wv1"]), (wo1[:, :], dram["wo1"]),
                     (bq1[:, :], dram["bq1"]), (bk1[:, :], dram["bk1"]), (gamma[:, :], dram["gamma"]), (beta[:, :], dram["beta"]),
                     (wgT[:, :], dram["wgT"]), (W1[:, :, :], dram["W1"].rearrange("e p n -> p e n")),
                     (W2[:, :, :, :].rearrange("p e c n -> p (e c) n"), dram["W2"].rearrange("e (c p) n -> p (e c) n", p=P)),
                     (b1[:, :], dram["b1"]), (b2[:, :], dram["b2"]), (causal_f, dram["causal_neg"]), (slide_f, dram["slide_neg"]),
                     (earlier[:, :], dram["earlier"]), (x_in[:, :, :], x_v[0])]
            for dst, src in loads[:-1]:
                sp.dma_start(dst, src).then_inc(S["weights"], 16)
            sp.dma_start(*loads[-1]).then_inc(S["x_loaded"], 16)
            assert len(loads) - 1 == N_LOADS
            for n, name in enumerate(("q", "k", "qm")):
                sp.dma_start(scratch[name][:, 3 * D:4 * D, :], dram["slot_k" if name == "k" else "slot_q"]).then_inc(S["slots_set"], 16)
            sp.wait_ge(S["slots_set"], 16 * len(scratch))
            sp.wait_ge(S["keys_cleared"], 1)
            for i in range(HG):
                row = ROWS * i + 3 * D
                sp.dma_start(K[row:row + D, i:H:HG, :].bitcast(F32), scratch["k"].rearrange("(g i) r t -> i r g t", i=HG)[i][3 * D:4 * D])\
                    .then_inc(S["slots_set"], 16)
            sp.wait_ge(S["slots_set"], 16 * (len(scratch) + HG))

            def send(name, part, slots):
                src = {"q": 0, "k": 1, "qm": 0}[name]
                view = scratch[name].rearrange("h (s d) t -> s h d t", d=D)
                for s in slots:
                    sp.dma_start(view[s], part[:, src, :].bitcast(F32)).then_inc(S[f"sent_{name}"], 16)

            def fetch(name):
                if name == "k":
                    groups = scratch[name].rearrange("(g i) r t -> i r g t", i=HG)
                    for i in range(HG):
                        sp.dma_start(K[ROWS * i:ROWS * i + 3 * D, i:H:HG, :].bitcast(F32), groups[i][0:3 * D]).then_inc(S["slots_k"], 16)
                else:
                    to = Q if name == "q" else QM
                    sp.dma_start(to[:, :, :].bitcast(F32), scratch[name].rearrange("(g i) r t -> (i r) g t", i=HG)).then_inc(S[f"slots_{name}"], 16)

            def place_max(ring, unit):
                sp.wait_ge(taken_sem(ring, unit), taken_at(ring, unit))
                for i in range(HG):
                    row = ROWS * i + 3 * D
                    sp.dma_start(Q[row:row + 1, :, :].rearrange("p g (n t) -> p (g n) t", t=P).bitcast(F32),
                                 mrow[G * NT * i:G * NT * (i + 1), :].bitcast(F32)).then_inc(S["max_placed"], 16)

            def split_and_spread(ring, now, names, nth, groups_done):
                for name in names:
                    unit = f"{name}{nth}"
                    sp.wait_ge(S[f"hi_{name}"], due(f"hi_{name}", now, nth))
                    send(name, hi, (0, 2) if name == "k" else (0, 1))
                    sp.wait_ge(taken_sem(ring, unit), taken_at(ring, unit))
                    send(name, lo, (1,) if name == "k" else (2,))
                sp.wait_ge(S["heads_out"], due("heads_out", now, groups_done))
                sp.sem_inc(S["unread"], 1)
                for name in names:
                    sp.wait_ge(S[f"sent_{name}"], due(f"sent_{name}", now, SENT * nth))
                    fetch(name)

            def store(ring, result_of):
                sp.wait_ge(taken_sem(ring, f"moe{E - 1}_out"), taken_at(ring, f"moe{E - 1}_out"))
                sp.sem_inc(S["unread"], 1)
                sp.dma_start(out_v[result_of], y[:, :, :]).then_inc(S["stored"], 16)

            def body(b, after_another, ring):
                now = (b, 0)
                sp.wait_ge(S["xs_ready"], due("xs_ready", now, 1))
                sp.sem_inc(S["unread"], 1)
                sp.wait_ge(S["xn1"], due("xn1", now, 1))
                sp.sem_inc(S["unread"], 1)
                sp.dma_start(x_in[:, :, :], x_v[(b + 1) & (NB - 1)]).then_inc(S["x_loaded"], 16)
                split_and_spread(ring, now, ("q", "k", "qm"), 1, 0)
                place_max(ring, "slide_max")
                if after_another:
                    store(ring, b - 1)
                split_and_spread(ring, now, ("q", "k"), 2, 2 * G)
                place_max(ring, "causal_max")

            sp.wait_ge(S["setup_done"], 1)
            body(0, False, ("opening", 0))
            with sp.Fori(1, NB) as b:
                body(b, True, ("steady", b))
            store(("closing", NB), NB - 1)
            sp.wait_ge(S["stored"], 16 + 16 * NB)

        @block.tensor
        def _(pe):
            def to_bank(ring, unit):
                pe.wait_ge(taken_sem(ring, unit), free_at(ring, unit))
                return bank_of(ring, unit)

            def turn(ring, unit, tile, rows=P):
                bank = to_bank(ring, unit)
                for t in range(NT):
                    mm = pe.transpose(bank[0:rows, t * P:(t + 1) * P], tile(t), ident[:, :])
                mm.then_inc(full_sem(ring, unit), 1)

            def project(ring, unit, w, x):
                pe.matmul(to_bank(ring, unit)[:, :], w, x, start=True, stop=True).then_inc(full_sem(ring, unit), 1)

            def project_rows(ring, unit, x, w, n=P):
                bank = to_bank(ring, unit)
                for t in range(NT):
                    mm = pe.matmul(bank[:, t * n:(t + 1) * n], x[:, t * P:(t + 1) * P], w, start=True, stop=True)
                mm.then_inc(full_sem(ring, unit), 1)

            def dense(ring, unit, w, src, c, first, last):
                bank = to_bank(ring, unit) if first == 0 else bank_of(ring, unit)
                for k in range(first, last):
                    mm = pe.matmul(bank[:, :], w[:, k, c * P:(c + 1) * P], src[:, k, :], start=(k == 0), stop=(k == FC - 1),
                                   skip_group_check=True)
                if last == FC:
                    mm.then_inc(full_sem(ring, unit), 1)

            def scores_into(b, unit, parts):
                ring = ("score", b)
                bank = to_bank(ring, unit)
                for at, left, right, mask, mask_at in parts:
                    mm = pe.matmul(bank[:, at:at + right.shape[1]], left, right, start=True, stop=mask is None, skip_group_check=True)
                    if mask is not None:
                        at += mask_at
                        mm = pe.matmul(bank[:, at:at + mask.shape[1]], identb[:, :], mask, start=False, stop=True,
                                       skip_group_check=True)
                mm.then_inc(full_sem(ring, unit), 1)

            def q_part(buf, h, a, n):
                return buf[:, h // HG, a:a + n]

            def slide_max(b, first, last):
                for n in range(first, last):
                    h, parts = n // 2, []
                    for j in (2 * (n % 2), 2 * (n % 2) + 1):
                        if j == 0:
                            parts.append((0, q_part(Q, h, 0, P), K[:, h, 0:P], slide_neg[:, WIN:WQ], 0))
                        else:
                            parts.append((WQ * (j % 2), q_part(Q, h, P * j, P), K[:, h, P * j - WIN:P * (j + 1)], slide_neg[:, :], 0))
                    scores_into(b, slide_units("smax")[n], parts)

            def causal_max(b, first, last):
                def part(h, j, at):
                    return (at, q_part(Q, h, P * j, P), K[:, h, 0:P * (j + 1)], causal_neg[:, :], P * j)
                for n in range(first, last):
                    p, u = n // 5, n % 5
                    h = 2 * p + u // 2
                    if u == 4:
                        parts = [part(2 * p, 1, 0), part(2 * p + 1, 1, 256)]
                    else:
                        parts = [part(h, 2, 0), part(h, 0, 384)] if u % 2 else [part(h, 3, 0)]
                    scores_into(b, tri_units("cmax")[n], parts)

            def tri_scores(b, tag, buf, first, last):
                def part(h, j, at):
                    return (at, K[:, h, P * j:P * (j + 1)], q_part(buf, h, P * j, TRI_N[j]), None, 0)
                for n in range(first, last):
                    p, u = n // 5, n % 5
                    h = 2 * p + u // 2
                    if u == 4:
                        parts = [part(2 * p, 2, 0), part(2 * p + 1, 2, 256)]
                    else:
                        parts = [part(h, 1, 0), part(h, 3, 384)] if u % 2 else [part(h, 0, 0)]
                    scores_into(b, tri_units(tag)[n], parts)

            def slide_scores(b, first, last):
                for n in range(first, last):
                    h, parts = n // 2, []
                    for j in (2 * (n % 2), 2 * (n % 2) + 1):
                        parts.append((WQ * (j % 2), K[:, h, P * j:P * (j + 1)], q_part(Q, h, P * j, SLIDE_N[j]), None, 0))
                    scores_into(b, slide_units("slide")[n], parts)

            def weigh(sequence, kind, g, first=0, last=NT):
                nth = G * kind + g
                if first == 0:
                    pe.wait_ge(S["probs_ready"], due("probs_ready", sequence, 2 * nth + 2))
                    pe.wait_ge(S["heads_copied"], due("heads_copied", sequence, nth - 1))
                starts, widths, head = (SLIDE_AT, SLIDE_N, NT * WQ) if kind == SLIDE else (TRI_AT, TRI_N, PROBS)
                for j in range(first, last):
                    for i in range(HG):
                        at = head * (i % 2) + starts[j]
                        mm = pe.matmul(heads[nth % 2][ROWS * i:ROWS * (i + 1), P * j:P * j + widths[j]],
                                       V[:, j, HG * g + i, :], slot_of(kind, 2 * g + i // 2)[:, at:at + widths[j]],
                                       start=(j == 0), stop=(j == NT - 1), skip_group_check=True)
                if last == NT:
                    mm.then_inc(S["heads_out"], 1)

            def turn_heads(ring, sequence, kind, g):
                nth = G * kind + g
                pe.wait_ge(S["heads_copied"], due("heads_copied", sequence, nth + 1))
                turn(ring, f"rows{kind}_{g}", lambda t: ot[:, nth % 2, t * P:(t + 1) * P])

            def turn_attn(ring, kind):
                pe.wait_ge(taken_sem(ring, f"rows{kind}_{G - 1}"), taken_at(ring, f"rows{kind}_{G - 1}"))
                turn(ring, f"cols{kind}", lambda t: attn[:, t, :])

            def turn_max(ring, unit, b, last):
                pe.wait_ge(taken_sem(("score", b), last), taken_at(("score", b), last))
                pe.transpose(to_bank(ring, unit)[:, 0:P], mx[:, :], ident[:, :]).then_inc(full_sem(ring, unit), 1)

            def expert_in(ring, e, first=0, last=FC):
                for c in range(first, last):
                    project(ring, f"moe{e}_{c}", W1[:, e, c * P:(c + 1) * P], x1T[:, :])

            def expert_out(ring, e, first=0, last=NT):
                hidden, unit = (ha, hb)[e % 2], f"moe{e}_out"
                if first == 0:
                    for c in (FC - 2, FC - 1):
                        pe.wait_ge(taken_sem(ring, f"moe{e}_{c}"), taken_at(ring, f"moe{e}_{c}"))
                bank = to_bank(ring, unit) if first == 0 else bank_of(ring, unit)
                for t in range(first, last):
                    for k in range(FC):
                        mm = pe.matmul(bank[:, t * P:(t + 1) * P], hidden[:, k, t * P:(t + 1) * P], W2[:, e, k, :],
                                       start=(k == 0), stop=(k == FC - 1))
                if last == NT:
                    mm.then_inc(full_sem(ring, unit), 1)

            def mix_causal(sequence):
                pe.wait_ge(S["acc_read"], due("acc_read", sequence, 2))
                for t in range(NT):
                    o = acc[:, t * P:(t + 1) * P]
                    pe.matmul(o, gatesT[:, t * P:(t + 1) * P], b2[:, :], start=True, stop=False)
                    mm = pe.matmul(o, attnT[:, 0, t * P:(t + 1) * P], wo1[:, :], start=False, stop=True)
                mm.then_inc(S["acc_ready"], 1)

            def third_layer(ring, now, first, last):
                if first == 0:
                    pe.wait_ge(S["acc_read"], due("acc_read", now, 0))
                    for g in (G - 2, G - 1):
                        pe.wait_ge(taken_sem(ring, f"h2_{g}"), taken_at(ring, f"h2_{g}"))
                for t in range(first, last):
                    for k in range(FC):
                        mm = pe.matmul(acc[:, t * P:(t + 1) * P], ha[:, k, t * P:(t + 1) * P], w3T[:, k, :], start=(k == 0), stop=(k == FC - 1))
                if last == NT:
                    mm.then_inc(S["acc_ready"], 1)

            def first_block(b, after_another, ring):
                now, before = (b, 0), (b, -1)
                pe.wait_ge(S["hrow1"], due("hrow1", now, 1))
                turn(ring, "hT1", lambda t: hrow[:, t, :])
                pe.wait_ge(S["xn1"], due("xn1", now, 1))
                turn(ring, "xnT1", lambda t: xn[:, t, :])
                project(ring, "q1", wq[:, :], hT[:, :])
                project(ring, "k1", wk[:, :], hT[:, :])
                if after_another:
                    weigh(before, CAUSAL, G - 1)
                project_rows(ring, "v1", hT, wv[:, :])
                if after_another:
                    turn_heads(ring, before, CAUSAL, G - 1)
                project(ring, "qm1", wqm[:, :], hT[:, :])
                for c in range(FC):
                    project(ring, f"gate{c}", w1T[:, c * P:(c + 1) * P], xnT[:, :])
                    if c == 0 and after_another:
                        turn_attn(ring, CAUSAL)
                    project(ring, f"up{c}", w2T[:, c * P:(c + 1) * P], xnT[:, :])
                    if c == 0 and after_another:
                        pe.wait_ge(taken_sem(ring, f"cols{CAUSAL}"), taken_at(ring, f"cols{CAUSAL}"))
                        mix_causal(before)
                pe.wait_ge(S["slots_q"], due("slots_q", now, 16))
                pe.wait_ge(S["slots_k"], due("slots_k", now, PLACED))
                for c in range(FC):
                    for k in range(FC):
                        slide_max(b, 2 * (FC * c + k), 2 * (FC * c + k) + 2)
                        if c == k == 0:
                            pe.wait_ge(taken_sem(ring, f"up{FC - 1}"), taken_at(ring, f"up{FC - 1}"))
                        dense(ring, f"h1_{c}", h1T, ha, c, k, k + 1)
                turn_max(ring, "slide_max", b, f"smax{H - 1}b")
                pe.wait_ge(S["slots_qm"], due("slots_qm", now, 16))
                for g in range(G):
                    tri_scores(b, "lin", QM, 10 * g, 10 * g + 3)
                    dense(ring, f"h2_{g}", h2T, hb, g, 0, 2)
                    tri_scores(b, "lin", QM, 10 * g + 3, 10 * g + 5)
                    if g:
                        weigh(now, LIN, g - 1)
                    tri_scores(b, "lin", QM, 10 * g + 5, 10 * g + 8)
                    dense(ring, f"h2_{g}", h2T, hb, g, 2, 4)
                    tri_scores(b, "lin", QM, 10 * g + 8, 10 * g + 10)
                    if g:
                        turn_heads(ring, now, LIN, g - 1)
                pe.wait_ge(S["max_placed"], due("max_placed", now, PLACED))
                for g in range(G):
                    kind, last = (SLIDE, g - 1) if g else (LIN, G - 1)
                    expert = OUT_BESIDE.get(g) if after_another else None
                    slide_scores(b, 8 * g, 8 * g + 3)
                    if g == 0:
                        third_layer(ring, now, 0, 2)
                    if expert:
                        expert_out(ring, expert, 0, 2)
                    slide_scores(b, 8 * g + 3, 8 * g + 4)
                    weigh(now, kind, last)
                    slide_scores(b, 8 * g + 4, 8 * g + 7)
                    if g == 0:
                        third_layer(ring, now, 2, 4)
                    if expert:
                        expert_out(ring, expert, 2, 4)
                    slide_scores(b, 8 * g + 7, 8 * g + 8)
                    turn_heads(ring, now, kind, last)
                    if after_another and g in IN_BEHIND:
                        expert_in(ring, IN_BEHIND[g])
                    if g == 0:
                        turn_attn(ring, LIN)
                weigh(now, SLIDE, G - 1)
                if after_another:
                    expert_out(ring, 6)
                turn_heads(ring, now, SLIDE, G - 1)
                if after_another:
                    expert_in(ring, 7, 0, 2)
                turn_attn(ring, SLIDE)
                if after_another:
                    expert_in(ring, 7, 2, 4)
                for kind in (LIN, SLIDE):
                    pe.wait_ge(taken_sem(ring, f"cols{kind}"), taken_at(ring, f"cols{kind}"))
                pe.wait_ge(S["acc_read"], due("acc_read", now, 1))
                for t in range(NT):
                    for kind in (LIN, SLIDE):
                        mm = pe.matmul(acc[:, t * P:(t + 1) * P], attnT[:, kind, t * P:(t + 1) * P], wout[:, kind, :],
                                       start=(kind == LIN), stop=(kind == SLIDE))
                mm.then_inc(S["acc_ready"], 1)
                if after_another:
                    expert_out(ring, 7)

            def second_block(b, ring):
                now = (b, 0)
                pe.wait_ge(S["hrow2"], due("hrow2", now, 1))
                turn(ring, "hT2", lambda t: hrow[:, t, :])
                pe.wait_ge(S["xn2"], due("xn2", now, 1))
                turn(ring, "xnT2", lambda t: xn[:, t, :])
                project(ring, "q2", wq1[:, :], hT[:, :])
                project(ring, "k2", wk1[:, :], hT[:, :])
                project_rows(ring, "v2", hT, wv1[:, :])
                project_rows(ring, "logits", x1T, wgT[:, :], E)
                expert_in(ring, 0)
                expert_out(ring, 0)
                for n in range(CMAX_STEPS):
                    if n // FC % 2 == 0:
                        expert_in(ring, n // (2 * FC) + 1, n % FC, n % FC + 1)
                    else:
                        expert_out(ring, n // (2 * FC) + 1, n % FC, n % FC + 1)
                    if n == 0:
                        pe.wait_ge(S["slots_q"], due("slots_q", now, 2 * 16))
                        pe.wait_ge(S["slots_k"], due("slots_k", now, 2 * PLACED))
                    causal_max(b, *cmax_units(n))
                turn_max(ring, "causal_max", b, f"cmax_{H // 2 - 1}")
                pe.wait_ge(S["gated"], due("gated", now, 1))
                turn(ring, "gatesT", lambda t: gates[:, t, :], rows=E)
                expert_in(ring, 3)
                pe.wait_ge(S["max_placed"], due("max_placed", now, 2 * PLACED))
                for g in range(G):
                    tri_scores(b, "causal", Q, 10 * g, 10 * g + 3)
                    if g == OUT3_BESIDE:
                        expert_out(ring, 3, 0, 2)
                    tri_scores(b, "causal", Q, 10 * g + 3, 10 * g + 5)
                    if g:
                        weigh(now, CAUSAL, g - 1, 0, 1)
                    tri_scores(b, "causal", Q, 10 * g + 5, 10 * g + 7)
                    if g:
                        weigh(now, CAUSAL, g - 1, 1, NT)
                    tri_scores(b, "causal", Q, 10 * g + 7, 10 * g + 8)
                    if g == OUT3_BESIDE:
                        expert_out(ring, 3, 2, 4)
                    tri_scores(b, "causal", Q, 10 * g + 8, 10 * g + 10)
                    if g:
                        turn_heads(ring, now, CAUSAL, g - 1)

            def closing(ring):
                before = (NB, -1)
                weigh(before, CAUSAL, G - 1)
                expert_in(ring, 4)
                expert_out(ring, 4)
                turn_heads(ring, before, CAUSAL, G - 1)
                expert_in(ring, 5)
                turn_attn(ring, CAUSAL)
                expert_out(ring, 5)
                pe.wait_ge(taken_sem(ring, f"cols{CAUSAL}"), taken_at(ring, f"cols{CAUSAL}"))
                mix_causal(before)
                for e in (6, 7):
                    expert_in(ring, e)
                    expert_out(ring, e)

            pe.wait_ge(S["weights"], 16 * N_LOADS)
            pe.matmul(acc[:, 0:P], wqfT, wkfT, start=True, stop=True).then_inc(S["setup_pe"], 1)
            pe.wait_ge(S["setup_dve"], 1)
            pe.matmul(acc[:, P:2 * P], wqT, bdm, start=True, stop=True).then_inc(S["setup_pe"], 1)
            pe.wait_ge(S["setup_done"], 1)
            pe.wait_ge(S["slots_set"], 16 * (len(scratch) + HG))
            first_block(0, False, ("opening", 0))
            second_block(0, ("opening", 0))
            for unit in last_units(("opening", 0)):
                pe.wait_ge(taken_sem(("opening", 0), unit), taken_at(("opening", 0), unit))
            with pe.Fori(1, NB) as b:
                first_block(b, True, ("steady", b))
                second_block(b, ("steady", b))
            for unit in last_units(("steady", NB - 1)):
                pe.wait_ge(taken_sem(("steady", NB - 1), unit), taken_at(("steady", NB - 1), unit))
            closing(("closing", NB))

        @block.scalar
        def _(act):
            def evacuate(ring, unit, to, func, scale=1.0, bias=0.0):
                act.wait_ge(full_sem(ring, unit), full_at(ring, unit))
                return act.activation(to, bank_of(ring, unit)[:, :], func, scale=scale, bias=bias)

            def split_hi(ring, now, name, nth, bias=0.0):
                before = {("q", 1): ("q", 0), ("qm", 1): ("q", 1), ("q", 2): ("qm", 1), ("k", 1): ("k", 0), ("k", 2): ("k", 1)}
                other, times = before[name, nth]
                act.wait_ge(S[f"sent_{other}"], due(f"sent_{other}", now, SENT * times))
                evacuate(ring, f"{name}{nth}", hi[:, {"q": 0, "k": 1, "qm": 0}[name], :], ACT.Identity, bias=bias)\
                    .then_inc(S[f"hi_{name}"], 1)

            def probs_from(b, unit, to, func, scale, bias, n=512):
                ring = ("score", b)
                act.wait_ge(full_sem(ring, unit), full_at(ring, unit))
                bank = bank_of(ring, unit)[:, 0:n]
                if len(to.shape) == 3:
                    bank = bank.rearrange("p (a n) -> p a n", a=2)
                return act.activation(to, bank, func, scale=scale, bias=bias).then_inc(taken_sem(ring, unit), 1)

            def pair_slot(b, kind, p):
                slots = SLOTS + 1 if kind == CAUSAL else SLOTS
                if kind != CAUSAL or p >= slots:
                    act.wait_ge(S["heads_out"], due("heads_out", (b, 0), (H // 2 * kind + p - slots) // 2 + 1))
                return slot_of(kind, p)

            def tri_probs(b, kind, tag, p, func, scale, bias):
                slot = pair_slot(b, kind, p)
                for n, h in enumerate((2 * p, 2 * p + 1)):
                    probs_from(b, f"{tag}{h}a", slot[:, PROBS * n:PROBS * n + 512], func, scale, bias)
                    probs_from(b, f"{tag}{h}b", slot[:, PROBS * n + 512:PROBS * n + 1024], func, scale, bias)
                probs_from(b, f"{tag}_{p}", slot.rearrange("p (h n) -> p h n", h=2)[:, :, 1024:PROBS], func, scale, bias)

            def slide_probs(b, p):
                slot = pair_slot(b, SLIDE, p)
                for n, h in enumerate((2 * p, 2 * p + 1)):
                    at = NT * WQ * n
                    probs_from(b, f"slide{h}a", slot[:, at:at + 2 * WQ], ACT.Exp, SCALE, 0.0, 2 * WQ)
                    probs_from(b, f"slide{h}b", slot[:, at + 2 * WQ:at + 3 * WQ + P], ACT.Exp, SCALE, 0.0, WQ + P)

            def gelu(ring, e):
                hidden = (ha, hb)[e % 2]
                for c in range(FC):
                    evacuate(ring, f"moe{e}_{c}", hidden[:, c, :], ACT.Gelu, bias=b1[:, FC * e + c:FC * e + c + 1])\
                        .then_inc(taken_sem(ring, f"moe{e}_{c}"), 1)

            def first_block(b, after_another, ring):
                now = (b, 0)
                evacuate(ring, "hT1", hT[:, :], ACT.Identity, scale=norm_w[:, 0:1]).then_inc(taken_sem(ring, "hT1"), 1)
                for name in ("q", "k", "qm"):
                    split_hi(ring, now, name, 1)
                for c in range(FC):
                    evacuate(ring, f"gate{c}", ha[:, c, :], ACT.Silu, scale=s1[:, c:c + 1]).then_inc(taken_sem(ring, f"gate{c}"), 1)
                for c in range(FC):
                    evacuate(ring, f"h1_{c}", hb[:, c, :], ACT.Gelu, scale=sh1[:, c:c + 1]).then_inc(taken_sem(ring, f"h1_{c}"), 1)
                for g in range(G):
                    tri_probs(b, LIN, "lin", 2 * g, ACT.Square, 0.5, 1.0)
                    tri_probs(b, LIN, "lin", 2 * g + 1, ACT.Square, 0.5, 1.0)
                    evacuate(ring, f"h2_{g}", ha[:, g, :], ACT.Gelu, scale=sh2[:, g:g + 1]).then_inc(taken_sem(ring, f"h2_{g}"), 1)
                for g in range(G):
                    slide_probs(b, 2 * g)
                    slide_probs(b, 2 * g + 1)
                    if after_another and g in IN_BEHIND:
                        gelu(ring, IN_BEHIND[g])
                if after_another:
                    gelu(ring, 7)

            def second_block(b, ring):
                now = (b, 0)
                evacuate(ring, "hT2", hT[:, :], ACT.Identity, scale=gamma[:, 0:1], bias=beta[:, 0:1]).then_inc(taken_sem(ring, "hT2"), 1)
                split_hi(ring, now, "q", 2, bq1[:, 0:1])
                split_hi(ring, now, "k", 2, bk1[:, 0:1])
                for e in range(EARLY):
                    gelu(ring, e)
                for p in range(H // 2):
                    tri_probs(b, CAUSAL, "causal", p, ACT.Exp, SCALE, 0.0)

            act.wait_ge(S["setup_done"], 1)
            act.wait_ge(S["weights"], 16 * N_LOADS)
            first_block(0, False, ("opening", 0))
            second_block(0, ("opening", 0))
            with act.Fori(1, NB) as b:
                first_block(b, True, ("steady", b))
                second_block(b, ("steady", b))
            for e in range(EARLY, E):
                gelu(("closing", NB), e)

        @block.gpsimd
        def _(pool):
            def mask_tri(b, kind, tag, p):
                pair = slot_of(kind, p).rearrange("p (h n) -> p h n", h=2)
                last_unit = f"{tag}_{p}"
                pool.wait_ge(taken_sem(("score", b), last_unit), taken_at(("score", b), last_unit))
                pool.sem_inc(S["unread"], 1)
                for n in range(2):
                    three = pair[:, n, :].rearrange("p (n c) -> p n c", c=256)[:, 0:5:2, 0:P]
                    pool.affine_select(out=three, in_=three, compare_op=ALU.is_ge, fill=0.0, base=0,
                                       pattern=[[0, 3], [1, P]], channel_multiplier=-1)
                last = pair[:, :, TRI_AT[3]:TRI_AT[3] + P]
                pool.affine_select(out=last, in_=last, compare_op=ALU.is_ge, fill=0.0, base=0,
                                   pattern=[[0, 2], [1, P]], channel_multiplier=-1).then_inc(S["probs_ready"], 1)

            def mask_slide(b, p):
                last_unit = f"slide{2 * p + 1}b"
                pool.wait_ge(taken_sem(("score", b), last_unit), taken_at(("score", b), last_unit))
                pool.sem_inc(S["unread"], 1)
                tiles = slot_of(SLIDE, p)[:, 0:2 * NT * WQ].rearrange("p (n c) -> p n c", c=WQ)
                near, far = tiles[:, :, 0:P], tiles[:, :, WIN:WQ]
                pool.affine_select(out=near, in_=near, compare_op=ALU.is_ge, fill=0.0, base=0,
                                   pattern=[[0, 2 * NT], [1, P]], channel_multiplier=-1).then_inc(S["slide_near"], 1)
                pool.wait_ge(S["slide_near"], due("slide_near", (b, 0), p + 1))
                pool.sem_inc(S["unread"], 1)
                pool.affine_select(out=far, in_=far, compare_op=ALU.is_ge, fill=0.0, base=0,
                                   pattern=[[0, 2 * NT], [-1, P]], channel_multiplier=1).then_inc(S["probs_ready"], 1)

            def power(sequence, nth):
                pool.wait_ge(S[f"stats{nth}"], due(f"stats{nth}", sequence, 1))
                for n in (1, 0):
                    pool.tensor_tensor(rs[:, n, :], pw[:, n, :], half_neg[:, :], ALU.pow).then_inc(S[f"powered{nth}"], 1)

            def norm_first(sequence):
                power(sequence, 1)
                pool.wait_ge(S["xn1"], due("xn1", sequence, 1))
                pool.tensor_tensor(xs[:, :, :], x_in[:, :, :], xn[:, :, :], ALU.add).then_inc(S["xs_ready"], 1)

            def body(b):
                now, after = (b, 0), (b, 1)
                for p in range(H // 2):
                    mask_tri(b, LIN, "lin", p)
                for p in range(H // 2):
                    mask_slide(b, p)
                power(now, 2)
                pool.wait_ge(S["acc_read"], due("acc_read", now, 2))
                pool.sem_inc(S["unread"], 1)
                pool.wait_ge(S["stored"], due("stored", now, 0))
                pool.tensor_tensor(y[:, :, :], x1[:, :, :], bo1[:, :].unsqueeze(1).to_broadcast([P, NT, P]), ALU.add)\
                    .then_inc(S["y_init"], 1)
                pool.wait_ge(S["shifted"], due("shifted", now, 1))
                pool.tensor_tensor(ex[:, :, :], euler[:, :, :], lgs[:, :, :], ALU.pow).then_inc(S["exped"], 1)
                for p in range(H // 2):
                    mask_tri(b, CAUSAL, "causal", p)
                    if p == 3:
                        norm_first(after)

            pool.wait_ge(S["setup_done"], 1)
            norm_first((0, 0))
            body(0)
            with pool.Fori(1, NB) as b:
                body(b)

        @block.vector
        def _(dve):
            def lap(name, sequence, n, ins):
                ins.then_inc(S[name], 1)
                dve.wait_ge(S[name], due(name, sequence, n))

            def normalize(sequence, nth, src, eps_inner):
                for t in range(NT):
                    last = dve.bn_stats(bn[:, t, :], src[:, t, :])
                lap(f"norm{nth}_laps", sequence, 1, last)
                dve.sem_inc(S["unread"], 1)
                for t in range(NT):
                    last = dve.bn_aggr(mv[:, t, :], bn[:, t, :])
                lap(f"norm{nth}_laps", sequence, 2, last)
                dve.tensor_scalar(pw[:, 0, :], mv[:, :, 1], EPS_LN, None, ALU.add)
                dve.tensor_scalar(pw[:, 1, :], mv[:, :, 1], 1.0 + eps_inner, eps_inner * EPS_LN, ALU.mult, ALU.add)\
                    .then_inc(S[f"stats{nth}"], 1)
                for n, to, name in ((1, hrow, "hrow"), (0, xn, "xn")):
                    dve.wait_ge(S[f"powered{nth}"], due(f"powered{nth}", sequence, 2 - n))
                    for t in range(NT):
                        last = dve.tensor_scalar(to[:, t, :], src[:, t, :], mv[:, t, 0:1], rs[:, n, t:t + 1], ALU.subtract, ALU.mult)
                    last.then_inc(S[f"{name}{nth}"], 1)

            def take(ring, unit, to, view=lambda x: x[:, :]):
                dve.wait_ge(full_sem(ring, unit), full_at(ring, unit))
                dve.tensor_copy(to, view(bank_of(ring, unit))).then_inc(taken_sem(ring, unit), 1)

            def split_lo(ring, now, name, nth, bias=None):
                part, unit = {"q": 0, "k": 1, "qm": 0}[name], f"{name}{nth}"
                dve.wait_ge(S[f"hi_{name}"], due(f"hi_{name}", now, nth))
                if bias is None:
                    ins = dve.tensor_tensor(lo[:, part, :], bank_of(ring, unit)[:, :], hi[:, part, :].bitcast(F32), ALU.subtract)
                else:
                    ins = dve.scalar_tensor_tensor(out=lo[:, part, :], in0=bank_of(ring, unit)[:, :], scalar=bias,
                                                   in1=hi[:, part, :].bitcast(F32), op0=ALU.add, op1=ALU.subtract)
                ins.then_inc(taken_sem(ring, unit), 1)

            def v_heads(bank):
                return bank[:, :].rearrange("p (n d) -> p n d", d=D)

            V_to = V[:, :, :, 0:D].rearrange("p t h d -> p (t h) d")

            def mx_at(h, j):
                at = (h % HG) * G * NT + (h // HG) * NT + j
                return mx[:, at:at + 1]

            def row_max(b, unit, heads_and_tiles):
                ring = ("score", b)
                dve.wait_ge(full_sem(ring, unit), full_at(ring, unit))
                for h, j, at, n in heads_and_tiles:
                    last = dve.tensor_reduce(mx_at(h, j), bank_of(ring, unit)[:, at:at + n], AX_X, ALU.max)
                last.then_inc(taken_sem(ring, unit), 1)

            def slide_max(b):
                for h in range(H):
                    row_max(b, f"smax{h}a", [(h, 0, 0, P), (h, 1, WQ, WQ)])
                    row_max(b, f"smax{h}b", [(h, 2, 0, WQ), (h, 3, WQ, WQ)])

            def causal_max(b, first, last):
                for n in range(first, last):
                    p, u = n // 5, n % 5
                    h = 2 * p + u // 2
                    if u == 4:
                        parts = [(2 * p, 1, 0, 256), (2 * p + 1, 1, 256, 256)]
                    else:
                        parts = [(h, 2, 0, 384), (h, 0, 384, 128)] if u % 2 else [(h, 3, 0, 512)]
                    row_max(b, tri_units("cmax")[n], parts)

            def negate_max(ring, unit):
                dve.wait_ge(full_sem(ring, unit), full_at(ring, unit))
                dve.tensor_scalar(mrow[:, :], bank_of(ring, unit)[0:H * NT, 0:P], -1.0, None, ALU.mult).then_inc(taken_sem(ring, unit), 1)

            def copy_heads(sequence, kind, g):
                nth = G * kind + g
                dve.wait_ge(S["heads_out"], due("heads_out", sequence, nth + 1))
                dve.tensor_copy(ot[:, nth % 2, :], heads[nth % 2][:, :]).then_inc(S["heads_copied"], 1)

            def divide_rows(ring, sequence, kind, g):
                unit = f"rows{kind}_{g}"
                dve.wait_ge(full_sem(ring, unit), full_at(ring, unit))
                bank = bank_of(ring, unit)[:, :].rearrange("p (t i r) -> p t i r", t=NT, r=ROWS)
                if kind == LIN:
                    lap("divide_laps", sequence, 2 * g + 1, dve.tensor_scalar(den[:, :, :], bank[:, :, :, D], EPS_LIN, None, ALU.add))
                    lap("divide_laps", sequence, 2 * g + 2, dve.reciprocal(rden[:, :, :], den[:, :, :]))
                else:
                    lap("divide_laps", sequence, G * (kind + 1) + g + 1, dve.reciprocal(rden[:, :, :], bank[:, :, :, D]))
                to = attn[:, :, HG * D * g:HG * D * (g + 1)].rearrange("p t (i d) -> p t i d", d=D)
                dve.tensor_tensor(to, bank[:, :, :, 0:D], rden[:, :, :].unsqueeze(3).to_broadcast([P, NT, HG, D]), ALU.mult)\
                    .then_inc(taken_sem(ring, unit), 1)

            def choose_experts(ring, now):
                dve.wait_ge(taken_sem(ring, "logits"), taken_at(ring, "logits"))
                lap("choice_laps", now, 1, dve.tensor_reduce(m1[:, :], lg[:, :, :], AX_X, ALU.max))
                dve.tensor_tensor(lgs[:, :, :], lg[:, :, :], m1[:, :].unsqueeze(2).to_broadcast([P, NT, E]), ALU.subtract).then_inc(S["shifted"], 1)
                other, own = lg[:, :, :].unsqueeze(2).to_broadcast([P, NT, E, E]), lg[:, :, :].unsqueeze(3).to_broadcast([P, NT, E, E])
                above4, equal4 = (x[:, :, :].rearrange("p t (e j) -> p t e j", j=E) for x in (above, equal))
                dve.tensor_tensor(above4, other, own, ALU.is_gt)
                lap("choice_laps", now, 2, dve.tensor_tensor(equal4, other, own, ALU.is_equal))
                lap("choice_laps", now, 3, dve.tensor_tensor(equal[:, :, :], equal[:, :, :], earlier[:, :].unsqueeze(1).to_broadcast([P, NT, E * E]), ALU.mult))
                lap("choice_laps", now, 4, dve.tensor_tensor(above[:, :, :], above[:, :, :], equal[:, :, :], ALU.add))
                lap("choice_laps", now, 5, dve.tensor_reduce(rank[:, :, :], above4, AX_X, ALU.add))
                dve.wait_ge(S["exped"], due("exped", now, 1))
                lap("choice_laps", now, 6, dve.scalar_tensor_tensor(out=exs[:, :, :], in0=rank[:, :, :], scalar=1.5, in1=ex[:, :, :], op0=ALU.is_lt, op1=ALU.mult))
                lap("choice_laps", now, 7, dve.tensor_reduce(gsum[:, :], exs[:, :, :], AX_X, ALU.add))
                lap("choice_laps", now, 8, dve.reciprocal(rsum[:, :], gsum[:, :]))
                dve.tensor_tensor(gates[:, :, :], exs[:, :, :], rsum[:, :].unsqueeze(2).to_broadcast([P, NT, E]), ALU.mult).then_inc(S["gated"], 1)
                dve.wait_ge(S["gated"], due("gated", now, 1))

            def combine(ring, e):
                unit = f"moe{e}_out"
                dve.wait_ge(full_sem(ring, unit), full_at(ring, unit))
                for t in range(NT):
                    last = dve.scalar_tensor_tensor(out=y[:, t, :], in0=bank_of(ring, unit)[:, t * P:(t + 1) * P], scalar=gates[:, t, e:e + 1],
                                                    in1=y[:, t, :], op0=ALU.mult, op1=ALU.add)
                last.then_inc(taken_sem(ring, unit), 1)
                dve.wait_ge(taken_sem(ring, unit), taken_at(ring, unit))

            def add_third_layer(now):
                dve.wait_ge(S["xs_ready"], due("xs_ready", now, 1))
                dve.sem_inc(S["unread"], 1)
                dve.wait_ge(S["acc_ready"], due("acc_ready", now, 1))
                dve.tensor_tensor(xs[:, :, :], acc[:, :].rearrange("p (t n) -> p t n", n=P), xs[:, :, :], ALU.add).then_inc(S["acc_read"], 1)
                dve.wait_ge(S["acc_read"], due("acc_read", now, 1))

            def add_mixed(sequence):
                dve.wait_ge(S["acc_ready"], due("acc_ready", sequence, 3))
                dve.tensor_tensor(y[:, :, :], acc[:, :].rearrange("p (t n) -> p t n", n=P), y[:, :, :], ALU.add).then_inc(S["acc_read"], 1)
                dve.wait_ge(S["acc_read"], due("acc_read", sequence, 3))

            def first_block(b, after_another, ring):
                now, before = (b, 0), (b, -1)
                take(ring, "xnT1", xnT[:, :])
                split_lo(ring, now, "q", 1)
                split_lo(ring, now, "k", 1)
                if after_another:
                    copy_heads(before, CAUSAL, G - 1)
                take(ring, "v1", V_to, v_heads)
                if after_another:
                    divide_rows(ring, before, CAUSAL, G - 1)
                split_lo(ring, now, "qm", 1)
                if after_another:
                    take(ring, f"cols{CAUSAL}", attnT[:, 0, :])
                for c in range(FC):
                    dve.wait_ge(taken_sem(ring, f"gate{c}"), taken_at(ring, f"gate{c}"))
                    dve.wait_ge(full_sem(ring, f"up{c}"), full_at(ring, f"up{c}"))
                    dve.scalar_tensor_tensor(out=ha[:, c, :], in0=bank_of(ring, f"up{c}")[:, :], scalar=s2[:, c:c + 1],
                                             in1=ha[:, c, :], op0=ALU.mult, op1=ALU.mult).then_inc(taken_sem(ring, f"up{c}"), 1)
                    if c == 0 and after_another:
                        add_mixed(before)
                slide_max(b)
                negate_max(ring, "slide_max")
                for g in range(G):
                    copy_heads(now, LIN, g)
                    if g == G - 1:
                        add_third_layer(now)
                    divide_rows(ring, now, LIN, g)
                take(ring, f"cols{LIN}", attnT[:, LIN, :])
                for g in range(G):
                    copy_heads(now, SLIDE, g)
                    if after_another and g + 1 in OUT_BESIDE:
                        combine(ring, OUT_BESIDE[g + 1])
                    if after_another and g == G - 1:
                        combine(ring, 6)
                    divide_rows(ring, now, SLIDE, g)
                take(ring, f"cols{SLIDE}", attnT[:, SLIDE, :])

            def second_block(b, after_another, ring):
                now = (b, 0)
                dve.wait_ge(S["acc_ready"], due("acc_ready", now, 2))
                dve.tensor_tensor(x1[:, :, :], acc[:, :].rearrange("p (t n) -> p t n", n=P), xs[:, :, :], ALU.add).then_inc(S["acc_read"], 1)
                dve.wait_ge(S["acc_read"], due("acc_read", now, 2))
                normalize(now, 2, x1, EPS_LN)
                if after_another:
                    combine(ring, 7)
                take(ring, "xnT2", x1T[:, :])
                split_lo(ring, now, "q", 2, bq1[:, 0:1])
                split_lo(ring, now, "k", 2, bk1[:, 0:1])
                dve.wait_ge(full_sem(ring, "v2"), full_at(ring, "v2"))
                dve.tensor_tensor(V[:, :, :, 0:D], bank_of(ring, "v2")[:, :].rearrange("p (t h d) -> p t h d", t=NT, d=D),
                                  bv1[:, :].rearrange("p (h d) -> p h d", d=D).unsqueeze(1).to_broadcast([P, NT, H, D]), ALU.add)\
                    .then_inc(taken_sem(ring, "v2"), 1)
                take(ring, "logits", lg[:, :, :], lambda x: x[:, 0:NT * E].rearrange("p (t e) -> p t e", e=E))
                choose_experts(ring, now)
                dve.wait_ge(S["y_init"], due("y_init", now, 1))
                combine(ring, 0)
                for n in range(CMAX_STEPS):
                    causal_max(b, *cmax_units(n))
                    if n % (2 * FC) == 2 * FC - 1:
                        combine(ring, n // (2 * FC) + 1)
                negate_max(ring, "causal_max")
                take(ring, "gatesT", gatesT[:, :], lambda x: x[0:E, :])
                for g in range(G - 1):
                    if g == OUT3_BESIDE:
                        combine(ring, 3)
                    copy_heads(now, CAUSAL, g)
                    divide_rows(ring, now, CAUSAL, g)
                    if g == 0:
                        first_norm((b, 1))

            def first_norm(sequence):
                dve.wait_ge(S["x_loaded"], due("x_loaded", sequence, 16))
                normalize(sequence, 1, x_in, EPS_RMS)

            dve.memset(half_neg[:, :], -0.5)
            dve.memset(euler[:, :, :], math.e)
            dve.memset(mx[:, :], 0.0)
            dve.memset(probs[:, :, :], 0.0)
            dve.memset(K[:, :, :].bitcast(F32), 0.0).then_inc(S["keys_cleared"], 1)
            dve.memset(V[:, :, :, D + 1:ROWS], 0.0)
            dve.memset(V[:, :, :, D:D + 1], 1.0)
            dve.wait_ge(S["weights"], 16 * N_LOADS)
            dve.tensor_copy(identb[:, :], ident[:, :])
            dve.tensor_copy(causal_neg[:, :], causal_f)
            dve.tensor_copy(slide_neg[:, :], slide_f)
            dve.tensor_tensor(w3T[:, :, :], w3T[:, :, :], s3.unsqueeze(1).to_broadcast([P, FC, P]), ALU.mult)
            dve.wait_ge(S["setup_pe"], 1)
            dve.tensor_tensor(bdm, acc[:, 0:P], blocks, ALU.mult).then_inc(S["setup_dve"], 1)
            dve.wait_ge(S["setup_pe"], 2)
            for name, (_, first) in counts.items():
                if first:
                    dve.sem_inc(S[name], first)
            dve.tensor_copy(wqm[:, :], acc[:, P:2 * P]).then_inc(S["setup_done"], 1)
            first_norm((0, 0))
            first_block(0, False, ("opening", 0))
            second_block(0, False, ("opening", 0))
            with dve.Fori(1, NB) as b:
                first_block(b, True, ("steady", b))
                second_block(b, True, ("steady", b))
            copy_heads((NB, -1), CAUSAL, G - 1)
            combine(("closing", NB), 4)
            divide_rows(("closing", NB), (NB, -1), CAUSAL, G - 1)
            take(("closing", NB), f"cols{CAUSAL}", attnT[:, 0, :])
            combine(("closing", NB), 5)
            add_mixed((NB, -1))
            combine(("closing", NB), 6)
            combine(("closing", NB), 7)


def lay_out(i):
    import numpy as np

    def c(a):
        return np.ascontiguousarray(np.asarray(a, np.float32))

    def chunks(a):
        return c(np.reshape(a, (-1, P)).T)

    q, k = np.arange(P)[:, None], np.arange(P)[None, :]
    w = np.arange(WQ)[None, :]
    e = np.arange(E)
    ones = np.zeros((H, D, T), np.float32)
    ones[:, 0] = 1.0
    return {
        "x": c(i["L0_attn_x"]), "wq": c(i["L0_attn_Wq"]), "wqT": c(np.transpose(i["L0_attn_Wq"])), "wk": c(i["L0_attn_Wk"]),
        "wv": c(i["L0_attn_Wv"]), "wqfT": c(np.tile(np.transpose(i["L0_attn_Wqf"]), (1, H))),
        "wkfT": c(np.tile(np.transpose(i["L0_attn_Wkf"]), (1, H))), "wout": c(np.reshape(i["L0_attn_Wout"], (2, P, P))),
        "norm_w": c(np.reshape(i["L0_attn_norm_w"], (P, 1))),
        "w1T": c(np.transpose(i["L0_ffn_w1_w"])), "w2T": c(np.transpose(i["L0_ffn_w2_w"])), "h1T": c(np.transpose(i["L0_ffn_h1_w"])),
        "h2T": c(np.transpose(i["L0_ffn_h2_w"])), "w3T": c(np.transpose(i["L0_ffn_w3_w"])),
        "s1": chunks(i["L0_ffn_w1_s"]), "s2": chunks(i["L0_ffn_w2_s"]), "sh1": chunks(i["L0_ffn_h1_s"]), "sh2": chunks(i["L0_ffn_h2_s"]),
        "s3": c(i["L0_ffn_w3_s"]),
        "wq1": c(i["L1_attn_Wq"]), "wk1": c(i["L1_attn_Wk"]), "wv1": c(i["L1_attn_Wv"]), "wo1": c(i["L1_attn_Wo"]),
        "bq1": c(np.reshape(i["L1_attn_bq"], (P, 1))), "bk1": c(np.reshape(i["L1_attn_bk"], (P, 1))), "bv1": c(i["L1_attn_bv"]),
        "bo1": c(i["L1_attn_bo"]), "gamma": c(np.reshape(i["L1_attn_ln_gamma"], (P, 1))), "beta": c(np.reshape(i["L1_attn_ln_beta"], (P, 1))),
        "wgT": c(np.transpose(i["L1_ffn_Wg"])), "W1": c(i["L1_ffn_W1"]), "b1": chunks(i["L1_ffn_b1"]), "W2": c(i["L1_ffn_W2"]), "b2": c(i["L1_ffn_b2"]),
        "ident": np.eye(P, dtype=np.float32), "causal_neg": np.where(k <= q, 0.0, NEG).astype(np.float32),
        "slide_neg": np.where((w - WIN <= q) & (w >= q), 0.0, NEG).astype(np.float32),
        "earlier": c(np.broadcast_to((e[None, :] < e[:, None]).reshape(1, -1), (P, E * E))),
        "blocks": (q // D == k // D).astype(np.float32), "slot_q": np.zeros((H, D, T), np.float32), "slot_k": ones,
    }


def kernel(**inputs):
    import concourse.bacc as bacc
    from concourse.bass_utils import run_bass_kernel_spmd as run

    nc = bacc.Bacc("TRN2", target_bir_lowering=False, num_devices=1)
    arrays = lay_out(inputs)
    dram = {name: nc.dram_tensor(f"in_{name}", shape, F32, kind="ExternalInput").ap() for name, shape in SHAPES.items()}
    out = nc.dram_tensor("out", (NB, T, P), F32, kind="ExternalOutput").ap()
    build(nc, dram, out)
    r = run(nc, [{f"in_{name}": a for name, a in arrays.items()}], core_ids=[0])
    return r.results[0]["out"]
```

```python
from contextlib import ExitStack
import math

import concourse.bass as bass
from concourse import mybir

F32 = mybir.dt.float32
F32R = mybir.dt.float32r
BF16 = mybir.dt.bfloat16
ALU = mybir.AluOpType
ACT = mybir.ActivationFunctionType
AX_X = mybir.AxisListType.X

P = 128
NB, T = 8, 512
NT = T // P
H, D = 16, 8
G, HG = 4, 4
ROWS = 32
FC = 4
E = 8
WIN = 64
WQ = P + WIN
LIN, SLIDE, CAUSAL = range(3)
NEG = -1e30
EPS_LN, EPS_RMS, EPS_LIN = 1e-5, 1e-6, 1e-6
SCALE = float(D) ** -0.5

TRI_AT = {0: 0, 1: 512, 3: 896, 2: 1024}
TRI_N = {j: T - P * j for j in range(NT)}
PROBS = 1280
SLIDE_AT = {j: WQ * j for j in range(NT)}
SLIDE_N = {j: min(WQ, T - P * j) for j in range(NT)}

EARLY = 4
SENT, PLACED = 3 * 16, HG * 16
SETUP_LOADS, FIRST_LOADS, LATER_LOADS, EXPERT_LOADS = 5, 10, 20, 3
SLOTS = 3

OUT_BESIDE = {(1, 0): (4, 0, 2), (1, 1): (4, 2, 4), (2, 0): (5, 0, 1), (2, 1): (5, 1, 2), (3, 0): (5, 2, 4)}
OUT3_BESIDE = 0
CMAX_STEPS = 16
IN_BEHIND = {0: 4, 1: 5, 3: 6}

def banks_of(ring):
    return 4 if ring == "score" else 3


def tri_units(tag):
    return [f"{tag}{u}" for p in range(H // 2) for u in (f"{2 * p}a", f"{2 * p}b", f"{2 * p + 1}a", f"{2 * p + 1}b", f"_{p}")]


def slide_units(tag):
    return [f"{tag}{h}{u}" for h in range(H) for u in "ab"]


def expert_in_units(e):
    return [f"moe{e}_{c}" for c in range(FC)]


def expert_units(e):
    return expert_in_units(e) + [f"moe{e}_out"]


def misc_units(after_another):
    def late(units):
        return units if after_another else []
    units = ["hT1", "xnT1", "q1", "k1", "v1"] + late([f"rows{CAUSAL}_{G - 1}"]) + ["qm1", "gate0"] + late([f"cols{CAUSAL}"]) + ["up0"]
    units += late(["mixed_causal"])
    units += [f"{w}{c}" for c in range(1, FC) for w in ("gate", "up")] + [f"h1_{c}" for c in range(FC)] + ["slide_max"]
    for g in range(G):
        units += [f"h2_{g}"] + ([f"rows{LIN}_{g - 1}"] if g else [])
    for g in range(G):
        units += late([f"moe{e}_out" for (beside, _), (e, first, _) in OUT_BESIDE.items() if beside == g and first == 0])
        units += [] if g else ["third_layer"]
        units += [f"rows{SLIDE}_{g - 1}" if g else f"rows{LIN}_{G - 1}"]
        units += late(expert_in_units(IN_BEHIND[g]) if g in IN_BEHIND else []) + ([] if g else [f"cols{LIN}"])
    units += late(["moe6_out"]) + [f"rows{SLIDE}_{G - 1}"] + late(["moe7_0", "moe7_1"]) + [f"cols{SLIDE}"]
    units += late(["moe7_2", "moe7_3"]) + ["mixed_first"] + late(["moe7_out"])
    units += ["hT2", "xnT2", "q2", "k2", "v2", "logits"] + [u for e in range(EARLY - 1) for u in expert_units(e)]
    return units + ["causal_max", "gatesT"] + expert_units(EARLY - 1) + [f"rows{CAUSAL}_{g}" for g in range(G - 1)]


UNITS = {
    "score": slide_units("smax") + tri_units("lin") + slide_units("slide") + tri_units("cmax") + tri_units("causal"),
    "opening": misc_units(False), "steady": misc_units(True),
    "closing": expert_in_units(4) + [f"rows{CAUSAL}_{G - 1}"] + expert_in_units(5) + ["moe4_out", f"cols{CAUSAL}"] + expert_in_units(6)
    + ["moe5_out", "mixed_causal"] + expert_in_units(7) + ["moe6_out", "moe7_out"],
}
PLACE = {ring: {u: (n % banks_of(ring), n // banks_of(ring)) for n, u in enumerate(units)} for ring, units in UNITS.items()}


def cmax_units(n):
    each = 5 * H // 2
    steps = CMAX_STEPS - 2
    return min(each * n // steps, each), min(each * (n + 1) // steps, each)


def units_in(ring, bank):
    return len(range(bank, len(UNITS[ring]), banks_of(ring)))


SHAPES = {
    "x": (NB, T, P), "wq": (P, P), "wqT": (P, P), "wk": (P, P), "wv": (P, P), "wqfT": (16, P), "wkfT": (16, P),
    "wout": (2, P, P), "norm_w": (P, 1),
    "w1T": (P, T), "w2T": (P, T), "h1T": (T, T), "h2T": (T, T), "w3T": (T, P),
    "s1": (P, FC), "s2": (P, FC), "sh1": (P, FC), "sh2": (P, FC), "s3": (P,),
    "wq1": (P, P), "wk1": (P, P), "wv1": (P, P), "wo1": (P, P), "bq1": (P, 1), "bk1": (P, 1), "bv1": (P,), "bo1": (P,),
    "gamma": (P, 1), "beta": (P, 1), "wgT": (P, E),
    "W1": (E, P, T), "b1": (P, E * FC), "W2": (E, T, P), "b2": (E, P),
    "ident": (P, P), "causal_neg": (P, P), "slide_neg": (P, WQ), "earlier": (P, E * E), "blocks": (P, P),
    "slot_q": (H, D, T), "slot_k": (H, D, T),
}


def build(nc, dram, out):
    with ExitStack() as ctx:
        def sb(name, shape, dt=F32):
            return ctx.enter_context(nc.sbuf_tensor(name, shape, dt))

        def pb(name, shape=(P, 512)):
            return ctx.enter_context(nc.psum_tensor(name, list(shape), F32))

        wq, wk, wv, wqm = (sb(n, [P, P]) for n in ("wq_s", "wk_s", "wv_s", "wqm_s"))
        wout = sb("wout_s", [P, 2, P])
        norm_w, gamma, beta, bq1, bk1 = (sb(n + "_s", [P, 1]) for n in ("norm_w", "gamma", "beta", "bq1", "bk1"))
        w1T, w2T = sb("w1T_s", [P, T]), sb("w2T_s", [P, T])
        h1T, h2T, w3T = sb("h1T_s", [P, FC, T]), sb("h2T_s", [P, FC, T]), sb("w3T_s", [P, FC, P])
        s1, s2, sh1, sh2 = (sb(n + "_s", [P, FC]) for n in ("s1", "s2", "sh1", "sh2"))
        bv1, bo1 = (sb(n + "_s", [P, P]) for n in ("bv1", "bo1"))
        wq1, wk1, wv1, wo1 = (sb(n + "_s", [P, P]) for n in ("wq1", "wk1", "wv1", "wo1"))
        wgT = sb("wgT_s", [P, E])
        W1, W2 = sb("W1_s", [P, E, T]), sb("W2_s", [P, E, FC, P])
        b1, b2 = sb("b1_s", [P, E * FC]), sb("b2_s", [E, P])
        ident, identb = sb("ident_s", [P, P]), sb("identb", [P, P], BF16)
        causal_neg, slide_neg = sb("causal_neg_s", [P, P], BF16), sb("slide_neg_s", [P, WQ], BF16)
        earlier = sb("earlier_s", [P, E * E])
        half_neg, euler = sb("half_neg", [P, NT]), sb("euler", [P, NT, E])

        x_in, xs, xn, hrow = (sb(n, [P, NT, P]) for n in ("x_in", "xs", "xn", "hrow"))
        xnT, hT = sb("xnT_s", [P, T]), sb("hT_s", [P, T])
        bn, mv, pw, rs = sb("bn", [P, NT, 6]), sb("mv", [P, NT, 2]), sb("pw", [P, 2, NT]), sb("rs", [P, 2, NT])
        hi, lo = sb("hi", [P, 2, T], F32R), sb("lo", [P, 2, T], F32R)
        Q, QM, K = sb("Q", [P, G, T], F32R), sb("QM", [P, G, T], F32R), sb("K", [P, H, T], F32R)
        V = sb("V", [P, NT, H, D + 1])
        probs = sb("probs", [P, SLOTS, 2 * PROBS])
        shared = sb("shared", [P, 2 * PROBS + FC * T])
        mx, mrow = sb("mx", [P, P]), sb("mrow", [HG * G * NT, P], F32R)
        ot = sb("ot", [P, 2, T])
        den, rden = sb("den", [P, NT, HG]), sb("rden", [P, NT, HG])
        attn = sb("attn", [P, NT, P])
        attnT = sb("attnT", [P, 2, T])
        ha, hb = (shared[:, at:at + FC * T].rearrange("p (c t) -> p c t", t=T) for at in (2 * PROBS - FC * T, 2 * PROBS))
        x1, y = sb("x1", [P, NT, P]), sb("y", [P, NT, P])
        lg, lgs, ex, exs, gates, rank = (sb(n, [P, NT, E]) for n in ("lg", "lgs", "ex", "exs", "gates", "rank"))
        above, equal = (hrow[:, n:n + 2, :].rearrange("p a (b e) -> p (a b) e", e=E * E) for n in (0, 2))
        m1, gsum, rsum = (sb(n, [P, NT]) for n in ("m1", "gsum", "rsum"))
        gatesT = sb("gatesT_s", [E, T])
        x1T = sb("x1T", [P, T])
        wqT, blocks, bdm = (ha[:, 0, P * n:P * (n + 1)] for n in range(3))
        causal_f, slide_f = x1[:, 0, :], x1[:, 1:3, :].rearrange("p a n -> p (a n)")[:, 0:WQ]
        s3 = y[:, 0, :]
        wqfT, wkfT = (hb[0:16, 0, P * n:P * (n + 1)] for n in range(2))

        score = [pb(f"score{i}") for i in range(banks_of("score"))]
        misc = [pb(f"misc{i}") for i in range(banks_of("steady"))]
        heads = pb("heads")

        scratch = {n: nc.dram_tensor(f"slots_of_{n}", (H, ROWS, T), F32, kind="Internal").ap() for n in ("q", "k", "qm")}

        counts = {
            "unread": (0, 0), "setup_weights": (0, 0), "first_weights": (0, 0), "masks_ready": (0, 0), "later_weights": (0, 0), "expert_weights": (0, 0), "w3_scaled": (0, 0), "cleared": (0, 0), "slots_set": (0, 0), "keys_cleared": (0, 0), "setup_pe": (0, 0), "setup_dve": (0, 0), "setup_done": (0, 0),
            "x_loaded": (16, 0), "stored": (16, 16), "xs_ready": (1, 0), "y_init": (1, 0),
            "stats1": (1, 0), "stats2": (1, 0), "powered1": (2, 0), "powered2": (2, 0), "xn1": (1, 0), "xn2": (1, 0), "hrow1": (1, 0), "hrow2": (1, 0),
            "norm1_laps": (2, 0), "norm2_laps": (2, 0), "divide_laps": (4 * G, 0), "choice_laps": (8, 0),
            "hi_q": (2, 0), "hi_k": (2, 0), "hi_qm": (1, 0),
            "sent_q": (2 * SENT, 16), "sent_k": (2 * SENT, 16), "sent_qm": (SENT, 16),
            "slots_q": (2 * 16, 0), "slots_k": (2 * PLACED, 0), "slots_qm": (16, 0), "max_placed": (2 * PLACED, 0),
            "slide_near": (H // 2, 0), "probs_ready": (3 * H // 2, 0),
            "heads_out": (3 * G, 2), "heads_copied": (3 * G, 2),
            "x1_ready": (1, 0), "shifted": (1, 0), "exped": (1, 0), "gated": (1, 0),
        }
        for ring in UNITS:
            for bank in range(banks_of(ring)):
                counts[f"{ring}_full{bank}"] = (units_in(ring, bank), 0)
                counts[f"{ring}_taken{bank}"] = (units_in(ring, bank), 1)
        def slot_of(kind, p):
            if kind == CAUSAL:
                return shared[:, 0:2 * PROBS] if p % (SLOTS + 1) == SLOTS else probs[:, p % (SLOTS + 1), :]
            return probs[:, (H // 2 * kind + p) % SLOTS, :]

        S = {name: ctx.enter_context(nc.semaphore(name)) for name in counts}

        def due(name, sequence, count):
            (b, ahead), (per_sequence, setup) = sequence, counts[name]
            return b * per_sequence + (ahead * per_sequence + setup + count)

        def ring_count(ring, bank, n):
            (name, b), per_body = ring, units_in(ring[0], bank)
            if name == "score":
                return b * per_body + n
            return b * per_body + (n - per_body) if name == "steady" else n

        def full_sem(ring, unit):
            return S[f"{ring[0]}_full{PLACE[ring[0]][unit][0]}"]

        def taken_sem(ring, unit):
            return S[f"{ring[0]}_taken{PLACE[ring[0]][unit][0]}"]

        def full_at(ring, unit):
            bank, n = PLACE[ring[0]][unit]
            return ring_count(ring, bank, n + 1)

        def taken_at(ring, unit):
            bank, n = PLACE[ring[0]][unit]
            return ring_count(ring, bank, n + 2)

        def free_at(ring, unit):
            bank, n = PLACE[ring[0]][unit]
            return ring_count(ring, bank, n + 1)

        def last_units(ring):
            return UNITS[ring[0]][-banks_of(ring[0]):]

        def bank_of(ring, unit):
            return (score if ring[0] == "score" else misc)[PLACE[ring[0]][unit][0]]

        block = ctx.enter_context(nc.Block())
        x_v = dram["x"].rearrange("b (t p) d -> b p t d", p=P)
        out_v = out.rearrange("b (t p) d -> b p t d", p=P)

        @block.sync
        def _(sp):
            sp.dma_start(x_in[:, :, :], x_v[0]).then_inc(S["x_loaded"], 16)
            setup_loads = [(wqfT, dram["wqfT"]), (wkfT, dram["wkfT"]), (wqT, dram["wqT"]), (blocks, dram["blocks"]), (ident[:, :], dram["ident"])]
            for dst, src in setup_loads:
                sp.dma_start(dst, src).then_inc(S["setup_weights"], 16)
            first_loads = [(wq[:, :], dram["wq"]), (wk[:, :], dram["wk"]), (wv[:, :], dram["wv"]), (norm_w[:, :], dram["norm_w"]),
                           (w1T[:, :], dram["w1T"]), (w2T[:, :], dram["w2T"]), (s1[:, :], dram["s1"]), (s2[:, :], dram["s2"]),
                           (causal_f, dram["causal_neg"]), (slide_f, dram["slide_neg"])]
            for dst, src in first_loads:
                sp.dma_start(dst, src).then_inc(S["first_weights"], 16)
            assert (len(setup_loads), len(first_loads)) == (SETUP_LOADS, FIRST_LOADS)
            for n, name in enumerate(("q", "k", "qm")):
                sp.dma_start(scratch[name][:, 3 * D:4 * D, :], dram["slot_k" if name == "k" else "slot_q"]).then_inc(S["slots_set"], 16)
            sp.wait_ge(S["slots_set"], 16 * len(scratch))
            sp.wait_ge(S["keys_cleared"], 2)
            for i in range(HG):
                row = ROWS * i + 3 * D
                sp.dma_start(K[row:row + D, i:H:HG, :].bitcast(F32), scratch["k"].rearrange("(g i) r t -> i r g t", i=HG)[i][3 * D:4 * D])\
                    .then_inc(S["slots_set"], 16)
            sp.wait_ge(S["slots_set"], 16 * (len(scratch) + HG))

            def send(name, part, slots):
                src = {"q": 0, "k": 1, "qm": 0}[name]
                view = scratch[name].rearrange("h (s d) t -> s h d t", d=D)
                for s in slots:
                    sp.dma_start(view[s], part[:, src, :].bitcast(F32)).then_inc(S[f"sent_{name}"], 16)

            def fetch(name):
                if name == "k":
                    groups = scratch[name].rearrange("(g i) r t -> i r g t", i=HG)
                    for i in range(HG):
                        sp.dma_start(K[ROWS * i:ROWS * i + 3 * D, i:H:HG, :].bitcast(F32), groups[i][0:3 * D]).then_inc(S["slots_k"], 16)
                else:
                    to = Q if name == "q" else QM
                    sp.dma_start(to[:, :, :].bitcast(F32), scratch[name].rearrange("(g i) r t -> (i r) g t", i=HG)).then_inc(S[f"slots_{name}"], 16)

            def place_max(ring, unit):
                sp.wait_ge(taken_sem(ring, unit), taken_at(ring, unit))
                for i in range(HG):
                    row = ROWS * i + 3 * D
                    sp.dma_start(Q[row:row + 1, :, :].rearrange("p g (n t) -> p (g n) t", t=P).bitcast(F32),
                                 mrow[G * NT * i:G * NT * (i + 1), :].bitcast(F32)).then_inc(S["max_placed"], 16)

            def split_and_spread(ring, now, names, nth, groups_done):
                for name in names:
                    unit = f"{name}{nth}"
                    sp.wait_ge(S[f"hi_{name}"], due(f"hi_{name}", now, nth))
                    send(name, hi, (0, 2) if name == "k" else (0, 1))
                    sp.wait_ge(taken_sem(ring, unit), taken_at(ring, unit))
                    send(name, lo, (1,) if name == "k" else (2,))
                sp.wait_ge(S["heads_out"], due("heads_out", now, groups_done))
                sp.sem_inc(S["unread"], 1)
                for name in names:
                    sp.wait_ge(S[f"sent_{name}"], due(f"sent_{name}", now, SENT * nth))
                    fetch(name)

            def store(ring, result_of):
                sp.wait_ge(taken_sem(ring, f"moe{E - 1}_out"), taken_at(ring, f"moe{E - 1}_out"))
                sp.sem_inc(S["unread"], 1)
                sp.dma_start(out_v[result_of], y[:, :, :]).then_inc(S["stored"], 16)

            def body(b, after_another, ring):
                now = (b, 0)
                sp.wait_ge(S["xs_ready"], due("xs_ready", now, 1))
                sp.sem_inc(S["unread"], 1)
                sp.wait_ge(S["xn1"], due("xn1", now, 1))
                sp.sem_inc(S["unread"], 1)
                sp.dma_start(x_in[:, :, :], x_v[(b + 1) & (NB - 1)]).then_inc(S["x_loaded"], 16)
                split_and_spread(ring, now, ("q", "k"), 1, 0)
                split_and_spread(ring, now, ("qm",), 1, 0)
                place_max(ring, "slide_max")
                if after_another:
                    store(ring, b - 1)
                split_and_spread(ring, now, ("q", "k"), 2, 2 * G)
                place_max(ring, "causal_max")

            sp.wait_ge(S["setup_done"], 1)
            body(0, False, ("opening", 0))
            with sp.Fori(1, NB) as b:
                body(b, True, ("steady", b))
            store(("closing", NB), NB - 1)
            sp.wait_ge(S["stored"], 16 + 16 * NB)

        @block.tensor
        def _(pe):
            def to_bank(ring, unit):
                pe.wait_ge(taken_sem(ring, unit), free_at(ring, unit))
                return bank_of(ring, unit)

            def turn(ring, unit, tile, rows=P):
                bank = to_bank(ring, unit)
                for t in range(NT):
                    mm = pe.transpose(bank[0:rows, t * P:(t + 1) * P], tile(t), ident[:, :])
                mm.then_inc(full_sem(ring, unit), 1)

            def project(ring, unit, w, x):
                pe.matmul(to_bank(ring, unit)[:, :], w, x, start=True, stop=True).then_inc(full_sem(ring, unit), 1)

            def project_rows(ring, unit, x, w, n=P):
                bank = to_bank(ring, unit)
                for t in range(NT):
                    mm = pe.matmul(bank[:, t * n:(t + 1) * n], x[:, t * P:(t + 1) * P], w, start=True, stop=True)
                mm.then_inc(full_sem(ring, unit), 1)

            def dense(ring, unit, w, src, c, first, last):
                bank = to_bank(ring, unit) if first == 0 else bank_of(ring, unit)
                for k in range(first, last):
                    mm = pe.matmul(bank[:, :], w[:, k, c * P:(c + 1) * P], src[:, k, :], start=(k == 0), stop=(k == FC - 1),
                                   skip_group_check=True)
                if last == FC:
                    mm.then_inc(full_sem(ring, unit), 1)

            def scores_into(b, unit, parts):
                ring = ("score", b)
                bank = to_bank(ring, unit)
                for at, left, right, mask, mask_at in parts:
                    mm = pe.matmul(bank[:, at:at + right.shape[1]], left, right, start=True, stop=mask is None, skip_group_check=True)
                    if mask is not None:
                        at += mask_at
                        mm = pe.matmul(bank[:, at:at + mask.shape[1]], identb[:, :], mask, start=False, stop=True,
                                       skip_group_check=True)
                mm.then_inc(full_sem(ring, unit), 1)

            def q_part(buf, h, a, n):
                return buf[:, h // HG, a:a + n]

            def slide_max(b, first, last):
                for n in range(first, last):
                    h, parts = n // 2, []
                    for j in (2 * (n % 2), 2 * (n % 2) + 1):
                        if j == 0:
                            parts.append((0, q_part(Q, h, 0, P), K[:, h, 0:P], slide_neg[:, WIN:WQ], 0))
                        else:
                            parts.append((WQ * (j % 2), q_part(Q, h, P * j, P), K[:, h, P * j - WIN:P * (j + 1)], slide_neg[:, :], 0))
                    scores_into(b, slide_units("smax")[n], parts)

            def causal_max(b, first, last):
                def part(h, j, at):
                    return (at, q_part(Q, h, P * j, P), K[:, h, 0:P * (j + 1)], causal_neg[:, :], P * j)
                for n in range(first, last):
                    p, u = n // 5, n % 5
                    h = 2 * p + u // 2
                    if u == 4:
                        parts = [part(2 * p, 1, 0), part(2 * p + 1, 1, 256)]
                    else:
                        parts = [part(h, 2, 0), part(h, 0, 384)] if u % 2 else [part(h, 3, 0)]
                    scores_into(b, tri_units("cmax")[n], parts)

            def tri_scores(b, tag, buf, first, last):
                def part(h, j, at):
                    return (at, K[:, h, P * j:P * (j + 1)], q_part(buf, h, P * j, TRI_N[j]), None, 0)
                for n in range(first, last):
                    p, u = n // 5, n % 5
                    h = 2 * p + u // 2
                    if u == 4:
                        parts = [part(2 * p, 2, 0), part(2 * p + 1, 2, 256)]
                    else:
                        parts = [part(h, 1, 0), part(h, 3, 384)] if u % 2 else [part(h, 0, 0)]
                    scores_into(b, tri_units(tag)[n], parts)

            def slide_scores(b, first, last):
                for n in range(first, last):
                    h, parts = n // 2, []
                    for j in (2 * (n % 2), 2 * (n % 2) + 1):
                        parts.append((WQ * (j % 2), K[:, h, P * j:P * (j + 1)], q_part(Q, h, P * j, SLIDE_N[j]), None, 0))
                    scores_into(b, slide_units("slide")[n], parts)

            def weigh(sequence, kind, g, first=0, last=NT):
                nth = G * kind + g
                if first == 0:
                    pe.wait_ge(S["probs_ready"], due("probs_ready", sequence, 2 * nth + 2))
                    pe.wait_ge(S["heads_copied"], due("heads_copied", sequence, nth))
                starts, widths, head = (SLIDE_AT, SLIDE_N, NT * WQ) if kind == SLIDE else (TRI_AT, TRI_N, PROBS)
                for j in range(first, last):
                    for i in range(HG):
                        at = head * (i % 2) + starts[j]
                        mm = pe.matmul(heads[ROWS * i:ROWS * i + D + 1, P * j:P * j + widths[j]],
                                       V[:, j, HG * g + i, :], slot_of(kind, 2 * g + i // 2)[:, at:at + widths[j]],
                                       start=(j == 0), stop=(j == NT - 1), skip_group_check=True)
                if last == NT:
                    mm.then_inc(S["heads_out"], 1)

            def turn_heads(ring, sequence, kind, g):
                nth = G * kind + g
                pe.wait_ge(S["heads_copied"], due("heads_copied", sequence, nth + 1))
                turn(ring, f"rows{kind}_{g}", lambda t: ot[:, nth % 2, t * P:(t + 1) * P])

            def turn_attn(ring, kind):
                pe.wait_ge(taken_sem(ring, f"rows{kind}_{G - 1}"), taken_at(ring, f"rows{kind}_{G - 1}"))
                turn(ring, f"cols{kind}", lambda t: attn[:, t, :])

            def turn_max(ring, unit, b, last):
                pe.wait_ge(taken_sem(("score", b), last), taken_at(("score", b), last))
                pe.transpose(to_bank(ring, unit)[:, 0:P], mx[:, :], ident[:, :]).then_inc(full_sem(ring, unit), 1)

            def expert_in(ring, e, first=0, last=FC):
                for c in range(first, last):
                    project(ring, f"moe{e}_{c}", W1[:, e, c * P:(c + 1) * P], x1T[:, :])

            def expert_out(ring, e, first=0, last=NT):
                hidden, unit = (ha, hb)[e % 2], f"moe{e}_out"
                if first == 0:
                    for c in (FC - 2, FC - 1):
                        pe.wait_ge(taken_sem(ring, f"moe{e}_{c}"), taken_at(ring, f"moe{e}_{c}"))
                bank = to_bank(ring, unit) if first == 0 else bank_of(ring, unit)
                for t in range(first, last):
                    for k in range(FC):
                        mm = pe.matmul(bank[:, t * P:(t + 1) * P], hidden[:, k, t * P:(t + 1) * P], W2[:, e, k, :],
                                       start=(k == 0), stop=(k == FC - 1))
                if last == NT:
                    mm.then_inc(full_sem(ring, unit), 1)

            def mix_causal(ring):
                bank = to_bank(ring, "mixed_causal")
                for t in range(NT):
                    o = bank[:, t * P:(t + 1) * P]
                    pe.matmul(o, gatesT[:, t * P:(t + 1) * P], b2[:, :], start=True, stop=False)
                    mm = pe.matmul(o, attnT[:, 0, t * P:(t + 1) * P], wo1[:, :], start=False, stop=True)
                mm.then_inc(full_sem(ring, "mixed_causal"), 1)

            def third_layer(ring, first, last):
                if first == 0:
                    for g in (G - 2, G - 1):
                        pe.wait_ge(taken_sem(ring, f"h2_{g}"), taken_at(ring, f"h2_{g}"))
                bank = to_bank(ring, "third_layer") if first == 0 else bank_of(ring, "third_layer")
                for t in range(first, last):
                    for k in range(FC):
                        mm = pe.matmul(bank[:, t * P:(t + 1) * P], ha[:, k, t * P:(t + 1) * P], w3T[:, k, :], start=(k == 0), stop=(k == FC - 1))
                if last == NT:
                    mm.then_inc(full_sem(ring, "third_layer"), 1)

            def first_block(b, after_another, ring):
                now, before = (b, 0), (b, -1)
                pe.wait_ge(S["hrow1"], due("hrow1", now, 1))
                turn(ring, "hT1", lambda t: hrow[:, t, :])
                pe.wait_ge(S["xn1"], due("xn1", now, 1))
                turn(ring, "xnT1", lambda t: xn[:, t, :])
                pe.wait_ge(taken_sem(ring, "hT1"), taken_at(ring, "hT1"))
                project(ring, "q1", wq[:, :], hT[:, :])
                project(ring, "k1", wk[:, :], hT[:, :])
                if after_another:
                    weigh(before, CAUSAL, G - 1)
                project_rows(ring, "v1", hT, wv[:, :])
                if after_another:
                    turn_heads(ring, before, CAUSAL, G - 1)
                project(ring, "qm1", wqm[:, :], hT[:, :])
                pe.wait_ge(taken_sem(ring, "xnT1"), taken_at(ring, "xnT1"))
                for c in range(FC):
                    project(ring, f"gate{c}", w1T[:, c * P:(c + 1) * P], xnT[:, :])
                    if c == 0 and after_another:
                        turn_attn(ring, CAUSAL)
                    project(ring, f"up{c}", w2T[:, c * P:(c + 1) * P], xnT[:, :])
                    if c == 0 and after_another:
                        pe.wait_ge(taken_sem(ring, f"cols{CAUSAL}"), taken_at(ring, f"cols{CAUSAL}"))
                        mix_causal(ring)
                if not after_another:
                    pe.wait_ge(S["later_weights"], 16 * LATER_LOADS)
                    pe.wait_ge(S["w3_scaled"], 1)
                    pe.wait_ge(S["masks_ready"], 1)
                    pe.wait_ge(S["slots_set"], 16 * (len(scratch) + HG))
                pe.wait_ge(S["slots_q"], due("slots_q", now, 16))
                pe.wait_ge(S["slots_k"], due("slots_k", now, PLACED))
                for c in range(FC):
                    for k in range(FC):
                        slide_max(b, 2 * (FC * c + k), 2 * (FC * c + k) + 2)
                        if c == k == 0:
                            pe.wait_ge(taken_sem(ring, f"up{FC - 1}"), taken_at(ring, f"up{FC - 1}"))
                        dense(ring, f"h1_{c}", h1T, ha, c, k, k + 1)
                turn_max(ring, "slide_max", b, f"smax{H - 1}b")
                pe.wait_ge(S["slots_qm"], due("slots_qm", now, 16))
                for g in range(G):
                    tri_scores(b, "lin", QM, 10 * g, 10 * g + 3)
                    dense(ring, f"h2_{g}", h2T, hb, g, 0, 2)
                    tri_scores(b, "lin", QM, 10 * g + 3, 10 * g + 5)
                    if g:
                        weigh(now, LIN, g - 1)
                    tri_scores(b, "lin", QM, 10 * g + 5, 10 * g + 8)
                    dense(ring, f"h2_{g}", h2T, hb, g, 2, 4)
                    tri_scores(b, "lin", QM, 10 * g + 8, 10 * g + 10)
                    if g:
                        turn_heads(ring, now, LIN, g - 1)
                pe.wait_ge(S["max_placed"], due("max_placed", now, PLACED))
                for g in range(G):
                    kind, last = (SLIDE, g - 1) if g else (LIN, G - 1)
                    slide_scores(b, 8 * g, 8 * g + 3)
                    if g == 0:
                        third_layer(ring, 0, 2)
                    if after_another and (g, 0) in OUT_BESIDE:
                        expert_out(ring, *OUT_BESIDE[g, 0])
                    slide_scores(b, 8 * g + 3, 8 * g + 4)
                    weigh(now, kind, last)
                    slide_scores(b, 8 * g + 4, 8 * g + 7)
                    if g == 0:
                        third_layer(ring, 2, 4)
                    if after_another and (g, 1) in OUT_BESIDE:
                        expert_out(ring, *OUT_BESIDE[g, 1])
                    slide_scores(b, 8 * g + 7, 8 * g + 8)
                    turn_heads(ring, now, kind, last)
                    if after_another and g in IN_BEHIND:
                        expert_in(ring, IN_BEHIND[g])
                    if g == 0:
                        turn_attn(ring, LIN)
                weigh(now, SLIDE, G - 1)
                if after_another:
                    expert_out(ring, 6)
                turn_heads(ring, now, SLIDE, G - 1)
                if after_another:
                    expert_in(ring, 7, 0, 2)
                turn_attn(ring, SLIDE)
                if after_another:
                    expert_in(ring, 7, 2, 4)
                for kind in (LIN, SLIDE):
                    pe.wait_ge(taken_sem(ring, f"cols{kind}"), taken_at(ring, f"cols{kind}"))
                bank = to_bank(ring, "mixed_first")
                for t in range(NT):
                    for kind in (LIN, SLIDE):
                        mm = pe.matmul(bank[:, t * P:(t + 1) * P], attnT[:, kind, t * P:(t + 1) * P], wout[:, kind, :],
                                       start=(kind == LIN), stop=(kind == SLIDE))
                mm.then_inc(full_sem(ring, "mixed_first"), 1)
                if after_another:
                    expert_out(ring, 7)

            def second_block(b, ring):
                now = (b, 0)
                pe.wait_ge(S["hrow2"], due("hrow2", now, 1))
                turn(ring, "hT2", lambda t: hrow[:, t, :])
                pe.wait_ge(S["xn2"], due("xn2", now, 1))
                turn(ring, "xnT2", lambda t: xn[:, t, :])
                pe.wait_ge(taken_sem(ring, "hT2"), taken_at(ring, "hT2"))
                project(ring, "q2", wq1[:, :], hT[:, :])
                project(ring, "k2", wk1[:, :], hT[:, :])
                project_rows(ring, "v2", hT, wv1[:, :])
                pe.wait_ge(taken_sem(ring, "xnT2"), taken_at(ring, "xnT2"))
                project_rows(ring, "logits", x1T, wgT[:, :], E)
                expert_in(ring, 0)
                expert_out(ring, 0)
                for n in range(CMAX_STEPS):
                    if n // FC % 2 == 0:
                        expert_in(ring, n // (2 * FC) + 1, n % FC, n % FC + 1)
                    else:
                        expert_out(ring, n // (2 * FC) + 1, n % FC, n % FC + 1)
                    if n == 0:
                        pe.wait_ge(S["slots_q"], due("slots_q", now, 2 * 16))
                        pe.wait_ge(S["slots_k"], due("slots_k", now, 2 * PLACED))
                    causal_max(b, *cmax_units(n))
                turn_max(ring, "causal_max", b, f"cmax_{H // 2 - 1}")
                pe.wait_ge(S["gated"], due("gated", now, 1))
                turn(ring, "gatesT", lambda t: gates[:, t, :], rows=E)
                expert_in(ring, 3)
                pe.wait_ge(S["max_placed"], due("max_placed", now, 2 * PLACED))
                for g in range(G):
                    tri_scores(b, "causal", Q, 10 * g, 10 * g + 3)
                    if g == OUT3_BESIDE:
                        expert_out(ring, 3, 0, 1)
                    tri_scores(b, "causal", Q, 10 * g + 3, 10 * g + 5)
                    if g == OUT3_BESIDE:
                        expert_out(ring, 3, 1, 2)
                    tri_scores(b, "causal", Q, 10 * g + 5, 10 * g + 7)
                    if g == OUT3_BESIDE:
                        expert_out(ring, 3, 2, 3)
                    if g:
                        weigh(now, CAUSAL, g - 1, 0, 1)
                    tri_scores(b, "causal", Q, 10 * g + 7, 10 * g + 9)
                    if g == OUT3_BESIDE:
                        expert_out(ring, 3, 3, 4)
                    if g:
                        weigh(now, CAUSAL, g - 1, 1, 4)
                    tri_scores(b, "causal", Q, 10 * g + 9, 10 * g + 10)
                    if g:
                        turn_heads(ring, now, CAUSAL, g - 1)

            def closing(ring):
                before = (NB, -1)
                weigh(before, CAUSAL, G - 1)
                expert_in(ring, 4)
                turn_heads(ring, before, CAUSAL, G - 1)
                expert_in(ring, 5)
                expert_out(ring, 4)
                turn_attn(ring, CAUSAL)
                expert_in(ring, 6)
                expert_out(ring, 5)
                pe.wait_ge(taken_sem(ring, f"cols{CAUSAL}"), taken_at(ring, f"cols{CAUSAL}"))
                mix_causal(ring)
                expert_in(ring, 7)
                expert_out(ring, 6)
                expert_out(ring, 7)

            pe.wait_ge(S["setup_weights"], 16 * SETUP_LOADS)
            pe.matmul(misc[0][:, 0:P], wqfT, wkfT, start=True, stop=True).then_inc(S["setup_pe"], 1)
            pe.wait_ge(S["setup_dve"], 1)
            pe.matmul(misc[0][:, P:2 * P], wqT, bdm, start=True, stop=True).then_inc(S["setup_pe"], 1)
            pe.wait_ge(S["setup_done"], 1)
            pe.wait_ge(S["first_weights"], 16 * FIRST_LOADS)
            first_block(0, False, ("opening", 0))
            pe.wait_ge(S["expert_weights"], 16 * EXPERT_LOADS)
            second_block(0, ("opening", 0))
            for unit in last_units(("opening", 0)):
                pe.wait_ge(taken_sem(("opening", 0), unit), taken_at(("opening", 0), unit))
            with pe.Fori(1, NB) as b:
                first_block(b, True, ("steady", b))
                second_block(b, ("steady", b))
            for unit in last_units(("steady", NB - 1)):
                pe.wait_ge(taken_sem(("steady", NB - 1), unit), taken_at(("steady", NB - 1), unit))
            closing(("closing", NB))

        @block.scalar
        def _(act):
            def evacuate(ring, unit, to, func, scale=1.0, bias=0.0):
                act.wait_ge(full_sem(ring, unit), full_at(ring, unit))
                return act.activation(to, bank_of(ring, unit)[:, :], func, scale=scale, bias=bias)

            def split_hi(ring, now, name, nth, bias=0.0):
                before = {("q", 1): ("q", 0), ("qm", 1): ("q", 1), ("q", 2): ("qm", 1), ("k", 1): ("k", 0), ("k", 2): ("k", 1)}
                other, times = before[name, nth]
                act.wait_ge(S[f"sent_{other}"], due(f"sent_{other}", now, SENT * times))
                evacuate(ring, f"{name}{nth}", hi[:, {"q": 0, "k": 1, "qm": 0}[name], :], ACT.Identity, bias=bias)\
                    .then_inc(S[f"hi_{name}"], 1)

            def probs_from(b, unit, to, func, scale, bias, n=512):
                ring = ("score", b)
                act.wait_ge(full_sem(ring, unit), full_at(ring, unit))
                bank = bank_of(ring, unit)[:, 0:n]
                if len(to.shape) == 3:
                    bank = bank.rearrange("p (a n) -> p a n", a=2)
                return act.activation(to, bank, func, scale=scale, bias=bias).then_inc(taken_sem(ring, unit), 1)

            def pair_slot(b, kind, p):
                slots = SLOTS + 1 if kind == CAUSAL else SLOTS
                if kind != CAUSAL or p >= slots:
                    act.wait_ge(S["heads_out"], due("heads_out", (b, 0), (H // 2 * kind + p - slots) // 2 + 1))
                return slot_of(kind, p)

            def tri_probs(b, kind, tag, p, func, scale, bias):
                slot = pair_slot(b, kind, p)
                for n, h in enumerate((2 * p, 2 * p + 1)):
                    probs_from(b, f"{tag}{h}a", slot[:, PROBS * n:PROBS * n + 512], func, scale, bias)
                    probs_from(b, f"{tag}{h}b", slot[:, PROBS * n + 512:PROBS * n + 1024], func, scale, bias)
                probs_from(b, f"{tag}_{p}", slot.rearrange("p (h n) -> p h n", h=2)[:, :, 1024:PROBS], func, scale, bias)

            def slide_probs(b, p):
                slot = pair_slot(b, SLIDE, p)
                for n, h in enumerate((2 * p, 2 * p + 1)):
                    at = NT * WQ * n
                    probs_from(b, f"slide{h}a", slot[:, at:at + 2 * WQ], ACT.Exp, SCALE, 0.0, 2 * WQ)
                    probs_from(b, f"slide{h}b", slot[:, at + 2 * WQ:at + 3 * WQ + P], ACT.Exp, SCALE, 0.0, WQ + P)

            def gelu(ring, e):
                hidden = (ha, hb)[e % 2]
                for c in range(FC):
                    evacuate(ring, f"moe{e}_{c}", hidden[:, c, :], ACT.Gelu, bias=b1[:, FC * e + c:FC * e + c + 1])\
                        .then_inc(taken_sem(ring, f"moe{e}_{c}"), 1)

            def first_block(b, after_another, ring):
                now = (b, 0)
                evacuate(ring, "hT1", hT[:, :], ACT.Identity, scale=norm_w[:, 0:1]).then_inc(taken_sem(ring, "hT1"), 1)
                for name in ("q", "k", "qm"):
                    split_hi(ring, now, name, 1)
                for c in range(FC):
                    evacuate(ring, f"gate{c}", ha[:, c, :], ACT.Silu, scale=s1[:, c:c + 1]).then_inc(taken_sem(ring, f"gate{c}"), 1)
                if not after_another:
                    load_experts()
                    act.wait_ge(S["later_weights"], 16 * LATER_LOADS)
                for c in range(FC):
                    evacuate(ring, f"h1_{c}", hb[:, c, :], ACT.Gelu, scale=sh1[:, c:c + 1]).then_inc(taken_sem(ring, f"h1_{c}"), 1)
                for g in range(G):
                    tri_probs(b, LIN, "lin", 2 * g, ACT.Square, 0.5, 1.0)
                    tri_probs(b, LIN, "lin", 2 * g + 1, ACT.Square, 0.5, 1.0)
                    evacuate(ring, f"h2_{g}", ha[:, g, :], ACT.Gelu, scale=sh2[:, g:g + 1]).then_inc(taken_sem(ring, f"h2_{g}"), 1)
                for g in range(G):
                    slide_probs(b, 2 * g)
                    slide_probs(b, 2 * g + 1)
                    if after_another and g in IN_BEHIND:
                        gelu(ring, IN_BEHIND[g])
                if after_another:
                    gelu(ring, 7)

            def second_block(b, ring):
                now = (b, 0)
                evacuate(ring, "hT2", hT[:, :], ACT.Identity, scale=gamma[:, 0:1], bias=beta[:, 0:1]).then_inc(taken_sem(ring, "hT2"), 1)
                split_hi(ring, now, "q", 2, bq1[:, 0:1])
                split_hi(ring, now, "k", 2, bk1[:, 0:1])
                for e in range(EARLY):
                    gelu(ring, e)
                for p in range(H // 2):
                    tri_probs(b, CAUSAL, "causal", p, ACT.Exp, SCALE, 0.0)

            def load_experts():
                act.dma_start(W1[:, :, :], dram["W1"].rearrange("e p n -> p e n")).then_inc(S["expert_weights"], 16)
                act.dma_start(W2[:, :, :, :].rearrange("p e c n -> p (e c) n"), dram["W2"].rearrange("e (c p) n -> p (e c) n", p=P))\
                    .then_inc(S["expert_weights"], 16)
                act.dma_start(wo1[:, :], dram["wo1"]).then_inc(S["expert_weights"], 16)

            later_loads = [(sh1[:, :], dram["sh1"]), (h1T[:, :, :], dram["h1T"].rearrange("(c p) n -> p c n", p=P)),
                           (sh2[:, :], dram["sh2"]), (h2T[:, :, :], dram["h2T"].rearrange("(c p) n -> p c n", p=P)),
                           (s3, dram["s3"].partition_broadcast(P)), (w3T[:, :, :], dram["w3T"].rearrange("(c p) n -> p c n", p=P)),
                           (wout[:, :, :], dram["wout"].rearrange("a p n -> p a n")), (gamma[:, :], dram["gamma"]), (beta[:, :], dram["beta"]),
                           (wq1[:, :], dram["wq1"]), (wk1[:, :], dram["wk1"]), (wv1[:, :], dram["wv1"]), (bq1[:, :], dram["bq1"]), (bk1[:, :], dram["bk1"]),
                           (bv1[:, :], dram["bv1"].partition_broadcast(P)), (wgT[:, :], dram["wgT"]), (b1[:, :], dram["b1"]),
                           (bo1[:, :], dram["bo1"].partition_broadcast(P)), (earlier[:, :], dram["earlier"]), (b2[:, :], dram["b2"])]
            for dst, src in later_loads:
                act.dma_start(dst, src).then_inc(S["later_weights"], 16)
            assert len(later_loads) == LATER_LOADS
            act.wait_ge(S["setup_done"], 1)
            act.wait_ge(S["first_weights"], 16 * FIRST_LOADS)
            first_block(0, False, ("opening", 0))
            second_block(0, ("opening", 0))
            with act.Fori(1, NB) as b:
                first_block(b, True, ("steady", b))
                second_block(b, ("steady", b))
            for e in range(EARLY, E):
                gelu(("closing", NB), e)

        @block.gpsimd
        def _(pool):
            def mask_tri(b, kind, tag, p):
                pair = slot_of(kind, p).rearrange("p (h n) -> p h n", h=2)
                last_unit = f"{tag}_{p}"
                pool.wait_ge(taken_sem(("score", b), last_unit), taken_at(("score", b), last_unit))
                pool.sem_inc(S["unread"], 1)
                for n in range(2):
                    three = pair[:, n, :].rearrange("p (n c) -> p n c", c=256)[:, 0:5:2, 0:P]
                    pool.affine_select(out=three, in_=three, compare_op=ALU.is_ge, fill=0.0, base=0,
                                       pattern=[[0, 3], [1, P]], channel_multiplier=-1)
                last = pair[:, :, TRI_AT[3]:TRI_AT[3] + P]
                pool.affine_select(out=last, in_=last, compare_op=ALU.is_ge, fill=0.0, base=0,
                                   pattern=[[0, 2], [1, P]], channel_multiplier=-1).then_inc(S["probs_ready"], 1)

            def mask_slide(b, p):
                last_unit = f"slide{2 * p + 1}b"
                pool.wait_ge(taken_sem(("score", b), last_unit), taken_at(("score", b), last_unit))
                pool.sem_inc(S["unread"], 1)
                tiles = slot_of(SLIDE, p)[:, 0:2 * NT * WQ].rearrange("p (n c) -> p n c", c=WQ)
                near, far = tiles[:, :, 0:P], tiles[:, :, WIN:WQ]
                pool.affine_select(out=near, in_=near, compare_op=ALU.is_ge, fill=0.0, base=0,
                                   pattern=[[0, 2 * NT], [1, P]], channel_multiplier=-1).then_inc(S["slide_near"], 1)
                pool.wait_ge(S["slide_near"], due("slide_near", (b, 0), p + 1))
                pool.sem_inc(S["unread"], 1)
                pool.affine_select(out=far, in_=far, compare_op=ALU.is_ge, fill=0.0, base=0,
                                   pattern=[[0, 2 * NT], [-1, P]], channel_multiplier=1).then_inc(S["probs_ready"], 1)

            def power(sequence, nth):
                pool.wait_ge(S[f"stats{nth}"], due(f"stats{nth}", sequence, 1))
                for n in (1, 0):
                    pool.tensor_tensor(rs[:, n, :], pw[:, n, :], half_neg[:, :], ALU.pow).then_inc(S[f"powered{nth}"], 1)

            def norm_first(sequence):
                power(sequence, 1)
                pool.wait_ge(S["xn1"], due("xn1", sequence, 1))
                pool.tensor_tensor(xs[:, :, :], x_in[:, :, :], xn[:, :, :], ALU.add).then_inc(S["xs_ready"], 1)

            def body(b):
                now, after = (b, 0), (b, 1)
                for p in range(H // 2):
                    mask_tri(b, LIN, "lin", p)
                for p in range(H // 2):
                    mask_slide(b, p)
                power(now, 2)
                pool.wait_ge(S["x1_ready"], due("x1_ready", now, 1))
                pool.sem_inc(S["unread"], 1)
                pool.wait_ge(S["stored"], due("stored", now, 0))
                pool.tensor_tensor(y[:, :, :], x1[:, :, :], bo1[:, :].unsqueeze(1).to_broadcast([P, NT, P]), ALU.add)\
                    .then_inc(S["y_init"], 1)
                pool.wait_ge(S["shifted"], due("shifted", now, 1))
                pool.tensor_tensor(ex[:, :, :], euler[:, :, :], lgs[:, :, :], ALU.pow).then_inc(S["exped"], 1)
                for p in range(H // 2):
                    mask_tri(b, CAUSAL, "causal", p)
                    if p == 3:
                        norm_first(after)

            pool.memset(K[:, H // 2:H, :].bitcast(F32), 0.0).then_inc(S["keys_cleared"], 1)
            pool.memset(V[:, :, :, D:D + 1], 1.0)
            pool.memset(mx[:, :], 0.0)
            pool.memset(euler[:, :, :], math.e)
            pool.memset(half_neg[:, :], -0.5).then_inc(S["cleared"], 1)
            pool.wait_ge(S["setup_done"], 1)
            norm_first((0, 0))
            pool.wait_ge(S["later_weights"], 16 * LATER_LOADS)
            pool.tensor_tensor(w3T[:, :, :], w3T[:, :, :], s3.unsqueeze(1).to_broadcast([P, FC, P]), ALU.mult).then_inc(S["w3_scaled"], 1)
            body(0)
            with pool.Fori(1, NB) as b:
                body(b)

        @block.vector
        def _(dve):
            def lap(name, sequence, n, ins):
                ins.then_inc(S[name], 1)
                dve.wait_ge(S[name], due(name, sequence, n))

            def normalize(sequence, nth, src, eps_inner):
                for t in range(NT):
                    last = dve.bn_stats(bn[:, t, :], src[:, t, :])
                lap(f"norm{nth}_laps", sequence, 1, last)
                dve.sem_inc(S["unread"], 1)
                for t in range(NT):
                    last = dve.bn_aggr(mv[:, t, :], bn[:, t, :])
                lap(f"norm{nth}_laps", sequence, 2, last)
                dve.tensor_scalar(pw[:, 0, :], mv[:, :, 1], EPS_LN, None, ALU.add)
                dve.tensor_scalar(pw[:, 1, :], mv[:, :, 1], 1.0 + eps_inner, eps_inner * EPS_LN, ALU.mult, ALU.add)\
                    .then_inc(S[f"stats{nth}"], 1)
                for n, to, name in ((1, hrow, "hrow"), (0, xn, "xn")):
                    dve.wait_ge(S[f"powered{nth}"], due(f"powered{nth}", sequence, 2 - n))
                    for t in range(NT):
                        last = dve.tensor_scalar(to[:, t, :], src[:, t, :], mv[:, t, 0:1], rs[:, n, t:t + 1], ALU.subtract, ALU.mult)
                    last.then_inc(S[f"{name}{nth}"], 1)

            def take(ring, unit, to, view=lambda x: x[:, :]):
                dve.wait_ge(full_sem(ring, unit), full_at(ring, unit))
                dve.tensor_copy(to, view(bank_of(ring, unit))).then_inc(taken_sem(ring, unit), 1)

            def split_lo(ring, now, name, nth, bias=None):
                part, unit = {"q": 0, "k": 1, "qm": 0}[name], f"{name}{nth}"
                dve.wait_ge(S[f"hi_{name}"], due(f"hi_{name}", now, nth))
                if bias is None:
                    ins = dve.tensor_tensor(lo[:, part, :], bank_of(ring, unit)[:, :], hi[:, part, :].bitcast(F32), ALU.subtract)
                else:
                    ins = dve.scalar_tensor_tensor(out=lo[:, part, :], in0=bank_of(ring, unit)[:, :], scalar=bias,
                                                   in1=hi[:, part, :].bitcast(F32), op0=ALU.add, op1=ALU.subtract)
                ins.then_inc(taken_sem(ring, unit), 1)

            def v_heads(bank):
                return bank[:, :].rearrange("p (n d) -> p n d", d=D)

            V_to = V[:, :, :, 0:D].rearrange("p t h d -> p (t h) d")

            def mx_at(h, j):
                at = (h % HG) * G * NT + (h // HG) * NT + j
                return mx[:, at:at + 1]

            def row_max(b, unit, heads_and_tiles):
                ring = ("score", b)
                dve.wait_ge(full_sem(ring, unit), full_at(ring, unit))
                for h, j, at, n in heads_and_tiles:
                    last = dve.tensor_reduce(mx_at(h, j), bank_of(ring, unit)[:, at:at + n], AX_X, ALU.max)
                last.then_inc(taken_sem(ring, unit), 1)

            def slide_max(b):
                for h in range(H):
                    row_max(b, f"smax{h}a", [(h, 0, 0, P), (h, 1, WQ, WQ)])
                    row_max(b, f"smax{h}b", [(h, 2, 0, WQ), (h, 3, WQ, WQ)])

            def causal_max(b, first, last):
                for n in range(first, last):
                    p, u = n // 5, n % 5
                    h = 2 * p + u // 2
                    if u == 4:
                        parts = [(2 * p, 1, 0, 256), (2 * p + 1, 1, 256, 256)]
                    else:
                        parts = [(h, 2, 0, 384), (h, 0, 384, 128)] if u % 2 else [(h, 3, 0, 512)]
                    row_max(b, tri_units("cmax")[n], parts)

            def negate_max(ring, unit):
                dve.wait_ge(full_sem(ring, unit), full_at(ring, unit))
                dve.tensor_scalar(mrow[:, :], bank_of(ring, unit)[0:H * NT, 0:P], -1.0, None, ALU.mult).then_inc(taken_sem(ring, unit), 1)

            def copy_heads(sequence, kind, g):
                nth = G * kind + g
                dve.wait_ge(S["heads_out"], due("heads_out", sequence, nth + 1))
                dve.tensor_copy(ot[:, nth % 2, :], heads[:, :]).then_inc(S["heads_copied"], 1)

            def divide_rows(ring, sequence, kind, g):
                unit = f"rows{kind}_{g}"
                dve.wait_ge(full_sem(ring, unit), full_at(ring, unit))
                bank = bank_of(ring, unit)[:, :].rearrange("p (t i r) -> p t i r", t=NT, r=ROWS)
                if kind == LIN:
                    lap("divide_laps", sequence, 2 * g + 1, dve.tensor_scalar(den[:, :, :], bank[:, :, :, D], EPS_LIN, None, ALU.add))
                    lap("divide_laps", sequence, 2 * g + 2, dve.reciprocal(rden[:, :, :], den[:, :, :]))
                else:
                    lap("divide_laps", sequence, G * (kind + 1) + g + 1, dve.reciprocal(rden[:, :, :], bank[:, :, :, D]))
                to = attn[:, :, HG * D * g:HG * D * (g + 1)].rearrange("p t (i d) -> p t i d", d=D)
                dve.tensor_tensor(to, bank[:, :, :, 0:D], rden[:, :, :].unsqueeze(3).to_broadcast([P, NT, HG, D]), ALU.mult)\
                    .then_inc(taken_sem(ring, unit), 1)

            def choose_experts(ring, now):
                dve.wait_ge(taken_sem(ring, "logits"), taken_at(ring, "logits"))
                lap("choice_laps", now, 1, dve.tensor_reduce(m1[:, :], lg[:, :, :], AX_X, ALU.max))
                dve.tensor_tensor(lgs[:, :, :], lg[:, :, :], m1[:, :].unsqueeze(2).to_broadcast([P, NT, E]), ALU.subtract).then_inc(S["shifted"], 1)
                other, own = lg[:, :, :].unsqueeze(2).to_broadcast([P, NT, E, E]), lg[:, :, :].unsqueeze(3).to_broadcast([P, NT, E, E])
                above4, equal4 = (x[:, :, :].rearrange("p t (e j) -> p t e j", j=E) for x in (above, equal))
                dve.tensor_tensor(above4, other, own, ALU.is_gt)
                lap("choice_laps", now, 2, dve.tensor_tensor(equal4, other, own, ALU.is_equal))
                lap("choice_laps", now, 3, dve.tensor_tensor(equal[:, :, :], equal[:, :, :], earlier[:, :].unsqueeze(1).to_broadcast([P, NT, E * E]), ALU.mult))
                lap("choice_laps", now, 4, dve.tensor_tensor(above[:, :, :], above[:, :, :], equal[:, :, :], ALU.add))
                lap("choice_laps", now, 5, dve.tensor_reduce(rank[:, :, :], above4, AX_X, ALU.add))
                dve.wait_ge(S["exped"], due("exped", now, 1))
                lap("choice_laps", now, 6, dve.scalar_tensor_tensor(out=exs[:, :, :], in0=rank[:, :, :], scalar=1.5, in1=ex[:, :, :], op0=ALU.is_lt, op1=ALU.mult))
                lap("choice_laps", now, 7, dve.tensor_reduce(gsum[:, :], exs[:, :, :], AX_X, ALU.add))
                lap("choice_laps", now, 8, dve.reciprocal(rsum[:, :], gsum[:, :]))
                dve.tensor_tensor(gates[:, :, :], exs[:, :, :], rsum[:, :].unsqueeze(2).to_broadcast([P, NT, E]), ALU.mult).then_inc(S["gated"], 1)
                dve.wait_ge(S["gated"], due("gated", now, 1))

            def combine(ring, e):
                unit = f"moe{e}_out"
                dve.wait_ge(full_sem(ring, unit), full_at(ring, unit))
                for t in range(NT):
                    last = dve.scalar_tensor_tensor(out=y[:, t, :], in0=bank_of(ring, unit)[:, t * P:(t + 1) * P], scalar=gates[:, t, e:e + 1],
                                                    in1=y[:, t, :], op0=ALU.mult, op1=ALU.add)
                last.then_inc(taken_sem(ring, unit), 1)
                dve.wait_ge(taken_sem(ring, unit), taken_at(ring, unit))

            def add_third_layer(ring, now):
                dve.wait_ge(S["xs_ready"], due("xs_ready", now, 1))
                dve.sem_inc(S["unread"], 1)
                unit = "third_layer"
                dve.wait_ge(full_sem(ring, unit), full_at(ring, unit))
                dve.tensor_tensor(xs[:, :, :], bank_of(ring, unit)[:, :].rearrange("p (t n) -> p t n", n=P), xs[:, :, :], ALU.add).then_inc(taken_sem(ring, unit), 1)
                dve.wait_ge(taken_sem(ring, unit), taken_at(ring, unit))

            def add_mixed(ring):
                unit = "mixed_causal"
                dve.wait_ge(full_sem(ring, unit), full_at(ring, unit))
                dve.tensor_tensor(y[:, :, :], bank_of(ring, unit)[:, :].rearrange("p (t n) -> p t n", n=P), y[:, :, :], ALU.add).then_inc(taken_sem(ring, unit), 1)
                dve.wait_ge(taken_sem(ring, unit), taken_at(ring, unit))

            def first_block(b, after_another, ring):
                now, before = (b, 0), (b, -1)
                take(ring, "xnT1", xnT[:, :])
                split_lo(ring, now, "q", 1)
                split_lo(ring, now, "k", 1)
                if after_another:
                    copy_heads(before, CAUSAL, G - 1)
                take(ring, "v1", V_to, v_heads)
                if after_another:
                    divide_rows(ring, before, CAUSAL, G - 1)
                split_lo(ring, now, "qm", 1)
                if after_another:
                    take(ring, f"cols{CAUSAL}", attnT[:, 0, :])
                for c in range(FC):
                    dve.wait_ge(taken_sem(ring, f"gate{c}"), taken_at(ring, f"gate{c}"))
                    dve.wait_ge(full_sem(ring, f"up{c}"), full_at(ring, f"up{c}"))
                    dve.scalar_tensor_tensor(out=ha[:, c, :], in0=bank_of(ring, f"up{c}")[:, :], scalar=s2[:, c:c + 1],
                                             in1=ha[:, c, :], op0=ALU.mult, op1=ALU.mult).then_inc(taken_sem(ring, f"up{c}"), 1)
                    if c == 0 and after_another:
                        add_mixed(ring)
                slide_max(b)
                negate_max(ring, "slide_max")
                for g in range(G):
                    copy_heads(now, LIN, g)
                    if g == G - 1:
                        add_third_layer(ring, now)
                    divide_rows(ring, now, LIN, g)
                take(ring, f"cols{LIN}", attnT[:, LIN, :])
                for g in range(G):
                    copy_heads(now, SLIDE, g)
                    for (beside, _), (e, _, last) in OUT_BESIDE.items():
                        if after_another and beside == g + 1 and last == NT:
                            combine(ring, e)
                    if after_another and g == G - 1:
                        combine(ring, 6)
                    divide_rows(ring, now, SLIDE, g)
                take(ring, f"cols{SLIDE}", attnT[:, SLIDE, :])

            def second_block(b, after_another, ring):
                now = (b, 0)
                dve.wait_ge(full_sem(ring, "mixed_first"), full_at(ring, "mixed_first"))
                dve.tensor_tensor(x1[:, :, :], bank_of(ring, "mixed_first")[:, :].rearrange("p (t n) -> p t n", n=P), xs[:, :, :], ALU.add)\
                    .then_inc(taken_sem(ring, "mixed_first"), 1)
                dve.wait_ge(taken_sem(ring, "mixed_first"), taken_at(ring, "mixed_first"))
                dve.sem_inc(S["x1_ready"], 1)
                normalize(now, 2, x1, EPS_LN)
                if after_another:
                    combine(ring, 7)
                take(ring, "xnT2", x1T[:, :])
                split_lo(ring, now, "q", 2, bq1[:, 0:1])
                split_lo(ring, now, "k", 2, bk1[:, 0:1])
                dve.wait_ge(full_sem(ring, "v2"), full_at(ring, "v2"))
                dve.tensor_tensor(V[:, :, :, 0:D], bank_of(ring, "v2")[:, :].rearrange("p (t h d) -> p t h d", t=NT, d=D),
                                  bv1[:, :].rearrange("p (h d) -> p h d", d=D).unsqueeze(1).to_broadcast([P, NT, H, D]), ALU.add)\
                    .then_inc(taken_sem(ring, "v2"), 1)
                take(ring, "logits", lg[:, :, :], lambda x: x[:, 0:NT * E].rearrange("p (t e) -> p t e", e=E))
                choose_experts(ring, now)
                dve.wait_ge(S["y_init"], due("y_init", now, 1))
                combine(ring, 0)
                for n in range(CMAX_STEPS):
                    causal_max(b, *cmax_units(n))
                    if n % (2 * FC) == 2 * FC - 1:
                        combine(ring, n // (2 * FC) + 1)
                negate_max(ring, "causal_max")
                take(ring, "gatesT", gatesT[:, :], lambda x: x[0:E, :])
                for g in range(G - 1):
                    if g == OUT3_BESIDE:
                        combine(ring, 3)
                    copy_heads(now, CAUSAL, g)
                    divide_rows(ring, now, CAUSAL, g)
                    if g == 0:
                        first_norm((b, 1))

            def first_norm(sequence):
                dve.wait_ge(S["x_loaded"], due("x_loaded", sequence, 16))
                normalize(sequence, 1, x_in, EPS_RMS)

            dve.memset(heads[:, :], 0.0)
            dve.memset(K[:, 0:H // 2, :].bitcast(F32), 0.0).then_inc(S["keys_cleared"], 1)
            for name, (_, first) in counts.items():
                if first:
                    dve.sem_inc(S[name], first)
            dve.wait_ge(S["setup_weights"], 16 * SETUP_LOADS)
            dve.wait_ge(S["setup_pe"], 1)
            dve.tensor_tensor(bdm, misc[0][:, 0:P], blocks, ALU.mult).then_inc(S["setup_dve"], 1)
            dve.wait_ge(S["cleared"], 1)
            dve.wait_ge(S["setup_pe"], 2)
            dve.tensor_copy(wqm[:, :], misc[0][:, P:2 * P]).then_inc(S["setup_done"], 1)
            first_norm((0, 0))
            dve.wait_ge(S["first_weights"], 16 * FIRST_LOADS)
            dve.tensor_copy(identb[:, :], ident[:, :])
            dve.tensor_copy(causal_neg[:, :], causal_f)
            dve.tensor_copy(slide_neg[:, :], slide_f).then_inc(S["masks_ready"], 1)
            first_block(0, False, ("opening", 0))
            dve.wait_ge(S["later_weights"], 16 * LATER_LOADS)
            second_block(0, False, ("opening", 0))
            with dve.Fori(1, NB) as b:
                first_block(b, True, ("steady", b))
                second_block(b, True, ("steady", b))
            copy_heads((NB, -1), CAUSAL, G - 1)
            divide_rows(("closing", NB), (NB, -1), CAUSAL, G - 1)
            combine(("closing", NB), 4)
            take(("closing", NB), f"cols{CAUSAL}", attnT[:, 0, :])
            combine(("closing", NB), 5)
            add_mixed(("closing", NB))
            combine(("closing", NB), 6)
            combine(("closing", NB), 7)


def lay_out(i):
    import numpy as np

    def c(a):
        return np.ascontiguousarray(np.asarray(a, np.float32))

    def chunks(a):
        return c(np.reshape(a, (-1, P)).T)

    q, k = np.arange(P)[:, None], np.arange(P)[None, :]
    w = np.arange(WQ)[None, :]
    e = np.arange(E)
    ones = np.zeros((H, D, T), np.float32)
    ones[:, 0] = 1.0
    return {
        "x": c(i["L0_attn_x"]), "wq": c(i["L0_attn_Wq"]), "wqT": c(np.transpose(i["L0_attn_Wq"])), "wk": c(i["L0_attn_Wk"]),
        "wv": c(i["L0_attn_Wv"]), "wqfT": c(np.tile(np.transpose(i["L0_attn_Wqf"]), (1, H))),
        "wkfT": c(np.tile(np.transpose(i["L0_attn_Wkf"]), (1, H))), "wout": c(np.reshape(i["L0_attn_Wout"], (2, P, P))),
        "norm_w": c(np.reshape(i["L0_attn_norm_w"], (P, 1))),
        "w1T": c(np.transpose(i["L0_ffn_w1_w"])), "w2T": c(np.transpose(i["L0_ffn_w2_w"])), "h1T": c(np.transpose(i["L0_ffn_h1_w"])),
        "h2T": c(np.transpose(i["L0_ffn_h2_w"])), "w3T": c(np.transpose(i["L0_ffn_w3_w"])),
        "s1": chunks(i["L0_ffn_w1_s"]), "s2": chunks(i["L0_ffn_w2_s"]), "sh1": chunks(i["L0_ffn_h1_s"]), "sh2": chunks(i["L0_ffn_h2_s"]),
        "s3": c(i["L0_ffn_w3_s"]),
        "wq1": c(i["L1_attn_Wq"]), "wk1": c(i["L1_attn_Wk"]), "wv1": c(i["L1_attn_Wv"]), "wo1": c(i["L1_attn_Wo"]),
        "bq1": c(np.reshape(i["L1_attn_bq"], (P, 1))), "bk1": c(np.reshape(i["L1_attn_bk"], (P, 1))), "bv1": c(i["L1_attn_bv"]),
        "bo1": c(i["L1_attn_bo"]), "gamma": c(np.reshape(i["L1_attn_ln_gamma"], (P, 1))), "beta": c(np.reshape(i["L1_attn_ln_beta"], (P, 1))),
        "wgT": c(np.transpose(i["L1_ffn_Wg"])), "W1": c(i["L1_ffn_W1"]), "b1": chunks(i["L1_ffn_b1"]), "W2": c(i["L1_ffn_W2"]), "b2": c(i["L1_ffn_b2"]),
        "ident": np.eye(P, dtype=np.float32), "causal_neg": np.where(k <= q, 0.0, NEG).astype(np.float32),
        "slide_neg": np.where((w - WIN <= q) & (w >= q), 0.0, NEG).astype(np.float32),
        "earlier": c(np.broadcast_to((e[None, :] < e[:, None]).reshape(1, -1), (P, E * E))),
        "blocks": (q // D == k // D).astype(np.float32), "slot_q": np.zeros((H, D, T), np.float32), "slot_k": ones,
    }


def kernel(**inputs):
    import concourse.bacc as bacc
    from concourse.bass_utils import run_bass_kernel_spmd as run

    nc = bacc.Bacc("TRN2", target_bir_lowering=False, num_devices=1)
    arrays = lay_out(inputs)
    dram = {name: nc.dram_tensor(f"in_{name}", shape, F32, kind="ExternalInput").ap() for name, shape in SHAPES.items()}
    out = nc.dram_tensor("out", (NB, T, P), F32, kind="ExternalOutput").ap()
    build(nc, dram, out)
    r = run(nc, [{f"in_{name}": a for name, a in arrays.items()}], core_ids=[0])
    return r.results[0]["out"]
```
